# Optimizing a Trainium2 kernel written in Bass

```python
import numpy as np
import jax
import jax.numpy as jnp

def _softmax(x, axis=-1):
    return jax.nn.softmax(x, axis=axis)

def _gelu(x):
    return jax.nn.gelu(x, approximate=True)

def _silu(x):
    return jax.nn.silu(x)

def _sigmoid(x):
    return jax.nn.sigmoid(x)

def _layernorm(x, axis=-1, eps=1e-05):
    m = jnp.mean(x, axis=axis, keepdims=True)
    v = jnp.var(x, axis=axis, keepdims=True)
    return (x - m) / jnp.sqrt(v + eps)

def _scatter_add(tgt, idx, src, axis=0):
    return tgt.at[idx].add(src)

def _segment_sum(src, seg, n):
    return jax.ops.segment_sum(src, seg, n)
kernel_name = 'mk_gnn_preln_d4_gnn_r8_c3aec7'

def setup_inputs(seed: int=0):
    np.random.seed(seed)
    _w = jnp.asarray

    def _rec_inputs():
        import jax
        import jax.numpy as jnp
        _gk = jax.random.key(seed)
        x = -0.0002949 + 1 * jax.random.normal(jax.random.fold_in(_gk, 1), (1250, 512), jnp.float32)
        src = jax.random.randint(jax.random.fold_in(_gk, 2), (20000,), 0, 1250, jnp.int32)
        dst = jnp.minimum((1250 * jax.random.uniform(jax.random.fold_in(_gk, 3), (20000,)) ** 2.0).astype(jnp.int32), 9999)
        _o = jnp.argsort(dst, stable=True)
        src = src[_o]
        dst = dst[_o]
        edge_type_2 = jax.random.randint(jax.random.fold_in(_gk, 13), (20000,), 0, 2, jnp.int32)
        node_vec1 = jax.random.uniform(jax.random.fold_in(_gk, 14), (1250, 1), jnp.float32, 0.0, 0.999957)
        return (x, src, dst, edge_type_2, node_vec1)
    x, src, dst, edge_type_2, node_vec1 = _rec_inputs()

    def _L0_gnn_setup():
        import jax, jax.numpy as jnp
        import numpy as np
        N_NODES = 40962
        LATENT_DIM = 512
        N_EDGES = 81924
        NUM_BLOCKS = 4
        NUM_HEADS = 4
        NUM_FREQ = 32
        BASE_PERIOD = 16
        NOISE_EMB_DIM = 16
        EPS = 1e-05

        def _cond_layer_norm(x, cond, sw, sb, bw, bb):
            mu = jnp.mean(x, axis=-1, keepdims=True)
            var = jnp.var(x, axis=-1, keepdims=True)
            xn = (x - mu) * jax.lax.rsqrt(var + EPS)
            scale = cond @ sw + sb
            bias = cond @ bw + bb
            return xn * (1.0 + scale) + bias

        def _sparse_attention(x, src, dst, wq, bq, wk, bk, wv, bv, wo, bo):
            N, D = x.shape
            H, Dh = (NUM_HEADS, D // NUM_HEADS)
            q = (x @ wq + bq).reshape(N, H, Dh) * Dh ** (-0.5)
            k = (x @ wk + bk).reshape(N, H, Dh)
            v = (x @ wv + bv).reshape(N, H, Dh)
            scores = jnp.einsum('ehd,ehd->eh', q[src], k[dst])
            smax = jax.ops.segment_max(scores, src, num_segments=N)
            ex = jnp.exp(scores - smax[src])
            denom = jax.ops.segment_sum(ex, src, num_segments=N)
            attn = ex / denom[src]
            out = jax.ops.segment_sum(attn[:, :, None] * v[dst], src, num_segments=N)
            return out.reshape(N, D) @ wo + bo

        def _forward(x, edge_index, noise_levels, f_w1, f_b1, f_w2, f_b2, s1_w, s1_b, b1_w, b1_b, wq, bq, wk, bk, wv, bv, wo, bo, s2_w, s2_b, b2_w, b2_b, m_w1, m_b1, m_w2, m_b2):
            src, dst = (edge_index[0], edge_index[1])
            freqs = jnp.arange(1, NUM_FREQ + 1, dtype=x.dtype) * (2.0 * np.pi / BASE_PERIOD)
            ph = noise_levels * freqs
            emb = jnp.concatenate([jnp.sin(ph), jnp.cos(ph)], axis=-1)
            cond = jax.nn.silu(emb @ f_w1 + f_b1) @ f_w2 + f_b2
            for i in range(NUM_BLOCKS):
                y = _cond_layer_norm(x, cond, s1_w[i], s1_b[i], b1_w[i], b1_b[i])
                y = _sparse_attention(y, src, dst, wq[i], bq[i], wk[i], bk[i], wv[i], bv[i], wo[i], bo[i])
                x = x + y
                y = _cond_layer_norm(x, cond, s2_w[i], s2_b[i], b2_w[i], b2_b[i])
                y = jax.nn.relu(y @ m_w1[i] + m_b1[i]) @ m_w2[i] + m_b2[i]
                x = x + y
            return x
        key = jax.random.key(seed)
        ks = jax.random.split(key, 20)

        def w(k, shape, s=0.02):
            return jax.random.normal(k, shape, dtype=jnp.float32) * s
        D, B, C = (LATENT_DIM, NUM_BLOCKS, NOISE_EMB_DIM)
        z = lambda *s: jnp.zeros(s, jnp.float32)
        return {'latent_mesh_nodes': jax.random.normal(ks[0], (N_NODES, D), dtype=jnp.float32), 'edge_index': jax.random.randint(ks[1], (2, N_EDGES), 0, N_NODES, dtype=jnp.int32), 'noise_levels': jax.random.uniform(ks[2], (N_NODES, 1), dtype=jnp.float32), 'f_w1': w(ks[3], (2 * NUM_FREQ, C)), 'f_b1': z(C), 'f_w2': w(ks[4], (C, C)), 'f_b2': z(C), 's1_w': w(ks[5], (B, C, D)), 's1_b': z(B, D), 'b1_w': w(ks[6], (B, C, D)), 'b1_b': z(B, D), 'wq': w(ks[7], (B, D, D)), 'bq': z(B, D), 'wk': w(ks[8], (B, D, D)), 'bk': z(B, D), 'wv': w(ks[9], (B, D, D)), 'bv': z(B, D), 'wo': w(ks[10], (B, D, D)), 'bo': z(B, D), 's2_w': w(ks[11], (B, C, D)), 's2_b': z(B, D), 'b2_w': w(ks[12], (B, C, D)), 'b2_b': z(B, D), 'm_w1': w(ks[13], (B, D, D)), 'm_b1': z(B, D), 'm_w2': w(ks[14], (B, D, D)), 'm_b2': z(B, D)}
    _L0_gnn_all = _L0_gnn_setup()
    _L0_gnn_in = {k: v for k, v in _L0_gnn_all.items() if k in ('f_w1', 'f_b1', 'f_w2', 'f_b2', 's1_w', 's1_b', 'b1_w', 'b1_b', 'wq', 'bq', 'wk', 'bk', 'wv', 'bv', 'wo', 'bo', 's2_w', 's2_b', 'b2_w', 'b2_b', 'm_w1', 'm_b1', 'm_w2', 'm_b2')}
    del _L0_gnn_all

    def _L1_gnn_setup():
        import jax, jax.numpy as jnp
        import numpy as np
        N = 6250
        IN_CH = 512
        OUT_CH = 512
        DEG = 32
        E = N * DEG
        key = jax.random.key(seed)
        kx, kwc, kwn, kb, ke = jax.random.split(key, 5)
        x = jax.random.normal(kx, (N, IN_CH), dtype=jnp.float32)
        bound = 1.0 / np.sqrt(IN_CH)
        wc = jax.random.uniform(kwc, (IN_CH, OUT_CH), minval=-bound, maxval=bound, dtype=jnp.float32)
        wn = jax.random.uniform(kwn, (IN_CH, OUT_CH), minval=-bound, maxval=bound, dtype=jnp.float32)
        bias = jax.random.uniform(kb, (OUT_CH,), minval=-bound, maxval=bound, dtype=jnp.float32)
        src = jnp.repeat(jnp.arange(N, dtype=jnp.int64), DEG)
        dst = jax.random.randint(ke, (E,), 0, N, dtype=jnp.int64)
        edge_index = jnp.stack([src, dst], axis=0)
        return {'x': x, 'wc': wc, 'wn': wn, 'bias': bias, 'edge_index': edge_index}
    _L1_gnn_all = _L1_gnn_setup()
    _L1_gnn_in = {k: v for k, v in _L1_gnn_all.items() if k in ('wc', 'wn', 'bias')}
    del _L1_gnn_all

    def _L2_gnn_setup():
        import jax, jax.numpy as jnp
        import numpy as np
        NUM_RELATIONS = 2
        NUM_BASES = 30
        HIDDEN = 512
        N_NODES = 1250
        N_EDGES = 20000

        def rgcn_gate_layer(x, row, col, edge_type, basis, att, gate_w, root, bias):
            H = x.shape[1]
            w = jnp.einsum('rb,bio->rio', att, basis)
            x_j = x[col]
            msgs = []
            for r in range(NUM_RELATIONS):
                gate = jax.nn.sigmoid(x_j @ gate_w[r, :, 0])
                msgs.append(gate[:, None] * x_j @ w[r])
            msg = jnp.where((edge_type == 0)[:, None], msgs[0], msgs[1])
            agg = jax.ops.segment_sum(msg, row, num_segments=x.shape[0])
            return agg + x @ root + bias
        key = jax.random.key(seed)
        ks = jax.random.split(key, 16)
        H, R, B = (HIDDEN, NUM_RELATIONS, NUM_BASES)
        bound = 1.0 / np.sqrt(B * H)
        u = lambda k, shape: jax.random.uniform(k, shape, jnp.float32, -bound, bound)
        inp = {'x': jax.random.normal(ks[0], (N_NODES, H), jnp.float32), 'edge_index': jax.random.randint(ks[1], (2, N_EDGES), 0, N_NODES, jnp.int32), 'edge_type': jax.random.randint(ks[2], (N_EDGES,), 0, R, jnp.int32), 'basis1': u(ks[3], (B, H, H)), 'att1': u(ks[4], (R, B)), 'gate_w1': u(ks[5], (R, H, 1)), 'root1': u(ks[6], (H, H)), 'bias1': u(ks[7], (H,)), 'basis2': u(ks[8], (B, H, H)), 'att2': u(ks[9], (R, B)), 'gate_w2': u(ks[10], (R, H, 1)), 'root2': u(ks[11], (H, H)), 'bias2': u(ks[12], (H,))}
        return inp
    _L2_gnn_all = _L2_gnn_setup()
    _L2_gnn_in = {k: v for k, v in _L2_gnn_all.items() if k in ('basis1', 'att1', 'gate_w1', 'root1', 'bias1', 'basis2', 'att2', 'gate_w2', 'root2', 'bias2')}
    del _L2_gnn_all

    def _L3_gnn_setup():
        import jax, jax.numpy as jnp
        import numpy as np
        N_NODES = 1250
        N_EDGES = 20000
        D_IN = 512
        D_HID = 512
        D_OUT = 512

        def _sage_conv(x, src, dst, W_l, W_r, b):
            n = x.shape[0]
            summed = jax.ops.segment_sum(x[src], dst, num_segments=n)
            deg = jax.ops.segment_sum(jnp.ones((src.shape[0],), x.dtype), dst, num_segments=n)
            agg = summed / jnp.maximum(deg, 1.0)[:, None]
            return agg @ W_l.T + x @ W_r.T + b
        key = jax.random.key(seed)
        ks = jax.random.split(key, 8)
        x = jax.random.normal(ks[0], (N_NODES, D_IN), dtype=jnp.float32)
        edge_index = jax.random.randint(ks[1], (2, N_EDGES), 0, N_NODES, dtype=jnp.int64)
        label = jax.random.randint(ks[2], (1,), 0, 3, dtype=jnp.int64)
        batch = jnp.zeros((N_NODES,), dtype=jnp.int64)
        s1 = 1.0 / np.sqrt(D_IN)
        s2 = 1.0 / np.sqrt(D_HID)
        W1_l = jax.random.normal(ks[3], (D_HID, D_IN), dtype=jnp.float32) * s1
        W1_r = jax.random.normal(ks[4], (D_HID, D_IN), dtype=jnp.float32) * s1
        b1 = jnp.zeros((D_HID,), dtype=jnp.float32)
        W2_l = jax.random.normal(ks[5], (D_OUT, D_HID), dtype=jnp.float32) * s2
        W2_r = jax.random.normal(ks[6], (D_OUT, D_HID), dtype=jnp.float32) * s2
        b2 = jnp.zeros((D_OUT,), dtype=jnp.float32)
        return {'x': x, 'label': label, 'edge_index': edge_index, 'batch': batch, 'W1_l': W1_l, 'W1_r': W1_r, 'b1': b1, 'W2_l': W2_l, 'W2_r': W2_r, 'b2': b2}
    _L3_gnn_all = _L3_gnn_setup()
    _L3_gnn_in = {k: v for k, v in _L3_gnn_all.items() if k in ('label', 'W1_l', 'W1_r', 'b1', 'W2_l', 'W2_r', 'b2')}
    del _L3_gnn_all
    return {'x': x, 'src': src, 'dst': dst, 'edge_type_2': edge_type_2, 'node_vec1': node_vec1, 'L0_gnn_f_w1': _L0_gnn_in['f_w1'], 'L0_gnn_f_b1': _L0_gnn_in['f_b1'], 'L0_gnn_f_w2': _L0_gnn_in['f_w2'], 'L0_gnn_f_b2': _L0_gnn_in['f_b2'], 'L0_gnn_s1_w': _L0_gnn_in['s1_w'], 'L0_gnn_s1_b': _L0_gnn_in['s1_b'], 'L0_gnn_b1_w': _L0_gnn_in['b1_w'], 'L0_gnn_b1_b': _L0_gnn_in['b1_b'], 'L0_gnn_wq': _L0_gnn_in['wq'], 'L0_gnn_bq': _L0_gnn_in['bq'], 'L0_gnn_wk': _L0_gnn_in['wk'], 'L0_gnn_bk': _L0_gnn_in['bk'], 'L0_gnn_wv': _L0_gnn_in['wv'], 'L0_gnn_bv': _L0_gnn_in['bv'], 'L0_gnn_wo': _L0_gnn_in['wo'], 'L0_gnn_bo': _L0_gnn_in['bo'], 'L0_gnn_s2_w': _L0_gnn_in['s2_w'], 'L0_gnn_s2_b': _L0_gnn_in['s2_b'], 'L0_gnn_b2_w': _L0_gnn_in['b2_w'], 'L0_gnn_b2_b': _L0_gnn_in['b2_b'], 'L0_gnn_m_w1': _L0_gnn_in['m_w1'], 'L0_gnn_m_b1': _L0_gnn_in['m_b1'], 'L0_gnn_m_w2': _L0_gnn_in['m_w2'], 'L0_gnn_m_b2': _L0_gnn_in['m_b2'], 'L1_gnn_wc': _L1_gnn_in['wc'], 'L1_gnn_wn': _L1_gnn_in['wn'], 'L1_gnn_bias': _L1_gnn_in['bias'], 'L2_gnn_basis1': _L2_gnn_in['basis1'], 'L2_gnn_att1': _L2_gnn_in['att1'], 'L2_gnn_gate_w1': _L2_gnn_in['gate_w1'], 'L2_gnn_root1': _L2_gnn_in['root1'], 'L2_gnn_bias1': _L2_gnn_in['bias1'], 'L2_gnn_basis2': _L2_gnn_in['basis2'], 'L2_gnn_att2': _L2_gnn_in['att2'], 'L2_gnn_gate_w2': _L2_gnn_in['gate_w2'], 'L2_gnn_root2': _L2_gnn_in['root2'], 'L2_gnn_bias2': _L2_gnn_in['bias2'], 'L3_gnn_label': _L3_gnn_in['label'], 'L3_gnn_W1_l': _L3_gnn_in['W1_l'], 'L3_gnn_W1_r': _L3_gnn_in['W1_r'], 'L3_gnn_b1': _L3_gnn_in['b1'], 'L3_gnn_W2_l': _L3_gnn_in['W2_l'], 'L3_gnn_W2_r': _L3_gnn_in['W2_r'], 'L3_gnn_b2': _L3_gnn_in['b2']}

def reference(x, src, dst, edge_type_2, node_vec1, L0_gnn_f_w1, L0_gnn_f_b1, L0_gnn_f_w2, L0_gnn_f_b2, L0_gnn_s1_w, L0_gnn_s1_b, L0_gnn_b1_w, L0_gnn_b1_b, L0_gnn_wq, L0_gnn_bq, L0_gnn_wk, L0_gnn_bk, L0_gnn_wv, L0_gnn_bv, L0_gnn_wo, L0_gnn_bo, L0_gnn_s2_w, L0_gnn_s2_b, L0_gnn_b2_w, L0_gnn_b2_b, L0_gnn_m_w1, L0_gnn_m_b1, L0_gnn_m_w2, L0_gnn_m_b2, L1_gnn_wc, L1_gnn_wn, L1_gnn_bias, L2_gnn_basis1, L2_gnn_att1, L2_gnn_gate_w1, L2_gnn_root1, L2_gnn_bias1, L2_gnn_basis2, L2_gnn_att2, L2_gnn_gate_w2, L2_gnn_root2, L2_gnn_bias2, L3_gnn_label, L3_gnn_W1_l, L3_gnn_W1_r, L3_gnn_b1, L3_gnn_W2_l, L3_gnn_W2_r, L3_gnn_b2):
    import jax
    import jax.numpy as jnp

    def _L0_gnn_ref(latent_mesh_nodes, edge_index, noise_levels, f_w1, f_b1, f_w2, f_b2, s1_w, s1_b, b1_w, b1_b, wq, bq, wk, bk, wv, bv, wo, bo, s2_w, s2_b, b2_w, b2_b, m_w1, m_b1, m_w2, m_b2):
        import jax, jax.numpy as jnp
        import numpy as np
        N_NODES = 40962
        LATENT_DIM = 512
        N_EDGES = 81924
        NUM_BLOCKS = 4
        NUM_HEADS = 4
        NUM_FREQ = 32
        BASE_PERIOD = 16
        NOISE_EMB_DIM = 16
        EPS = 1e-05

        def _cond_layer_norm(x, cond, sw, sb, bw, bb):
            mu = jnp.mean(x, axis=-1, keepdims=True)
            var = jnp.var(x, axis=-1, keepdims=True)
            xn = (x - mu) * jax.lax.rsqrt(var + EPS)
            scale = cond @ sw + sb
            bias = cond @ bw + bb
            return xn * (1.0 + scale) + bias

        def _sparse_attention(x, src, dst, wq, bq, wk, bk, wv, bv, wo, bo):
            N, D = x.shape
            H, Dh = (NUM_HEADS, D // NUM_HEADS)
            q = (x @ wq + bq).reshape(N, H, Dh) * Dh ** (-0.5)
            k = (x @ wk + bk).reshape(N, H, Dh)
            v = (x @ wv + bv).reshape(N, H, Dh)
            scores = jnp.einsum('ehd,ehd->eh', q[src], k[dst])
            smax = jax.ops.segment_max(scores, src, num_segments=N)
            ex = jnp.exp(scores - smax[src])
            denom = jax.ops.segment_sum(ex, src, num_segments=N)
            attn = ex / denom[src]
            out = jax.ops.segment_sum(attn[:, :, None] * v[dst], src, num_segments=N)
            return out.reshape(N, D) @ wo + bo

        def _forward(x, edge_index, noise_levels, f_w1, f_b1, f_w2, f_b2, s1_w, s1_b, b1_w, b1_b, wq, bq, wk, bk, wv, bv, wo, bo, s2_w, s2_b, b2_w, b2_b, m_w1, m_b1, m_w2, m_b2):
            src, dst = (edge_index[0], edge_index[1])
            freqs = jnp.arange(1, NUM_FREQ + 1, dtype=x.dtype) * (2.0 * np.pi / BASE_PERIOD)
            ph = noise_levels * freqs
            emb = jnp.concatenate([jnp.sin(ph), jnp.cos(ph)], axis=-1)
            cond = jax.nn.silu(emb @ f_w1 + f_b1) @ f_w2 + f_b2
            for i in range(NUM_BLOCKS):
                y = _cond_layer_norm(x, cond, s1_w[i], s1_b[i], b1_w[i], b1_b[i])
                y = _sparse_attention(y, src, dst, wq[i], bq[i], wk[i], bk[i], wv[i], bv[i], wo[i], bo[i])
                x = x + y
                y = _cond_layer_norm(x, cond, s2_w[i], s2_b[i], b2_w[i], b2_b[i])
                y = jax.nn.relu(y @ m_w1[i] + m_b1[i]) @ m_w2[i] + m_b2[i]
                x = x + y
            return x
        return _forward(latent_mesh_nodes, edge_index, noise_levels, f_w1, f_b1, f_w2, f_b2, s1_w, s1_b, b1_w, b1_b, wq, bq, wk, bk, wv, bv, wo, bo, s2_w, s2_b, b2_w, b2_b, m_w1, m_b1, m_w2, m_b2)

    def _L1_gnn_ref(x, wc, wn, bias, edge_index):
        import jax, jax.numpy as jnp
        import numpy as np
        N = 6250
        IN_CH = 512
        OUT_CH = 512
        DEG = 32
        E = N * DEG
        alpha = x @ wc
        beta = x @ wn
        src, dst = (edge_index[0], edge_index[1])
        sums = jax.ops.segment_sum(beta[dst], src, num_segments=x.shape[0])
        counts = jax.ops.segment_sum(jnp.ones_like(src, dtype=beta.dtype), src, num_segments=x.shape[0])
        gamma = sums / counts[:, None]
        return alpha + gamma + bias

    def _L2_gnn_ref(x, edge_index, edge_type, basis1, att1, gate_w1, root1, bias1, basis2, att2, gate_w2, root2, bias2):
        import jax, jax.numpy as jnp
        import numpy as np
        NUM_RELATIONS = 2
        NUM_BASES = 30
        HIDDEN = 512
        N_NODES = 1250
        N_EDGES = 20000

        def rgcn_gate_layer(x, row, col, edge_type, basis, att, gate_w, root, bias):
            H = x.shape[1]
            w = jnp.einsum('rb,bio->rio', att, basis)
            x_j = x[col]
            msgs = []
            for r in range(NUM_RELATIONS):
                gate = jax.nn.sigmoid(x_j @ gate_w[r, :, 0])
                msgs.append(gate[:, None] * x_j @ w[r])
            msg = jnp.where((edge_type == 0)[:, None], msgs[0], msgs[1])
            agg = jax.ops.segment_sum(msg, row, num_segments=x.shape[0])
            return agg + x @ root + bias
        row, col = (edge_index[0], edge_index[1])
        h = jax.nn.relu(rgcn_gate_layer(x, row, col, edge_type, basis1, att1, gate_w1, root1, bias1))
        out = rgcn_gate_layer(h, row, col, edge_type, basis2, att2, gate_w2, root2, bias2)
        return out

    def _L3_gnn_ref(x, label, edge_index, batch, W1_l, W1_r, b1, W2_l, W2_r, b2):
        import jax, jax.numpy as jnp
        import numpy as np
        N_NODES = 1250
        N_EDGES = 20000
        D_IN = 512
        D_HID = 512
        D_OUT = 512

        def _sage_conv(x, src, dst, W_l, W_r, b):
            n = x.shape[0]
            summed = jax.ops.segment_sum(x[src], dst, num_segments=n)
            deg = jax.ops.segment_sum(jnp.ones((src.shape[0],), x.dtype), dst, num_segments=n)
            agg = summed / jnp.maximum(deg, 1.0)[:, None]
            return agg @ W_l.T + x @ W_r.T + b
        src, dst = (edge_index[0], edge_index[1])
        h = _sage_conv(x, src, dst, W1_l, W1_r, b1)
        h = jnp.tanh(h)
        out = _sage_conv(h, src, dst, W2_l, W2_r, b2)
        return out
    edge_index = jnp.stack([src, dst])
    batch0 = jnp.zeros((1250,), jnp.int32)
    h = jnp.maximum(_layernorm(x, axis=-1), 0.0)
    x = x + _L0_gnn_ref(h, edge_index, node_vec1, L0_gnn_f_w1, L0_gnn_f_b1, L0_gnn_f_w2, L0_gnn_f_b2, L0_gnn_s1_w, L0_gnn_s1_b, L0_gnn_b1_w, L0_gnn_b1_b, L0_gnn_wq, L0_gnn_bq, L0_gnn_wk, L0_gnn_bk, L0_gnn_wv, L0_gnn_bv, L0_gnn_wo, L0_gnn_bo, L0_gnn_s2_w, L0_gnn_s2_b, L0_gnn_b2_w, L0_gnn_b2_b, L0_gnn_m_w1, L0_gnn_m_b1, L0_gnn_m_w2, L0_gnn_m_b2)
    h = jnp.maximum(_layernorm(x, axis=-1), 0.0)
    x = x + _L1_gnn_ref(h, L1_gnn_wc, L1_gnn_wn, L1_gnn_bias, edge_index)
    h = jnp.maximum(_layernorm(x, axis=-1), 0.0)
    x = x + _L2_gnn_ref(h, edge_index, edge_type_2, L2_gnn_basis1, L2_gnn_att1, L2_gnn_gate_w1, L2_gnn_root1, L2_gnn_bias1, L2_gnn_basis2, L2_gnn_att2, L2_gnn_gate_w2, L2_gnn_root2, L2_gnn_bias2)
    h = jnp.maximum(_layernorm(x, axis=-1), 0.0)
    x = x + _L3_gnn_ref(h, L3_gnn_label, edge_index, batch0, L3_gnn_W1_l, L3_gnn_W1_r, L3_gnn_b1, L3_gnn_W2_l, L3_gnn_W2_r, L3_gnn_b2)
    return x

_drawn_inputs = setup_inputs


def setup_inputs(seed=0):
    import zlib

    import numpy as np

    out = dict(_drawn_inputs(seed))
    spreads = {'L0_gnn_f_b1': (0.0, 0.8),
     'L0_gnn_f_b2': (0.0, 0.8),
     'L0_gnn_s1_b': (0.0, 0.751),
     'L0_gnn_b1_b': (0.0, 0.295),
     'L0_gnn_bq': (0.0, 0.8),
     'L0_gnn_bk': (0.0, 2.0),
     'L0_gnn_bv': (0.0, 0.1),
     'L0_gnn_bo': (0.0, 0.1),
     'L0_gnn_s2_b': (0.0, 0.471),
     'L0_gnn_b2_b': (0.0, 0.441),
     'L0_gnn_m_b1': (0.0, 0.1),
     'L0_gnn_m_b2': (0.0, 0.1),
     'L3_gnn_b1': (0.0, 0.1),
     'L3_gnn_b2': (0.0, 0.1)}
    factors = {'node_vec1': 8.0,
     'L0_gnn_f_w1': 8.0,
     'L0_gnn_f_w2': 8.0,
     'L0_gnn_s1_w': 8.0,
     'L0_gnn_b1_w': 8.0,
     'L0_gnn_wq': 4.709,
     'L0_gnn_wk': 4.581,
     'L0_gnn_s2_w': 8.0,
     'L0_gnn_b2_w': 8.0,
     'L1_gnn_bias': 4.023,
     'L2_gnn_basis1': 8.0,
     'L2_gnn_att1': 8.0,
     'L2_gnn_gate_w1': 8.0,
     'L2_gnn_root1': 8.0,
     'L2_gnn_bias1': 25.476,
     'L2_gnn_basis2': 8.0,
     'L2_gnn_att2': 8.0,
     'L2_gnn_gate_w2': 8.0,
     'L2_gnn_root2': 8.0,
     'L2_gnn_bias2': 23.659}
    for name, (base, spread) in spreads.items():
        noise = np.random.default_rng([zlib.crc32(name.encode()), seed]).standard_normal(out[name].shape)
        drawn = base * np.exp(spread * noise) if base else spread * noise
        out[name] = jnp.asarray(drawn.astype(out[name].dtype))
    for name, factor in factors.items():
        out[name] = (out[name] * factor).astype(out[name].dtype)
    return out
```

```python
from contextlib import ExitStack

import numpy as np
import concourse.bass as bass
from concourse import mybir

F32, F32R, F16, BF16 = mybir.dt.float32, mybir.dt.float32r, mybir.dt.float16, mybir.dt.bfloat16
I32 = mybir.dt.int32
ALU, ACT, AX = mybir.AluOpType, mybir.ActivationFunctionType, mybir.AxisListType

N, D, E = 1250, 512, 20000
P = 125
T = N // P
KD = D // 128
HEADS, BLOCKS, BASES = 4, 4, 30
DH = D // HEADS
COND, FREQS = 16, 32
EC = E // P
BUCKETS = 2 * T
GROUP, STEPS = 512, 4
GROUPS = (E + BUCKETS * (GROUP - 1)) // GROUP
SLOTS = GROUPS * STEPS
HALVES = ((0, 626), (626, 624))
COLS = ((0, 418), (418, 416), (834, 416))
WIDE = ((0, 512), (512, 512), (1024, 226))
EPS = 1e-5
BIG = 1.0e30
NO_NODE = 5000.0


class Job:

    def __init__(self, slot, full, reuse, emptied):
        self.slot, self.full, self.reuse, self.emptied = slot, full, reuse, emptied


class Walk:

    def __init__(self):
        self.n, self.i, self.per = 0, None, 0

    def enter(self, i, per):
        self.i, self.per = i, per

    def leave(self):
        self.n, self.i = self.n + (BLOCKS - 1) * self.per, None

    def take(self):
        n, self.n = self.n, self.n + 1
        if self.i is None:
            return Job(n % 2, n + 1, n // 2 or None, n // 2 + 1)
        a, b = self.i * self.per, self.i * (self.per // 2)
        return Job(n % 2, a + (n + 1), b + n // 2, b + (n // 2 + 1))


def at(i, per, k):
    return k if i is None else i * per + k


def plan_ln(w):
    s, b, t = [], [], []
    for n in range(T + 1):
        if n < T:
            s.append(w.take())
            b.append(w.take())
        if n:
            t.append(w.take())
    return s, b, t


def plan_block(w):
    g = {}
    g["ln1"] = plan_ln(w)
    g["v"] = [w.take() for _ in range(T)]
    g["proj"], g["mrow"], g["den"], g["out"] = {}, {}, {}, {}
    g["proj"][0] = [w.take() for _ in range(6)]
    g["mrow"][0] = [w.take() for _ in range(3)]
    for h in range(HEADS):
        if h + 1 < HEADS:
            g["proj"][h + 1] = [w.take() for _ in range(6)]
            g["mrow"][h + 1] = None
        if h + 1 < HEADS:
            g["mrow"][h + 1] = [w.take() for _ in range(3)]
        g["den"][h] = w.take()
        g["out"][h] = [w.take() for _ in range(T)]
    g["ln2"] = plan_ln(w)
    g["up"] = [w.take() for _ in range(3 * KD)]
    g["down"] = [w.take() for _ in range(T)]
    return g


_w = Walk()
plan_block(_w)
LIN_PER_BLOCK = _w.n


def plan_post(w):
    g = {}

    def tiles(*names):
        for name in names:
            g[name] = [w.take() for _ in range(T)]

    def woven(*names):
        for name in names:
            g[name] = []
        for _ in range(T):
            for name in names:
                g[name].append(w.take())

    tiles("norm1", "beta1")
    g["count"] = w.take()
    woven("mean1", "self1")
    tiles("norm2")
    g["gate", 0] = w.take()
    tiles(("msg", 0, 0), ("agg", 0, 0), ("msg", 0, 1), ("agg", 0, 1), "turn2")
    g["gate", 1] = w.take()
    tiles(("msg", 1, 0), ("agg", 1, 0), ("msg", 1, 1), ("agg", 1, 1))
    tiles("norm3")
    g["degree"] = w.take()
    tiles(("sage", 0))
    woven(("mean3", 0), ("self3", 0))
    tiles("turn3", ("sage", 1))
    woven(("mean3", 1), ("self3", 1))
    return g


class Score:

    def __init__(self, n, kind, h, j, before):
        self.n, self.slot, self.kind, self.h, self.j, self.before = n, n % 2, kind, h, j, before


def plan_scores():
    out, last = [], [None, None]

    def add(kind, h, j):
        s = Score(len(out), kind, h, j, last[len(out) % 2])
        last[s.slot] = s
        out.append(s)

    for j in range(2 * T):
        add("max", 0, j)
    for h in range(HEADS):
        for j in range(2 * T):
            add("exp", h, j)
            if h + 1 < HEADS:
                add("max", h + 1, j)
    return out


SCORES = {(s.kind, s.h, s.j): s for s in plan_scores()}
SCORES_PER_BLOCK = len(SCORES)
EXPS = MAXES = HEADS * 2 * T


def build(nc, a, out):
    stack = ExitStack()
    with stack:
        def sem(name):
            return stack.enter_context(nc.semaphore(name))

        def sb_in(ctx):
            return lambda name, shape, dt: ctx.enter_context(nc.sbuf_tensor(name, shape, dt))

        sb = sb_in(stack)
        edge_slots = nc.dram_tensor("edge_slots", (128 * SLOTS, 2), F32, kind="Internal").ap()
        typed_t = nc.dram_tensor("typed_t", (2 * N, N), F16, kind="Internal").ap()
        crow_d = nc.dram_tensor("crow_d", (N, N), F16, kind="Internal").ap()

        x = sb("x", [P, T, D], F32)
        yT = sb("yT", [128, KD, N], F32)
        big = sb("big", [128, T * D], F32)
        vrow = big[0:P, :].rearrange("p (t d) -> p t d", d=D)
        hidT = big[:, 0:KD * N].rearrange("p (k n) -> p k n", n=N)
        w = [sb(f"w{s}", [128, KD, D], F32) for s in range(3)]
        ct = sb("ct", [P, T, N], F16)
        ident = sb("ident", [128, 128], F32)
        brow = sb("brow", [P, 3, D], F32)
        stats = sb("stats", [P, T, 6], F32)
        mv = sb("mv", [P, T, 2], F32)
        var = sb("var", [P, T], F32)
        rstd = sb("rstd", [P, T], F32)
        nmr = sb("nmr", [P, T], F32)
        mhalf = sb("mhalf", [P, T], F32)
        ones_f = sb("ones_f", [128, 1], F32)
        zcol = sb("zcol", [P, 1], F32)
        tick = sb("tick", [1, MAXES], F32)
        ps = stack.enter_context(nc.psum_tensor("ps", [128, 8 * 512], F32))

        def score_ps(slot, n):
            return ps[0:P, slot * 1024:slot * 1024 + n]

        def lin_ps(job, parts, n, c0=0):
            return ps[0:parts, 3072 + 512 * job.slot + c0:3072 + 512 * job.slot + c0 + n]

        o_ps = ps[:, 2048:3072]

        lin_full = sem("lin_full")
        lin_empty = [sem(f"lin_empty{s}") for s in range(2)]
        consts_set = sem("consts_set")
        edges_in = sem("edges_in")
        slots_init = sem("slots_init")
        rows_init = sem("rows_init")
        payload_ready = sem("payload_ready")
        ecount_ready = sem("ecount_ready")
        tri_done = sem("tri_done")
        scattered = sem("scattered")
        sorted_in = sem("sorted_in")
        onehot_ready = sem("onehot_ready")
        onehot_used = sem("onehot_used")
        group_full = sem("group_full")
        run_ready = sem("run_ready")
        rows_out = [sem(f"rows_out{s}") for s in range(2)]
        typed_in = [sem(f"typed_in{s}") for s in range(2)]
        ct_ready = sem("ct_ready")
        crow_ps_full = sem("crow_ps_full")
        crow_copied = sem("crow_copied")
        mneg_ready = sem("mneg_ready")
        crow_out = [sem(f"crow_out{s}") for s in range(2)]
        pre_in = sem("pre_in")
        phase_ready = sem("phase_ready")
        emb_ready = sem("emb_ready")
        silu_ready = sem("silu_ready")
        zexp_ready = sem("zexp_ready")
        var_ready = sem("var_ready")
        rstd_ready = sem("rstd_ready")
        norm_ready = sem("norm_ready")
        xn_ready = sem("xn_ready")
        x0_ready = sem("x0_ready")
        blk_done = sem("blk_done")
        blkc_in = sem("blkc_in")
        w_in = [sem(f"w_in{s}") for s in range(3)]
        hi_ready = sem("hi_ready")
        score_full = sem("score_full")
        exp_done = sem("exp_done")
        max_done = sem("max_done")
        neg_max_ready = sem("neg_max_ready")
        prob_ready = sem("prob_ready")
        pv_done = sem("pv_done")
        psum_done = sem("psum_done")
        o_copied = sem("o_copied")
        xbias_done = sem("xbias_done")
        out_done = sem("out_done")
        sums_read = sem("sums_read")

        keep = ExitStack()
        sk = sb_in(keep)
        mneg = sk("mneg", [P, T, N], BF16)
        condT = sk("condT", [COND + 1, N], F32)
        fw1 = sk("fw1", [2 * FREQS, COND], F32)
        fw2 = sk("fw2", [COND, COND], F32)
        fb1 = sk("fb1", [COND, 1], F32)
        fb2 = sk("fb2", [COND, 1], F32)
        freq = sk("freq", [2 * FREQS, 1], F32)
        quarter = sk("quarter", [2 * FREQS, 1], F32)
        noise = yT[0:2 * FREQS, 0, :]
        turns = yT[0:2 * FREQS, 1, :]
        whole = yT[0:2 * FREQS, 2, :]
        emb = yT[0:2 * FREQS, 3, :]
        z = hidT[0:COND, 0, :]
        zexp = hidT[0:COND, 1, :]
        silu = hidT[0:COND, 2, :]

        adj = ExitStack()
        sa = sb_in(adj)
        onehot_src = sa("onehot_src", [128, 4, N], F16)
        onehot_dst = sa("onehot_dst", [128, 4, P], F16)
        col_iota = sa("col_iota", [128, N], F16)
        run = sa("run", [P, 2, N], F16)
        typed = sa("typed", [P, 2, 2, N], F16)
        crow = sa("crow", [P, 2, N], F16)
        zero_row = sa("zero_row", [P, N], F16)
        ident16 = sa("ident16", [P, P], F16)
        pad = sa("pad", [128, SLOTS, 2], F32)
        esrc = sa("esrc", [P, EC], I32)
        edst = sa("edst", [P, EC], I32)
        etyp = sa("etyp", [P, EC], I32)
        key = sa("key", [P, EC], F32)
        thr = sa("thr", [P, BUCKETS + 1], F32)
        ge = yT[0:P, :, :].rearrange("p k n -> p (k n)")[:, 0:(BUCKETS + 1) * EC].rearrange("p (b c) -> p b c", c=EC)
        oh = mneg[:].rearrange("p t n -> p (t n)").bitcast(F32)[:, 0:BUCKETS * EC].rearrange("p (b c) -> p b c", c=EC)
        incl = big[0:P, 0:BUCKETS * EC].rearrange("p (b c) -> p b c", c=EC)
        zero = sa("zero", [128, 1], F32)
        bsum = sa("bsum", [P, EC], F32)
        payload = sa("payload", [P, EC, 2], F32)
        cnt = sa("cnt", [P, BUCKETS], F32)
        tri = sa("tri", [P, P], F32)
        ones_sq = sa("ones_sq", [P, 128], F32)
        toti = sa("toti", [128, BUCKETS], I32)
        ngr = sa("ngr", [128, BUCKETS], F32)
        egr = sa("egr", [128, BUCKETS], F32)
        base = sa("base", [P, BUCKETS], F32)
        base2 = sa("base2", [P, BUCKETS], F32)
        pos = sa("pos", [P, EC], F32)
        posi = sa("posi", [P, EC], I32)
        ia = sa("ia", [P, EC], I32)
        ib = sa("ib", [P, EC], I32)
        ic = sa("ic", [P, EC], I32)
        slot_idx = sa("slot_idx", [P, EC], I32)
        gi = sa("gi", [128, GROUPS + 1], F32)
        gcmp = sa("gcmp", [128, GROUPS + 1, BUCKETS], F32)
        bk = sa("bk", [128, GROUPS + 1], F32)
        same = sa("same", [128, GROUPS], F32)
        rowf = sa("rowf", [128, GROUPS], F32)
        rowi = sa("rowi", [128, GROUPS], I32)
        part = sa("part", [128, 1], F32)
        es = sa("es", [128, SLOTS, 2], F32)
        adj.close()

        att = ExitStack()
        sl = sb_in(att)
        qk_hi = sl("qk_hi", [128, 2, 2, N], F32R)
        qk_lo = sl("qk_lo", [128, 2, 2, N], F32R)
        prob = sl("prob", [P, 3, HALVES[0][1]], F32)
        pacc = sl("pacc", [P, N], F32)
        oT = sl("oT", [128, N], F32)
        xn = pacc[:, 0:2 * D].rearrange("p (s d) -> p s d", d=D)
        y = prob[:].rearrange("p s n -> p (s n)")[:, 0:2 * D].rearrange("p (s d) -> p s d", d=D)
        cw = sl("cw", [COND + 1, 4, D], F32)
        mrow = sl("mrow", [1, N], F32R)
        bcol = sl("bcol", [128, 3, KD], F32)
        mxp = sl("mxp", [P, T, 2], F32)
        nmx = sl("nmx", [P, T], F32)
        rden = sl("rden", [P, T], F32)
        ones_r = sl("ones_r", [1, 128], F32R)
        att.close()
        keep.close()

        post = ExitStack()
        so = sb_in(post)
        pieces = so("pieces", [P, 3, T, D], BF16)
        ct2 = so("ct2", [P, T, N], F16)
        agg = so("agg", [P, T, D], F32)
        ring = [so(f"basis{s}", [128, KD // 2, D], F32) for s in range(3)]
        py = so("py", [P, 2, D], F32)
        rest = so("rest", [P, 2, D], F32)
        prow = so("prow", [P, 2, D], F32)
        att_w = so("att_w", [128, 2, 2, BASES], F32)
        gate_w = so("gate_w", [128, 2, KD, 2], F32)
        gate = so("gate", [P, T, 2], F32)
        per_node = so("per_node", [P, T], F32)
        ones_h = so("ones_h", [P, 1], F16)
        post.close()
        mixed = [[big[:, r * KD * D:(r + 1) * KD * D].rearrange("p (k n) -> p k n", n=D) for r in range(2)],
                 [w[0], w[1]]]
        post_in = sem("post_in")
        pw_in = sem("pw_in")
        ct2_in = sem("ct2_in")
        ctr_in = sem("ctr_in")
        basis_in = [sem(f"basis_in{s}") for s in range(3)]
        basis_used = sem("basis_used")
        xout_ready = sem("xout_ready")
        row_ready = sem("row_ready")
        first_piece = sem("first_piece")
        pieces_ready = sem("pieces_ready")
        gate_exp = sem("gate_exp")
        gate_ready = sem("gate_ready")
        mixed_ready = sem("mixed_ready")
        agg_ready = sem("agg_ready")
        pbias_done = sem("pbias_done")
        tile_ready = sem("tile_ready")

        block = stack.enter_context(nc.Block())

        @block.sync
        def _(sp):
            for dst_, name in ((esrc, "src"), (edst, "dst"), (etyp, "edge_type_2")):
                sp.dma_start(dst_[:], a[name].rearrange("(p c) -> p c", c=EC)).then_inc(edges_in, 16)
            sp.dma_start(x[:], a["x"].rearrange("(t p) d -> p t d", p=P)).then_inc(pre_in, 16)
            for dst_, name in ((fw1, "L0_gnn_f_w1"), (fw2, "L0_gnn_f_w2"), (fb1, "f_b1"), (fb2, "f_b2")):
                sp.dma_start(dst_[:], a[name]).then_inc(pre_in, 16)
            for s, name in ((0, "wv"), (1, "wq"), (2, "wk")):
                sp.dma_start(w[s][:], a[name][0].rearrange("(k p) n -> p k n", p=128)).then_inc(w_in[s], 16)
            sp.wait_ge(consts_set, 1)
            sp.dma_start(edge_slots.rearrange("(p s) c -> p s c", p=128), pad[:]).then_inc(slots_init, 16)
            for b in range(BUCKETS):
                sp.dma_start(typed_t[b * P:(b + 1) * P, :], zero_row[:]).then_inc(rows_init, 16)
            sp.wait_ge(payload_ready, 1)
            sp.dma_start(noise, a["node_vec1"].partition_broadcast(2 * FREQS)).then_inc(phase_ready, 16)
            sp.wait_ge(scattered, 16 * EC)
            sp.dma_start(es[:], edge_slots.rearrange("(p s) c -> p s c", p=128)).then_inc(sorted_in, 16)
            for s in range(2):
                sp.wait_ge(rows_out[s], 16 * ((GROUPS + 1 - s) // 2))
            for t in range(T):
                if t >= 2:
                    sp.wait_ge(ct_ready, t - 1)
                for r in range(2):
                    sp.dma_start(typed[:, t % 2, r, :],
                                 typed_t[r * N + t * P:r * N + (t + 1) * P, :]).then_inc(typed_in[t % 2], 16)
            walk = Walk()
            walk.n = 8
            with sp.Fori(0, BLOCKS) as i:
                walk.enter(i, LIN_PER_BLOCK)
                g = plan_block(walk)
                sp.wait_ge(blk_done, at(i, 1, 1))
                sp.dma_start(brow[:], a["brow"][i].partition_broadcast(P)).then_inc(blkc_in, 16)
                sp.dma_start(cw[:], a["cw"][i]).then_inc(blkc_in, 16)
                sp.dma_start(bcol[:].rearrange("p k c -> p (k c)"), a["bcol"][i]).then_inc(blkc_in, 16)

                def load(s, name, j):
                    sp.dma_start(w[s][:], a[name][j].rearrange("(k p) n -> p k n", p=128)).then_inc(w_in[s], 16)

                sp.wait_ge(lin_full, g["v"][-1].full)
                load(0, "wo", i)
                sp.wait_ge(lin_full, g["proj"][HEADS - 1][-1].full)
                load(1, "m_w1", i)
                load(2, "m_w2", i)
                sp.wait_ge(lin_full, g["out"][HEADS - 1][-1].full)
                load(0, "wv", i + 1)
                sp.wait_ge(lin_full, g["up"][-1].full)
                load(1, "wq", i + 1)
                sp.wait_ge(lin_full, g["down"][-1].full)
                load(2, "wk", i + 1)
            walk.leave()
            sp.wait_ge(blk_done, BLOCKS + 1)
            sp.dma_start(big[0:P, :].rearrange("p (t d) -> p t d", d=D),
                         a["x"].rearrange("(t p) d -> p t d", p=P)).then_inc(post_in, 16)
            sp.dma_start(att_w[:].rearrange("p a r b -> p (a r b)"), a["att"].partition_broadcast(128)).then_inc(post_in, 16)
            sp.dma_start(gate_w[:].rearrange("p a k r -> p (a k r)"), a["gate_w"]).then_inc(post_in, 16)
            sp.dma_start(brow[:], a["post_rows"][0:3, :].partition_broadcast(P)).then_inc(post_in, 16)
            sp.dma_start(prow[:], a["post_rows"][3:5, :].partition_broadcast(P)).then_inc(post_in, 16)
            for n in range(2 * BASES * 2):
                layer, b, half = n // (2 * BASES), n // 2 % BASES, n % 2
                if n >= 3:
                    sp.wait_ge(basis_used, n - 2)
                sp.dma_start(ring[n % 3][:], a[f"basis{layer + 1}"][b, half * 256:(half + 1) * 256, :]
                             .rearrange("(k p) n -> p k n", p=128)).then_inc(basis_in[n % 3], 16)
            for t in range(T):
                sp.wait_ge(tile_ready, t + 1)
                sp.dma_start(out[t * P:(t + 1) * P, :], x[:, t, :]).then_inc(out_done, 16)
            sp.wait_ge(out_done, 16 * T)

        @block.gpsimd
        def _(pool):
            def drained_inc(s):
                nc.gpsimd.drain().then_inc(s, 1)

            nc.gpsimd.memset(pad[:], NO_NODE)
            nc.gpsimd.memset(zero_row[:], 0.0)
            drained_inc(consts_set)
            nc.gpsimd.iota(thr[:], pattern=[[P, BUCKETS + 1]], base=0, channel_multiplier=0,
                           allow_small_or_imprecise_dtypes=True)
            nc.gpsimd.memset(zero[:], 0.0)
            nc.gpsimd.memset(tri[:], 1.0)
            nc.gpsimd.memset(ones_sq[:], 1.0)
            nc.gpsimd.memset(ident[:], 0.0)
            nc.gpsimd.memset(ident16[:], 0.0)
            nc.gpsimd.memset(mhalf[:], -0.5)
            nc.gpsimd.memset(ones_f[:], 1.0)
            nc.gpsimd.memset(zcol[:], 0.0)
            nc.gpsimd.memset(tick[:], 0.0)
            nc.gpsimd.iota(gi[:], pattern=[[1, GROUPS + 1]], base=0, channel_multiplier=0,
                           allow_small_or_imprecise_dtypes=True)
            nc.gpsimd.iota(part[:], pattern=[[0, 1]], base=0, channel_multiplier=1,
                           allow_small_or_imprecise_dtypes=True)
            nc.gpsimd.iota(col_iota[:], pattern=[[1, N]], base=0, channel_multiplier=0,
                           allow_small_or_imprecise_dtypes=True)
            for half in range(2):
                rows = slice(half * FREQS, (half + 1) * FREQS)
                nc.gpsimd.drain()
                nc.gpsimd.iota(freq[rows, :], pattern=[[0, 1]], base=1, channel_multiplier=1,
                               allow_small_or_imprecise_dtypes=True)
                nc.gpsimd.memset(quarter[rows, :], 0.25 * half)
            nc.gpsimd.memset(condT[:], 1.0)
            nc.gpsimd.drain()
            nc.gpsimd.affine_select(out=tri[:], in_=tri[:], compare_op=ALU.is_gt, fill=0.0, base=0,
                                    pattern=[[1, P]], channel_multiplier=-1)
            nc.gpsimd.affine_select(out=ident[:], in_=ident[:], compare_op=ALU.not_equal, fill=1.0, base=0,
                                    pattern=[[-1, 128]], channel_multiplier=1)
            nc.gpsimd.affine_select(out=ident16[:], in_=ident16[:], compare_op=ALU.not_equal, fill=1.0, base=0,
                                    pattern=[[-1, P]], channel_multiplier=1)
            drained_inc(consts_set)
            pool.wait_ge(slots_init, 16)
            pool.wait_ge(payload_ready, 1)
            for c in range(EC):
                nc.gpsimd.indirect_dma_start(
                    out=edge_slots, out_offset=bass.IndirectOffsetOnAxis(ap=slot_idx[:, c:c + 1], axis=0),
                    in_=payload[:, c, :], in_offset=None,
                    bounds_check=128 * SLOTS - 1, oob_is_err=False).then_inc(scattered, 16)
            pool.wait_ge(var_ready, 1)
            nc.gpsimd.tensor_tensor(rstd[:], var[:], mhalf[:], ALU.pow).then_inc(rstd_ready, 1)
            pool.wait_ge(rows_init, 16 * BUCKETS)
            for g in range(GROUPS):
                pool.wait_ge(run_ready, g + 1)
                nc.gpsimd.indirect_dma_start(
                    out=typed_t, out_offset=bass.IndirectOffsetOnAxis(ap=rowi[0:P, g:g + 1], axis=0),
                    in_=run[:, g % 2, :], in_offset=None,
                    bounds_check=2 * N - 1, oob_is_err=False).then_inc(rows_out[g % 2], 16)
            with pool.Fori(0, BLOCKS) as i:
                for half in range(2):
                    pool.wait_ge(var_ready, at(i, 2, 2 + half))
                    nc.gpsimd.tensor_tensor(rstd[:], var[:], mhalf[:], ALU.pow).then_inc(rstd_ready, 1)
                    pool.wait_ge(xn_ready, at(i, 2 * T, T * (half + 1)))
                    pool.wait_ge(blkc_in, at(i, 48, 48))
                    nc.gpsimd.tensor_tensor(x[:], x[:], brow[:, 1 + half:2 + half, :].to_broadcast([P, T, D]),
                                            ALU.add).then_inc(xbias_done, 1)
                    if half:
                        continue
                    for h in range(HEADS):
                        for j in range(2 * T):
                            n = h * 2 * T + j
                            c0, nn = HALVES[j // T]
                            pool.wait_ge(prob_ready, at(i, EXPS, n + 1))
                            if j == 0 and h:
                                pool.wait_ge(sums_read, at(i, HEADS, h))
                            if j % T == 0:
                                nc.gpsimd.tensor_tensor(pacc[:, c0:c0 + nn], prob[:, n % 3, 0:nn],
                                                        zcol[:].to_broadcast([P, nn]), ALU.add).then_inc(psum_done, 1)
                            else:
                                pool.wait_ge(psum_done, at(i, EXPS, n))
                                nc.gpsimd.tensor_tensor(pacc[:, c0:c0 + nn], pacc[:, c0:c0 + nn], prob[:, n % 3, 0:nn],
                                                        ALU.add).then_inc(psum_done, 1)

            walk = Walk()
            walk.n = 8 + BLOCKS * LIN_PER_BLOCK
            g = plan_post(walk)
            pool.wait_ge(blk_done, BLOCKS + 1)
            nc.gpsimd.memset(ones_h[:], 1.0)
            nc.gpsimd.drain().then_inc(consts_set, 1)
            nc.gpsimd.dma_start(ct2[:], typed_t[N:2 * N, :].rearrange("(t p) n -> p t n", p=P)).then_inc(ct2_in, 16)
            pool.wait_ge(post_in, 80)

            def norm_power(count):
                pool.wait_ge(var_ready, count)
                nc.gpsimd.tensor_tensor(rstd[:], var[:], mhalf[:], ALU.pow).then_inc(rstd_ready, 1)

            def add_bias(rows, row, read):
                pool.wait_ge(row_ready, read)
                nc.gpsimd.tensor_tensor(x[:], x[:], rows[:, row:row + 1, :].to_broadcast([P, T, D]),
                                        ALU.add).then_inc(pbias_done, 1)

            def late_load(dst_, src_, job, signal):
                pool.wait_ge(lin_full, job.full)
                nc.gpsimd.dma_start(dst_, src_).then_inc(signal, 16)

            def matrix(name):
                return a[name].rearrange("(k p) n -> p k n", p=128)

            def count_rows(d):
                return d.rearrange("(t p) n -> p t n", p=P)

            norm_power(10)
            add_bias(brow, 0, T)
            late_load(ct[:], count_rows(typed_t[0:N, :]), g["mean1"][-1], ctr_in)
            norm_power(11)
            add_bias(brow, 2, 2 * T)
            late_load(w[2][:], matrix("root2"), g["agg", 0, 0][-1], pw_in)
            late_load(w[0][:], matrix("W1_l"), g["msg", 1, 0][-1], pw_in)
            late_load(ct[:], count_rows(crow_d), g["agg", 1, 0][-1], ctr_in)
            late_load(w[2][:], matrix("W2_l"), g["agg", 1, 0][-1], pw_in)
            late_load(w[1][:], matrix("W1_r"), g["msg", 1, 1][-1], pw_in)
            norm_power(12)
            add_bias(prow, 1, 4 * T)
            late_load(w[0][:], matrix("W2_r"), g["sage", 0][-1], pw_in)

        @block.vector
        def _(dve):
            V = nc.vector

            def statistics(count):
                V.drain()
                for t in range(T):
                    V.bn_stats(stats[:, t, :], x[:, t, :])
                V.drain()
                for t in range(T):
                    V.bn_aggr(mv[:, t, :], stats[:, t, :])
                V.drain()
                V.tensor_scalar(var[:], mv[:, :, 1], EPS, None, ALU.add).then_inc(var_ready, 1)
                dve.wait_ge(rstd_ready, count)
                V.scalar_tensor_tensor(out=nmr[:], in0=mv[:, :, 0], scalar=-1.0, in1=rstd[:],
                                       op0=ALU.mult, op1=ALU.mult).then_inc(norm_ready, 1)

            walk = Walk()
            jb, jt = walk.take(), walk.take()
            dve.wait_ge(edges_in, 48)
            dve.wait_ge(consts_set, 2)
            V.tensor_scalar(key[:], etyp[:], 0.0, float(N), ALU.not_equal, ALU.mult)
            V.drain()
            V.tensor_tensor(key[:], key[:], edst[:], ALU.add)
            V.drain()
            V.tensor_tensor(ge, key[:].unsqueeze(1).to_broadcast([P, BUCKETS + 1, EC]),
                            thr[:].unsqueeze(2).to_broadcast([P, BUCKETS + 1, EC]), ALU.is_ge)
            V.drain()
            V.tensor_tensor(oh, ge[:, 0:BUCKETS, :], ge[:, 1:BUCKETS + 1, :], ALU.subtract)
            V.tensor_reduce(bsum[:], ge[:, 1:BUCKETS, :].rearrange("p b c -> p c b"), AX.X, ALU.add)
            V.drain()
            V.tensor_reduce(cnt[:], oh, AX.X, ALU.add)
            V.tensor_tensor_scan(incl.rearrange("p b c -> p (b c)"), oh.rearrange("p b c -> p (b c)"),
                                 zero[0:P, :].to_broadcast([P, BUCKETS * EC]), 0.0, ALU.add, ALU.add)
            V.tensor_copy(payload[:, :, 0], esrc[:])
            V.scalar_tensor_tensor(out=payload[:, :, 1], in0=bsum[:], scalar=-float(P), in1=key[:],
                                   op0=ALU.mult, op1=ALU.add)
            V.drain().then_inc(ecount_ready, 1)
            dve.wait_ge(lin_full, jt.full)
            V.tensor_scalar(toti[:], lin_ps(jt, 128, BUCKETS), float(GROUP - 1), None,
                            ALU.add).then_inc(lin_empty[jt.slot], 1)
            V.tensor_copy(base[:], lin_ps(jb, P, BUCKETS)).then_inc(lin_empty[jb.slot], 1)
            V.drain()
            V.tensor_scalar(toti[:], toti[:], 9, None, ALU.logical_shift_right)
            V.drain()
            V.tensor_copy(ngr[:], toti[:])
            V.drain()
            V.tensor_tensor_scan(egr[:], ngr[:], zero[:].to_broadcast([128, BUCKETS]), 0.0, ALU.add, ALU.add)
            V.drain()
            V.tensor_tensor(base2[:], egr[0:P, :], ngr[0:P, :], ALU.subtract)
            V.drain()
            V.scalar_tensor_tensor(out=base[:], in0=base2[:], scalar=float(GROUP), in1=base[:],
                                   op0=ALU.mult, op1=ALU.add)
            V.drain()
            V.tensor_tensor(base[:, 1:], base[:, 1:], incl[:, 0:BUCKETS - 1, EC - 1], ALU.subtract)
            V.drain()
            V.tensor_tensor(incl, incl, base[:].unsqueeze(2).to_broadcast([P, BUCKETS, EC]), ALU.add)
            V.drain()
            V.tensor_tensor(incl, incl, oh, ALU.mult)
            V.drain()
            V.tensor_reduce(pos[:], incl.rearrange("p b c -> p c b"), AX.X, ALU.add)
            V.drain()
            V.tensor_scalar(posi[:], pos[:], -1.0, None, ALU.add)
            V.drain()
            V.tensor_scalar(ia[:], posi[:], 9, 2, ALU.logical_shift_right, ALU.logical_shift_left)
            V.tensor_scalar(ib[:], posi[:], 2, 127, ALU.logical_shift_right, ALU.bitwise_and)
            V.tensor_scalar(ic[:], posi[:], 3, None, ALU.bitwise_and)
            V.drain()
            V.scalar_tensor_tensor(out=pos[:], in0=ib[:], scalar=float(SLOTS), in1=ia[:], op0=ALU.mult, op1=ALU.add)
            V.drain()
            V.tensor_tensor(slot_idx[:], pos[:], ic[:], ALU.add)
            V.drain().then_inc(payload_ready, 1)
            V.tensor_tensor(gcmp[:], egr[:].unsqueeze(1).to_broadcast([128, GROUPS + 1, BUCKETS]),
                            gi[:].unsqueeze(2).to_broadcast([128, GROUPS + 1, BUCKETS]), ALU.is_le)
            V.drain()
            V.tensor_reduce(bk[:], gcmp[:], AX.X, ALU.add)
            V.drain()
            V.tensor_tensor(same[:], bk[:, 0:GROUPS], bk[:, 1:GROUPS + 1], ALU.is_equal)
            V.tensor_scalar(rowf[:], bk[:, 0:GROUPS], float(P), part[:], ALU.mult, ALU.add)
            V.drain()
            V.scalar_tensor_tensor(out=rowf[:], in0=same[:], scalar=1.0e6, in1=rowf[:], op0=ALU.mult, op1=ALU.add)
            V.drain()
            V.tensor_copy(rowi[:], rowf[:])

            dve.wait_ge(pre_in, 80)
            statistics(1)
            dve.wait_ge(phase_ready, 16)
            V.tensor_scalar(turns, noise, freq[:], 0.5 / 8.0, ALU.mult, ALU.mult)
            V.drain()
            V.tensor_scalar(turns, turns, quarter[:], None, ALU.add)
            V.drain()
            V.tensor_scalar(whole, turns, 12582912.0, -12582912.0, ALU.add, ALU.add)
            V.drain()
            V.tensor_tensor(turns, turns, whole, ALU.subtract)
            V.drain().then_inc(emb_ready, 1)
            dve.wait_ge(zexp_ready, 1)
            V.tensor_scalar(zexp, zexp, 1.0, None, ALU.add)
            V.drain()
            V.reciprocal(zexp, zexp)
            V.drain()
            V.tensor_tensor(silu, z, zexp, ALU.mult)
            V.drain().then_inc(silu_ready, 1)
            for _ in range(6):
                walk.take()

            dve.wait_ge(sorted_in, 16)
            for g in range(GROUPS):
                for j in range(STEPS):
                    n = g * STEPS + j
                    if n >= 4:
                        dve.wait_ge(onehot_used, n - 3)
                    V.tensor_scalar(onehot_dst[:, n % 4, :], col_iota[:, 0:P], es[:, n, 1:2], None, ALU.is_equal)
                    V.tensor_scalar(onehot_src[:, n % 4, :], col_iota[:], es[:, n, 0:1], None, ALU.is_equal)
                    V.drain().then_inc(onehot_ready, 1)
                dve.wait_ge(onehot_used, (g + 1) * STEPS)
                if g >= 2:
                    dve.wait_ge(rows_out[g % 2], 16 * (g // 2))
                gp = ps[0:P, (g % 2) * 1536:(g % 2) * 1536 + N]
                if g == 0:
                    V.tensor_copy(run[:, 0, :], gp).then_inc(run_ready, 1)
                else:
                    V.scalar_tensor_tensor(out=run[:, g % 2, :], in0=run[:, (g - 1) % 2, :], scalar=same[0:P, g - 1:g],
                                           in1=gp, op0=ALU.mult, op1=ALU.add).then_inc(run_ready, 1)
                V.drain()
            for t in range(T):
                dve.wait_ge(typed_in[t % 2], 32 * (t // 2 + 1))
                V.tensor_tensor(ct[:, t, :], typed[:, t % 2, 0, :], typed[:, t % 2, 1, :], ALU.add).then_inc(ct_ready, 1)
            for s in range(T):
                dve.wait_ge(crow_copied, s + 1)
                V.tensor_scalar(mneg[:, s, :], crow[:, s % 2, :], 0.0, -BIG, ALU.is_equal, ALU.mult).then_inc(mneg_ready, 1)
            dve.wait_ge(x0_ready, T)
            for s in range(2):
                dve.wait_ge(crow_out[s], 16 * (T // 2))
            V.memset(ones_r[:].bitcast(F32), 1.0)
            V.drain().then_inc(blk_done, 1)

            def shift_and_scale(jobs):
                s, b, tr = jobs
                for t in range(T):
                    dve.wait_ge(lin_full, s[t].full)
                    dve.wait_ge(xn_ready, xn_count(t))
                    if t >= 2:
                        dve.wait_ge(lin_full, tr[t - 2].full)
                    V.scalar_tensor_tensor(out=y[:, t % 2, :], in0=lin_ps(s[t], P, D), scalar=1.0, in1=xn[:, t % 2, :],
                                           op0=ALU.add, op1=ALU.mult).then_inc(lin_empty[s[t].slot], 1)
                    V.drain()
                    dve.wait_ge(lin_full, b[t].full)
                    V.tensor_tensor(y[:, t % 2, :], y[:, t % 2, :], lin_ps(b[t], P, D),
                                    ALU.add).then_inc(lin_empty[b[t].slot], 1)

            with dve.Fori(0, BLOCKS) as i:
                walk.enter(i, LIN_PER_BLOCK)
                g = plan_block(walk)
                statistics(at(i, 2, 2))
                xn_count = lambda t: at(i, 2 * T, t + 1)
                shift_and_scale(g["ln1"])
                dve.wait_ge(blkc_in, at(i, 48, 48))
                for t, job in enumerate(g["v"]):
                    dve.wait_ge(lin_full, job.full)
                    V.tensor_tensor(vrow[:, t, :], lin_ps(job, P, D), brow[:, 0, :], ALU.add).then_inc(lin_empty[job.slot], 1)

                def low_parts(h):
                    for n, job in enumerate(g["proj"][h]):
                        which, (c0, nn) = n // 3, COLS[n % 3]
                        dve.wait_ge(hi_ready, at(i, 6 * HEADS, 6 * h + n + 1))
                        V.scalar_tensor_tensor(out=qk_lo[:, h % 2, which, c0:c0 + nn], in0=lin_ps(job, 128, nn),
                                               scalar=bcol[:, which, h:h + 1],
                                               in1=qk_hi[:, h % 2, which, c0:c0 + nn].bitcast(F32),
                                               op0=ALU.add, op1=ALU.subtract).then_inc(lin_empty[job.slot], 1)

                def masked_max(h, j):
                    s = SCORES["max", h, j]
                    t, (c0, nn) = j // 2, HALVES[j % 2]
                    dve.wait_ge(score_full, at(i, SCORES_PER_BLOCK, s.n + 1))
                    V.tensor_tensor(tick[:, MAXES // HEADS * h + j:MAXES // HEADS * h + j + 1], zcol[0:1, :], zcol[0:1, :], ALU.add)
                    V.tensor_tensor_reduce(out=score_ps(s.slot, nn), in0=score_ps(s.slot, nn), in1=mneg[:, t, c0:c0 + nn],
                                           scale=1.0, scalar=-BIG, op0=ALU.add, op1=ALU.max,
                                           accum_out=mxp[:, t, j % 2:j % 2 + 1]).then_inc(max_done, 1)

                def negate_max(h):
                    V.drain()
                    V.tensor_tensor(nmx[:], mxp[:, :, 0], mxp[:, :, 1], ALU.max)
                    V.drain()
                    V.tensor_scalar(nmx[:], nmx[:], -1.0, None, ALU.mult)
                    V.drain().then_inc(neg_max_ready, 1)

                low_parts(0)
                for j in range(2 * T):
                    masked_max(0, j)
                negate_max(0)
                for h in range(HEADS):
                    if h + 1 < HEADS:
                        low_parts(h + 1)
                    for j in range(2 * T):
                        n = h * 2 * T + j
                        t, (c0, nn) = j % T, HALVES[j // T]
                        dve.wait_ge(exp_done, at(i, EXPS, n + 1))
                        V.scalar_tensor_tensor(out=prob[:, n % 3, 0:nn], in0=prob[:, n % 3, 0:nn], scalar=BIG,
                                               in1=ct[:, t, c0:c0 + nn], op0=ALU.min, op1=ALU.mult).then_inc(prob_ready, 1)
                        if h + 1 < HEADS:
                            masked_max(h + 1, j)
                    if h + 1 < HEADS:
                        negate_max(h + 1)
                    job = g["den"][h]
                    dve.wait_ge(lin_full, job.full)
                    V.tensor_scalar(rden[:], lin_ps(job, P, T), 1.0e-30, None, ALU.max).then_inc(lin_empty[job.slot], 1)
                    V.drain()
                    V.reciprocal(rden[:], rden[:])
                    V.drain().then_inc(sums_read, 1)
                    if h == 0:
                        dve.wait_ge(xbias_done, at(i, 2, 1))
                    for t, job in enumerate(g["out"][h]):
                        dve.wait_ge(lin_full, job.full)
                        V.scalar_tensor_tensor(out=x[:, t, :], in0=lin_ps(job, P, D), scalar=rden[:, t:t + 1],
                                               in1=x[:, t, :], op0=ALU.mult, op1=ALU.add).then_inc(lin_empty[job.slot], 1)
                statistics(at(i, 2, 3))
                xn_count = lambda t: at(i, 2 * T, T + t + 1)
                shift_and_scale(g["ln2"])
                dve.wait_ge(xbias_done, at(i, 2, 2))
                for t, job in enumerate(g["down"]):
                    dve.wait_ge(lin_full, job.full)
                    V.tensor_tensor(x[:, t, :], x[:, t, :], lin_ps(job, P, D), ALU.add).then_inc(lin_empty[job.slot], 1)
                V.drain().then_inc(blk_done, 1)
            walk.leave()

            g = plan_post(walk)
            units = [0]

            def mix(n):
                for _ in range(n):
                    u = units[0]
                    units[0] += 1
                    layer, b, half = u // (2 * BASES), u // 2 % BASES, u % 2
                    dve.wait_ge(basis_in[u % 3], 16 * (u // 3 + 1))
                    for r in range(2):
                        acc = mixed[layer][r][:, 2 * half:2 * half + 2, :]
                        scale = att_w[:, layer, r, b:b + 1]
                        if b == 0:
                            V.tensor_scalar(acc, ring[u % 3][:], scale, None, ALU.mult)
                        else:
                            V.scalar_tensor_tensor(out=acc, in0=ring[u % 3][:], scalar=scale, in1=acc,
                                                   op0=ALU.mult, op1=ALU.add)
                    V.drain().then_inc(basis_used, 1)
                    if u % (2 * BASES) == 2 * BASES - 1:
                        V.drain().then_inc(mixed_ready, 1)

            split = [0]

            def split_rows(jobs, scale, extra):
                for t, job in enumerate(jobs):
                    split[0] += 1
                    dve.wait_ge(first_piece, split[0])
                    if scale is None:
                        V.tensor_tensor(rest[:, t % 2, :], lin_ps(job, P, D), pieces[:, 0, t, :],
                                        ALU.subtract).then_inc(lin_empty[job.slot], 1)
                    else:
                        V.scalar_tensor_tensor(out=rest[:, t % 2, :], in0=lin_ps(job, P, D), scalar=scale(t),
                                               in1=pieces[:, 0, t, :], op0=ALU.mult,
                                               op1=ALU.subtract).then_inc(lin_empty[job.slot], 1)
                    V.drain()
                    V.tensor_copy(pieces[:, 1, t, :], rest[:, t % 2, :])
                    V.drain()
                    V.tensor_tensor(pieces[:, 2, t, :], rest[:, t % 2, :], pieces[:, 1, t, :], ALU.subtract)
                    V.drain().then_inc(pieces_ready, 1)
                    mix(extra)

            def add_to(rows, t, job, scale=None):
                dve.wait_ge(lin_full, job.full)
                if scale is None:
                    return V.tensor_tensor(rows[:, t, :], rows[:, t, :], lin_ps(job, P, D), ALU.add)
                return V.scalar_tensor_tensor(out=rows[:, t, :], in0=lin_ps(job, P, D), scalar=scale, in1=rows[:, t, :],
                                              op0=ALU.mult, op1=ALU.add)

            dve.wait_ge(post_in, 80)
            V.tensor_tensor(x[:], x[:], big[0:P, :].rearrange("p (t d) -> p t d", d=D), ALU.add)
            statistics(10)
            mix(6)
            split_rows(g["beta1"], None, 1)
            job = g["count"]
            dve.wait_ge(lin_full, job.full)
            V.reciprocal(per_node[:], lin_ps(job, P, T)).then_inc(lin_empty[job.slot], 1)
            V.drain()
            dve.wait_ge(pbias_done, 1)
            for t in range(T):
                job = g["mean1"][t]
                add_to(x, t, job, per_node[:, t:t + 1]).then_inc(lin_empty[job.slot], 1)
                V.drain()
                job = g["self1"][t]
                add_to(x, t, job).then_inc(lin_empty[job.slot], 1)
                mix(3)

            statistics(11)
            mix(14)

            def gates(layer):
                dve.wait_ge(gate_exp, layer + 1)
                V.tensor_scalar(gate[:], gate[:], 1.0, None, ALU.add)
                V.drain()
                V.reciprocal(gate[:], gate[:])
                V.drain().then_inc(gate_ready, 1)

            gates(0)
            for r in range(2):
                split_rows(g["msg", 0, r], lambda t: gate[:, t, r:r + 1], 1)
                for t, job in enumerate(g["agg", 0, r]):
                    if r == 0:
                        dve.wait_ge(lin_full, job.full)
                        V.tensor_tensor(agg[:, t, :], lin_ps(job, P, D), brow[:, 1, :], ALU.add).then_inc(lin_empty[job.slot], 1)
                    else:
                        add_to(agg, t, job).then_inc(lin_empty[job.slot], 1)
                        V.drain().then_inc(agg_ready, 1)
                    mix(2)
            gates(1)
            dve.wait_ge(pbias_done, 2)
            for r in range(2):
                split_rows(g["msg", 1, r], lambda t: gate[:, t, r:r + 1], 0)
                for t, job in enumerate(g["agg", 1, r]):
                    add_to(x, t, job).then_inc(lin_empty[job.slot], 1)
                V.drain()

            statistics(12)
            job = g["degree"]
            dve.wait_ge(lin_full, job.full)
            V.tensor_scalar(per_node[:], lin_ps(job, P, T), 1.0, None, ALU.max).then_inc(lin_empty[job.slot], 1)
            V.drain()
            V.reciprocal(per_node[:], per_node[:])
            V.drain()
            split_rows(g["sage", 0], None, 0)
            for t in range(T):
                job = g["mean3", 0][t]
                dve.wait_ge(lin_full, job.full)
                V.scalar_tensor_tensor(out=agg[:, t, :], in0=lin_ps(job, P, D), scalar=per_node[:, t:t + 1],
                                       in1=prow[:, 0, :], op0=ALU.mult, op1=ALU.add).then_inc(lin_empty[job.slot], 1)
                V.drain()
                job = g["self3", 0][t]
                add_to(agg, t, job).then_inc(lin_empty[job.slot], 1)
                V.drain().then_inc(agg_ready, 1)
            split_rows(g["sage", 1], None, 0)
            dve.wait_ge(pbias_done, 3)
            for t in range(T):
                job = g["mean3", 1][t]
                add_to(x, t, job, per_node[:, t:t + 1]).then_inc(lin_empty[job.slot], 1)
                V.drain()
                job = g["self3", 1][t]
                add_to(x, t, job).then_inc(lin_empty[job.slot], 1)
                V.drain().then_inc(tile_ready, 1)

        @block.scalar
        def _(act):
            A = nc.scalar
            walk = Walk()
            walk.take(), walk.take()
            act.wait_ge(norm_ready, 1)
            for t in range(T):
                A.activation(x[:, t, :], x[:, t, :], ACT.Relu, bias=nmr[:, t:t + 1], scale=rstd[:, t:t + 1]).then_inc(x0_ready, 1)
            act.wait_ge(emb_ready, 1)
            A.activation(emb, turns, ACT.Sin, scale=6.2831850)
            A.drain().then_inc(emb_ready, 1)
            hj = [walk.take() for _ in range(3)]
            for (c0, nn), job in zip(COLS, hj):
                act.wait_ge(lin_full, job.full)
                A.activation(z[:, c0:c0 + nn], lin_ps(job, COND, nn), ACT.Identity, bias=fb1[:]).then_inc(lin_empty[job.slot], 1)
            A.drain()
            A.activation(zexp, z, ACT.Exp, scale=-1.0).then_inc(zexp_ready, 1)
            cj = [walk.take() for _ in range(3)]
            for (c0, nn), job in zip(COLS, cj):
                act.wait_ge(lin_full, job.full)
                A.activation(condT[0:COND, c0:c0 + nn], lin_ps(job, COND, nn), ACT.Identity,
                             bias=fb2[:]).then_inc(lin_empty[job.slot], 1)
            for s in range(T):
                act.wait_ge(crow_ps_full, s + 1)
                if s >= 2:
                    act.wait_ge(crow_out[s % 2], 16 * (s // 2))
                    act.wait_ge(mneg_ready, s - 1)
                src_ps = ps[0:P, (s % 2) * 1024:(s % 2) * 1024 + 1024].bitcast(F16)
                for t0, nt in ((0, 8), (8, T - 8)):
                    A.activation(crow[:, s % 2, t0 * P:(t0 + nt) * P].rearrange("p (t n) -> p t n", n=P),
                                 src_ps[:, t0 * 128:t0 * 128 + nt * (P + 1)].rearrange("p (t n) -> p t n", n=P + 1)[:, :, 0:P],
                                 ACT.Copy)
                A.drain().then_inc(crow_copied, 1)
                act.wait_ge(crow_copied, s + 1)
                act.dma_start(crow_d[s * P:(s + 1) * P, :], crow[:, s % 2, :]).then_inc(crow_out[s % 2], 16)

            def norm(jobs, count):
                s, b, tr = jobs
                act.wait_ge(norm_ready, count)
                for t in range(T + 1):
                    if t < T:
                        if t >= 2:
                            act.wait_ge(lin_empty[b[t - 2].slot], b[t - 2].emptied)
                        A.activation(xn[:, t % 2, :], x[:, t, :], ACT.Identity, bias=nmr[:, t:t + 1],
                                     scale=rstd[:, t:t + 1]).then_inc(xn_ready, 1)
                    if t:
                        job = tr[t - 1]
                        act.wait_ge(lin_full, job.full)
                        A.activation(yT[:, :, (t - 1) * P:t * P],
                                     lin_ps(job, 128, KD * P).rearrange("p (k n) -> p k n", k=KD),
                                     ACT.Copy).then_inc(lin_empty[job.slot], 1)

            with act.Fori(0, BLOCKS) as i:
                walk.enter(i, LIN_PER_BLOCK)
                g = plan_block(walk)
                act.wait_ge(blkc_in, at(i, 48, 48))
                norm(g["ln1"], at(i, 2, 2))

                def high_parts(h):
                    for n, job in enumerate(g["proj"][h]):
                        which, (c0, nn) = n // 3, COLS[n % 3]
                        act.wait_ge(lin_full, job.full)
                        A.activation(qk_hi[:, h % 2, which, c0:c0 + nn], lin_ps(job, 128, nn), ACT.Identity,
                                     bias=bcol[:, which, h:h + 1]).then_inc(hi_ready, 1)

                def max_row(h):
                    for n, job in enumerate(g["mrow"][h]):
                        c0, c1 = 4 * n * P, min(4 * n + 4, T) * P
                        act.wait_ge(lin_full, job.full)
                        A.activation(mrow[:, c0:c1], lin_ps(job, 1, c1 - c0), ACT.Copy).then_inc(lin_empty[job.slot], 1)

                def copy_o(h, half):
                    c0, nn = HALVES[half]
                    act.wait_ge(pv_done, at(i, EXPS, h * 2 * T + (half + 1) * T))
                    A.activation(oT[:, c0:c0 + nn], o_ps[:, 0:nn], ACT.Copy).then_inc(o_copied, 1)

                high_parts(0)
                max_row(0)
                for h in range(HEADS):
                    if h + 1 < HEADS:
                        high_parts(h + 1)
                    for j in range(2 * T):
                        s, n = SCORES["exp", h, j], h * 2 * T + j
                        nn = HALVES[j // T][1]
                        act.wait_ge(score_full, at(i, SCORES_PER_BLOCK, s.n + 1))
                        if n >= 3:
                            act.wait_ge(pv_done, at(i, EXPS, n - 2))
                            act.wait_ge(psum_done, at(i, EXPS, n - 2))
                        A.activation(prob[:, n % 3, 0:nn], score_ps(s.slot, nn), ACT.Exp, scale=DH ** -0.5).then_inc(exp_done, 1)
                        if j == T:
                            copy_o(h, 0)
                    copy_o(h, 1)
                    if h + 1 < HEADS:
                        max_row(h + 1)
                norm(g["ln2"], at(i, 2, 3))
                for n, job in enumerate(g["up"]):
                    k, (c0, nn) = n // 3, COLS[n % 3]
                    act.wait_ge(lin_full, job.full)
                    A.activation(hidT[:, k, c0:c0 + nn], lin_ps(job, 128, nn), ACT.Relu,
                                 bias=bcol[:, 2, k:k + 1]).then_inc(lin_empty[job.slot], 1)
            walk.leave()

            g = plan_post(walk)
            rows_made = [0]

            def turned(jobs, src_, func, to, ready=None, first=None, scaled=True):
                for t in range(T + 1):
                    if t < T:
                        if ready is not None:
                            act.wait_ge(ready, first + t + 1)
                        if t >= 2:
                            act.wait_ge(lin_full, jobs[t - 2].full)
                        if scaled:
                            A.activation(py[:, t % 2, :], src_[:, t, :], func, bias=nmr[:, t:t + 1],
                                         scale=rstd[:, t:t + 1]).then_inc(row_ready, 1)
                        else:
                            A.activation(py[:, t % 2, :], src_[:, t, :], func).then_inc(row_ready, 1)
                    if t:
                        job = jobs[t - 1]
                        act.wait_ge(lin_full, job.full)
                        A.activation(to[:, :, (t - 1) * P:t * P],
                                     lin_ps(job, 128, KD * P).rearrange("p (k n) -> p k n", k=KD),
                                     ACT.Copy).then_inc(lin_empty[job.slot], 1)

            def first_parts(jobs, scale=None):
                for t, job in enumerate(jobs):
                    act.wait_ge(lin_full, job.full)
                    A.activation(pieces[:, 0, t, :], lin_ps(job, P, D), ACT.Copy,
                                 scale=1.0 if scale is None else scale(t)).then_inc(first_piece, 1)

            def gate_logits(layer):
                job = g["gate", layer]
                act.wait_ge(lin_full, job.full)
                A.activation(gate[:].rearrange("p t r -> p (t r)"), lin_ps(job, P, 2 * T), ACT.Exp,
                             scale=-1.0).then_inc(lin_empty[job.slot], 1)
                A.drain().then_inc(gate_exp, 1)
                act.wait_ge(gate_ready, layer + 1)

            act.wait_ge(norm_ready, 10)
            turned(g["norm1"], x, ACT.Relu, yT)
            first_parts(g["beta1"])
            act.wait_ge(norm_ready, 11)
            turned(g["norm2"], x, ACT.Relu, yT)
            gate_logits(0)
            for r in range(2):
                first_parts(g["msg", 0, r], lambda t: gate[:, t, r:r + 1])
            turned(g["turn2"], agg, ACT.Relu, hidT, ready=agg_ready, first=0, scaled=False)
            gate_logits(1)
            for r in range(2):
                first_parts(g["msg", 1, r], lambda t: gate[:, t, r:r + 1])
            act.wait_ge(norm_ready, 12)
            turned(g["norm3"], x, ACT.Relu, yT)
            first_parts(g["sage", 0])
            turned(g["turn3"], agg, ACT.Tanh, hidT, ready=agg_ready, first=T, scaled=False)
            first_parts(g["sage", 1])

        @block.tensor
        def _(pe):
            mm = nc.tensor.matmul
            walk = Walk()

            def reuse(job):
                if job.reuse is not None:
                    pe.wait_ge(lin_empty[job.slot], job.reuse)

            jb, jt = walk.take(), walk.take()
            pe.wait_ge(consts_set, 2)
            pe.wait_ge(ecount_ready, 1)
            mm(lin_ps(jb, P, BUCKETS), tri[:], cnt[:], start=True, stop=True).then_inc(lin_full, 1)
            mm(lin_ps(jt, 128, BUCKETS), ones_sq[:], cnt[:], start=True, stop=True).then_inc(lin_full, 1)
            hj = [walk.take() for _ in range(3)]
            pe.wait_ge(pre_in, 80)
            pe.wait_ge(emb_ready, 2)
            for (c0, nn), job in zip(COLS, hj):
                reuse(job)
                mm(lin_ps(job, COND, nn), fw1[:], emb[:, c0:c0 + nn], start=True, stop=True).then_inc(lin_full, 1)
            cj = [walk.take() for _ in range(3)]
            pe.wait_ge(silu_ready, 1)
            for (c0, nn), job in zip(COLS, cj):
                reuse(job)
                mm(lin_ps(job, COND, nn), fw2[:], silu[:, c0:c0 + nn], start=True, stop=True).then_inc(lin_full, 1)
            for g in range(GROUPS):
                if g >= 2:
                    pe.wait_ge(run_ready, g - 1)
                for j in range(STEPS):
                    n = g * STEPS + j
                    pe.wait_ge(onehot_ready, n + 1)
                    for c0, nn in WIDE:
                        last = mm(ps[0:P, (g % 2) * 1536 + c0:(g % 2) * 1536 + c0 + nn], onehot_dst[:, n % 4, :],
                                  onehot_src[:, n % 4, c0:c0 + nn], start=(j == 0), stop=(j == STEPS - 1))
                    last.then_inc(onehot_used, 1)
            pe.wait_ge(run_ready, GROUPS)
            for s in range(T):
                if s >= 2:
                    pe.wait_ge(crow_copied, s - 1)
                dst_ps = ps[0:P, (s % 2) * 1024:(s % 2) * 1024 + 1024].bitcast(F16)
                for t in range(T):
                    if s == 0:
                        pe.wait_ge(ct_ready, t + 1)
                    c0 = t * (P + 1) if t < 8 else 1024 + (t - 8) * (P + 1)
                    last = nc.tensor.transpose(dst_ps[:, c0:c0 + P], ct[:, t, s * P:(s + 1) * P], ident16[:])
                last.then_inc(crow_ps_full, 1)
            pe.wait_ge(crow_copied, T)

            def affine_and_transpose(jobs):
                s, b, tr = jobs
                for t in range(T + 1):
                    if t < T:
                        for n, job in enumerate((s[t], b[t])):
                            reuse(job)
                            mm(lin_ps(job, P, D), condT[:, t * P:(t + 1) * P], cw[:, kind + n, :],
                               start=True, stop=True).then_inc(lin_full, 1)
                    if t:
                        job, prev = tr[t - 1], b[t - 1]
                        reuse(job)
                        pe.wait_ge(lin_empty[prev.slot], prev.emptied)
                        for k in range(KD):
                            last = nc.tensor.transpose(lin_ps(job, 128, P, k * P), y[:, (t - 1) % 2, k * 128:(k + 1) * 128],
                                                       ident[0:P, 0:P])
                        last.then_inc(lin_full, 1)
                for job in tr[T - 2:]:
                    pe.wait_ge(lin_empty[job.slot], job.emptied)

            def row_product(job, lhs, t, weight):
                reuse(job)
                for k in range(KD):
                    last = mm(lin_ps(job, P, D), lhs[:, k, t * P:(t + 1) * P], weight[:, k, :],
                              start=(k == 0), stop=(k == KD - 1))
                last.then_inc(lin_full, 1)

            def col_product(job, lhs, chunk, weight, m):
                c0, nn = COLS[chunk]
                reuse(job)
                for k in range(KD):
                    last = mm(lin_ps(job, 128, nn), weight[:, k, m * 128:(m + 1) * 128], lhs[:, k, c0:c0 + nn],
                              start=(k == 0), stop=(k == KD - 1))
                last.then_inc(lin_full, 1)

            with pe.Fori(0, BLOCKS) as i:
                walk.enter(i, LIN_PER_BLOCK)
                g = plan_block(walk)
                pe.wait_ge(blkc_in, at(i, 48, 48))
                kind = 0
                affine_and_transpose(g["ln1"])
                pe.wait_ge(w_in[0], at(i, 32, 16))
                for t, job in enumerate(g["v"]):
                    row_product(job, yT, t, w[0])
                pe.wait_ge(w_in[1], at(i, 32, 16))
                pe.wait_ge(w_in[2], at(i, 32, 16))

                def project(h):
                    for n, job in enumerate(g["proj"][h]):
                        col_product(job, yT, n % 3, w[1 + n // 3], h)

                def projected(h):
                    for job in g["proj"][h][-2:]:
                        pe.wait_ge(lin_empty[job.slot], job.emptied)

                def slot_free(s):
                    if s.before is not None:
                        b = s.before
                        if b.kind == "max":
                            pe.wait_ge(max_done, at(i, MAXES, b.h * 2 * T + b.j + 1))
                        else:
                            pe.wait_ge(exp_done, at(i, EXPS, b.h * 2 * T + b.j + 1))

                def max_scores(h, j):
                    s = SCORES["max", h, j]
                    t, (c0, nn) = j // 2, HALVES[j % 2]
                    slot_free(s)
                    for b0 in (0, 512):
                        bn = min(nn - b0, 512)
                        last = mm(score_ps(s.slot, nn)[:, b0:b0 + bn], qk_hi[:, h % 2, 0, t * P:(t + 1) * P],
                                  qk_hi[:, h % 2, 1, c0 + b0:c0 + b0 + bn], start=True, stop=True)
                    last.then_inc(score_full, 1)

                def exp_scores(h, j):
                    s = SCORES["exp", h, j]
                    t, (c0, nn) = j % T, HALVES[j // T]
                    slot_free(s)
                    rows = slice(t * P, (t + 1) * P)
                    hi, lo = qk_hi[:, h % 2, :, :], qk_lo[:, h % 2, :, :]
                    for b0 in (0, 512):
                        bn = min(nn - b0, 512)
                        cols = slice(c0 + b0, c0 + b0 + bn)
                        o = score_ps(s.slot, nn)[:, b0:b0 + bn]
                        mm(o, hi[:, 1, rows], hi[:, 0, cols], start=True, stop=False)
                        mm(o, hi[:, 1, rows], lo[:, 0, cols], start=False, stop=False)
                        mm(o, lo[:, 1, rows], hi[:, 0, cols], start=False, stop=False)
                        last = mm(o, ones_r[:, 0:P], mrow[:, cols], start=False, stop=True)
                    last.then_inc(score_full, 1)

                def weighted_values(h, j):
                    n, t, (c0, nn) = h * 2 * T + j, j % T, HALVES[j // T]
                    pe.wait_ge(prob_ready, at(i, EXPS, n + 1))
                    if t == 0 and n >= T:
                        pe.wait_ge(o_copied, at(i, 2 * HEADS, n // T))
                    for b0 in (0, 512):
                        bn = min(nn - b0, 512)
                        last = mm(o_ps[:, b0:b0 + bn], vrow[:, t, h * DH:(h + 1) * DH], prob[:, n % 3, b0:b0 + bn],
                                  start=(t == 0), stop=(t == T - 1))
                    last.then_inc(pv_done, 1)

                def max_row(h):
                    pe.wait_ge(neg_max_ready, at(i, HEADS, h + 1))
                    for n, job in enumerate(g["mrow"][h]):
                        reuse(job)
                        tiles = range(4 * n, min(4 * n + 4, T))
                        for t in tiles:
                            last = mm(lin_ps(job, 1, P, (t - 4 * n) * P), nmx[:, t:t + 1], ident[0:P, 0:P],
                                      start=True, stop=True)
                        last.then_inc(lin_full, 1)
                    for job in g["mrow"][h][-2:]:
                        pe.wait_ge(lin_empty[job.slot], job.emptied)

                project(0)
                for job in g["v"][-2:]:
                    pe.wait_ge(lin_empty[job.slot], job.emptied)
                projected(0)
                for j in range(2 * T):
                    max_scores(0, j)
                max_row(0)
                for h in range(HEADS):
                    if h + 1 < HEADS:
                        project(h + 1)
                        projected(h + 1)
                    for j in range(2 * T):
                        exp_scores(h, j)
                        if h + 1 < HEADS:
                            max_scores(h + 1, j)
                        if j:
                            weighted_values(h, j - 1)
                    weighted_values(h, 2 * T - 1)
                    if h + 1 < HEADS:
                        max_row(h + 1)
                    job = g["den"][h]
                    reuse(job)
                    pe.wait_ge(psum_done, at(i, EXPS, (h + 1) * 2 * T))
                    for t in range(T):
                        last = mm(lin_ps(job, P, 1, t), pacc[:, t * P:(t + 1) * P], ones_f[0:P, 0:1], start=True, stop=True)
                    last.then_inc(lin_full, 1)
                    if h == 0:
                        pe.wait_ge(w_in[0], at(i, 32, 32))
                    pe.wait_ge(o_copied, at(i, 2 * HEADS, 2 * h + 2))
                    for t, job in enumerate(g["out"][h]):
                        reuse(job)
                        mm(lin_ps(job, P, D), oT[:, t * P:(t + 1) * P], w[0][:, h, :], start=True, stop=True).then_inc(lin_full, 1)
                kind = 2
                affine_and_transpose(g["ln2"])
                pe.wait_ge(w_in[1], at(i, 32, 32))
                for n, job in enumerate(g["up"]):
                    col_product(job, yT, n % 3, w[1], n // 3)
                for job in g["up"][-2:]:
                    pe.wait_ge(lin_empty[job.slot], job.emptied)
                pe.wait_ge(w_in[2], at(i, 32, 32))
                for t, job in enumerate(g["down"]):
                    row_product(job, hidT, t, w[2])
            walk.leave()


            g = plan_post(walk)
            rows_turned = [0]
            split = [0]

            def turn(jobs):
                for t, job in enumerate(jobs):
                    reuse(job)
                    rows_turned[0] += 1
                    pe.wait_ge(row_ready, rows_turned[0])
                    for k in range(KD):
                        last = nc.tensor.transpose(lin_ps(job, 128, P, k * P), py[:, t % 2, k * 128:(k + 1) * 128],
                                                   ident[0:P, 0:P])
                    last.then_inc(lin_full, 1)
                for job in jobs[-2:]:
                    pe.wait_ge(lin_empty[job.slot], job.emptied)

            def gather(job, counts, t, first, self_=None):
                reuse(job)
                if self_ is not None:
                    lhs, weight = self_
                    for k in range(KD):
                        mm(lin_ps(job, P, D), lhs[:, k, t * P:(t + 1) * P], weight[:, k, :], start=(k == 0), stop=False)
                for k in range(T):
                    if t == 0:
                        pe.wait_ge(pieces_ready, first + k + 1)
                    for piece in range(3):
                        last = mm(lin_ps(job, P, D), counts[:, k, t * P:(t + 1) * P], pieces[:, piece, k, :],
                                  start=(self_ is None and k == 0 and piece == 0), stop=(k == T - 1 and piece == 2))
                last.then_inc(lin_full, 1)

            def edge_counts(job, mats):
                reuse(job)
                for t in range(T):
                    for k in range(T):
                        last = mm(lin_ps(job, P, 1, t), mats[:, k, t * P:(t + 1) * P], ones_h[:], start=(k == 0), stop=(k == T - 1))
                last.then_inc(lin_full, 1)

            pe.wait_ge(consts_set, 3)
            turn(g["norm1"])
            pe.wait_ge(w_in[0], 32 * BLOCKS + 16)
            for t, job in enumerate(g["beta1"]):
                row_product(job, yT, t, w[0])
            edge_counts(g["count"], ct)
            pe.wait_ge(w_in[1], 32 * BLOCKS + 16)
            for t in range(T):
                gather(g["mean1"][t], ct, t, 0)
                row_product(g["self1"][t], yT, t, w[1])

            turn(g["norm2"])
            pe.wait_ge(w_in[2], 32 * BLOCKS + 16)
            pe.wait_ge(ctr_in, 16)
            pe.wait_ge(ct2_in, 16)
            for layer, lhs in ((0, yT), (1, hidT)):
                job = g["gate", layer]
                reuse(job)
                for t in range(T):
                    for k in range(KD):
                        last = mm(lin_ps(job, P, 2, 2 * t), lhs[:, k, t * P:(t + 1) * P], gate_w[:, layer, k, :],
                                  start=(k == 0), stop=(k == KD - 1))
                last.then_inc(lin_full, 1)
                pe.wait_ge(mixed_ready, layer + 1)
                if layer:
                    pe.wait_ge(pw_in, 16)
                for r, counts in ((0, ct), (1, ct2)):
                    for t, job in enumerate(g["msg", layer, r]):
                        row_product(job, lhs, t, mixed[layer][r])
                    for t, job in enumerate(g["agg", layer, r]):
                        gather(job, counts, t, T * (1 + 2 * layer + r), (lhs, w[2]) if r == 0 else None)
                if layer == 0:
                    turn(g["turn2"])

            turn(g["norm3"])
            pe.wait_ge(ctr_in, 32)
            edge_counts(g["degree"], ct)
            pe.wait_ge(pw_in, 64)
            for t, job in enumerate(g["sage", 0]):
                row_product(job, yT, t, w[0])
            for t in range(T):
                gather(g["mean3", 0][t], ct, t, 5 * T)
                row_product(g["self3", 0][t], yT, t, w[1])
            turn(g["turn3"])
            for t, job in enumerate(g["sage", 1]):
                row_product(job, hidT, t, w[2])
            pe.wait_ge(pw_in, 80)
            for t in range(T):
                gather(g["mean3", 1][t], ct, t, 6 * T)
                row_product(g["self3", 1][t], hidT, t, w[0])


def kernel(**inputs):
    import concourse.bacc as bacc
    from concourse.bass_utils import run_bass_kernel_spmd as launch

    c = np.ascontiguousarray
    g = {k: np.asarray(v) for k, v in inputs.items()}
    L0 = {k[7:]: v for k, v in g.items() if k.startswith("L0_gnn_")}
    arrays = {
        "x": c(g["x"]), "src": c(g["src"]), "dst": c(g["dst"]), "edge_type_2": c(g["edge_type_2"]),
        "node_vec1": c(g["node_vec1"].reshape(N)),
        "L0_gnn_f_w1": c(L0["f_w1"]), "L0_gnn_f_w2": c(L0["f_w2"]),
        "f_b1": c(L0["f_b1"].reshape(COND, 1)), "f_b2": c(L0["f_b2"].reshape(COND, 1)),
        "wv": c(np.concatenate([L0["wv"], g["L1_gnn_wn"][None]])),
        "wq": c(np.concatenate([L0["wq"], g["L1_gnn_wc"][None]])),
        "wk": c(np.concatenate([L0["wk"], g["L2_gnn_root1"][None]])),
        "wo": c(L0["wo"]), "m_w1": c(L0["m_w1"]), "m_w2": c(L0["m_w2"]),
        "brow": c(np.stack([L0["bv"], L0["bo"], L0["m_b2"]], 1)),
        "bcol": c(np.stack([L0["bq"], L0["bk"], L0["m_b1"]], 1).reshape(BLOCKS, 3, KD, 128)
                  .transpose(0, 3, 1, 2).reshape(BLOCKS, 128, 3 * KD)),
        "cw": c(np.stack([np.concatenate([L0[m + "_w"], L0[m + "_b"][:, None, :]], 1)
                          for m in ("s1", "b1", "s2", "b2")], 2)),
    }
    arrays.update({
        "basis1": c(g["L2_gnn_basis1"]), "basis2": c(g["L2_gnn_basis2"]),
        "att": c(np.stack([g["L2_gnn_att1"], g["L2_gnn_att2"]]).reshape(-1)),
        "gate_w": c(np.stack([g["L2_gnn_gate_w1"], g["L2_gnn_gate_w2"]])[..., 0]
                    .reshape(2, 2, KD, 128).transpose(3, 0, 2, 1).reshape(128, 4 * KD)),
        "root2": c(g["L2_gnn_root2"]),
        "post_rows": c(np.stack([g["L1_gnn_bias"], g["L2_gnn_bias1"], g["L2_gnn_bias2"], g["L3_gnn_b1"], g["L3_gnn_b2"]])),
        "W1_l": c(g["L3_gnn_W1_l"].T), "W1_r": c(g["L3_gnn_W1_r"].T),
        "W2_l": c(g["L3_gnn_W2_l"].T), "W2_r": c(g["L3_gnn_W2_r"].T),
    })
    nc = bacc.Bacc("TRN2", target_bir_lowering=False, num_devices=1, dynamic_dma_scratch_size=8192)
    aps = {k: nc.dram_tensor("in_" + k, v.shape, mybir.dt.from_np(v.dtype), kind="ExternalInput").ap()
           for k, v in arrays.items()}
    out = nc.dram_tensor("out", (N, D), F32, kind="ExternalOutput").ap()
    build(nc, aps, out)
    return launch(nc, [{"in_" + k: v for k, v in arrays.items()}], core_ids=[0]).results[0]["out"]
```

```python
from contextlib import ExitStack

import numpy as np
import concourse.bass as bass
from concourse import mybir

F32, F32R, F16, BF16 = mybir.dt.float32, mybir.dt.float32r, mybir.dt.float16, mybir.dt.bfloat16
I32 = mybir.dt.int32
ALU, ACT, AX = mybir.AluOpType, mybir.ActivationFunctionType, mybir.AxisListType

N, D, E = 1250, 512, 20000
P = 125
T = N // P
KD = D // 128
HEADS, BLOCKS, BASES = 4, 4, 30
DH = D // HEADS
COND, FREQS = 16, 32
EC = E // P
BUCKETS = 2 * T
GROUP, STEPS = 512, 4
GROUPS = (E + BUCKETS * (GROUP - 1)) // GROUP
SLOTS = GROUPS * STEPS
HALVES = ((0, 626), (626, 624))
COLS = ((0, 418), (418, 416), (834, 416))
WIDE = ((0, 512), (512, 512), (1024, 226))
EPS = 1e-5
BIG = 1.0e30
PREP = (10, 20, 30, 40)


class Job:

    def __init__(self, slot, full, reuse, emptied):
        self.slot, self.full, self.reuse, self.emptied = slot, full, reuse, emptied


class Walk:

    def __init__(self):
        self.n, self.i, self.per = 0, None, 0

    def enter(self, i, per):
        self.i, self.per = i, per

    def leave(self):
        self.n, self.i = self.n + (BLOCKS - 1) * self.per, None

    def take(self):
        n, self.n = self.n, self.n + 1
        if self.i is None:
            return Job(n % 2, n + 1, n // 2 or None, n // 2 + 1)
        a, b = self.i * self.per, self.i * (self.per // 2)
        return Job(n % 2, a + (n + 1), b + n // 2, b + (n // 2 + 1))


def at(i, per, k):
    return k if i is None else i * per + k


def plan_block(w):
    g = {"proj": {}, "mrow": {}, "den": {}, "out": {}}

    def project(h):
        if h < HEADS:
            g["proj"][h] = [w.take() for _ in range(6)]

    def max_row(h):
        if h < HEADS:
            g["mrow"][h] = [w.take() for _ in range(3)]

    project(0)
    g["v"] = [w.take() for _ in range(T)]
    project(1)
    max_row(0)
    for h in range(HEADS):
        project(h + 2)
        max_row(h + 1)
        g["den"][h] = w.take()
        g["out"][h] = [w.take() for _ in range(T)]
    g["up"] = [w.take() for _ in range(3 * KD)]
    g["down"] = [w.take() for _ in range(T)]
    return g


_w = Walk()
plan_block(_w)
LIN_PER_BLOCK = _w.n


def plan_post(w):
    g = {}

    def tiles(*names):
        for name in names:
            g[name] = [w.take() for _ in range(T)]

    def woven(*names):
        for name in names:
            g[name] = []
        for _ in range(T):
            for name in names:
                g[name].append(w.take())

    tiles("norm1", "beta1")
    g["count"] = w.take()
    woven("mean1", "self1")
    tiles("norm2")
    g["gate", 0] = w.take()
    tiles(("msg", 0, 0), ("agg", 0, 0), ("msg", 0, 1), ("agg", 0, 1), "turn2")
    g["gate", 1] = w.take()
    tiles(("msg", 1, 0), ("agg", 1, 0), ("msg", 1, 1), ("agg", 1, 1))
    tiles("norm3")
    g["degree"] = w.take()
    tiles(("sage", 0))
    woven(("mean3", 0), ("self3", 0))
    tiles("turn3", ("sage", 1))
    woven(("mean3", 1), ("self3", 1))
    return g


class Score:

    def __init__(self, n, kind, h, j, before):
        self.n, self.slot, self.kind, self.h, self.j, self.before = n, n % 2, kind, h, j, before


def plan_scores():
    out, last = [], [None, None]

    def add(kind, h, j):
        s = Score(len(out), kind, h, j, last[len(out) % 2])
        last[s.slot] = s
        out.append(s)

    for j in range(2 * T):
        add("max", 0, j)
    for h in range(HEADS):
        for j in range(2 * T):
            add("exp", h, j)
            if h + 1 < HEADS:
                add("max", h + 1, j)
    return out


SCORES = {(s.kind, s.h, s.j): s for s in plan_scores()}
SCORES_PER_BLOCK = len(SCORES)
EXPS = MAXES = HEADS * 2 * T


def build(nc, a, out):
    stack = ExitStack()
    with stack:
        def sem(name):
            return stack.enter_context(nc.semaphore(name))

        def sb_in(ctx):
            return lambda name, shape, dt: ctx.enter_context(nc.sbuf_tensor(name, shape, dt))

        sb = sb_in(stack)
        typed_t = nc.dram_tensor("typed_t", (2 * N, N), F16, kind="Internal").ap()
        crow_d = nc.dram_tensor("crow_d", (N, N), F16, kind="Internal").ap()

        x = sb("x", [P, T, D], F32)
        yT = sb("yT", [128, KD, N], F32)
        big = sb("big", [128, T * D], F32)
        vrow = big[0:P, :].rearrange("p (t d) -> p t d", d=D)
        hidT = big[:, 0:KD * N].rearrange("p (k n) -> p k n", n=N)
        w = [sb(f"w{s}", [128, KD, D], F32) for s in range(3)]
        ct = sb("ct", [P, T, N], F16)
        ident = sb("ident", [128, 128], F32)
        brow = sb("brow", [P, 3, D], F32)
        stats = sb("stats", [P, T, 6], F32)
        mv = sb("mv", [P, T, 2], F32)
        var = sb("var", [P, T], F32)
        rstd = sb("rstd", [P, T], F32)
        nmr = sb("nmr", [P, T], F32)
        mhalf = sb("mhalf", [P, T], F32)
        ones_f = sb("ones_f", [128, 1], F32)
        zcol = sb("zcol", [P, 1], F32)
        tick = sb("tick", [1, MAXES], F32)
        ps = stack.enter_context(nc.psum_tensor("ps", [128, 8 * 512], F32))

        def score_ps(slot, n):
            return ps[0:P, slot * 1024:slot * 1024 + n]

        def lin_ps(job, parts, n, c0=0):
            return ps[0:parts, 3072 + 512 * job.slot + c0:3072 + 512 * job.slot + c0 + n]

        o_ps = ps[:, 2048:3072]

        def scale_ps(t):
            return ps[0:P, (t % 2) * 1024:(t % 2) * 1024 + D]

        def turn_ps(t):
            return ps[:, (t % 2) * 1024 + 512:(t % 2) * 1024 + 512 + KD * P].rearrange("p (k n) -> p k n", k=KD)

        lin_full = sem("lin_full")
        lin_empty = [sem(f"lin_empty{s}") for s in range(2)]
        consts_set = sem("consts_set")
        edges_in = sem("edges_in")
        rows_init = sem("rows_init")
        payload_ready = sem("payload_ready")
        ecount_ready = sem("ecount_ready")
        tri_done = sem("tri_done")
        slot_hot_ready = sem("slot_hot_ready")
        row_hot_ready = sem("row_hot_ready")
        edge_placed = sem("edge_placed")
        carry_ready = sem("carry_ready")
        onehot_ready = sem("onehot_ready")
        onehot_used = sem("onehot_used")
        group_full = sem("group_full")
        run_ready = sem("run_ready")
        rows_out = [sem(f"rows_out{s}") for s in range(2)]
        typed_in = [sem(f"typed_in{t}") for t in range(T // 2)]
        ct_ready = sem("ct_ready")
        crow_ps_full = sem("crow_ps_full")
        crow_copied = sem("crow_copied")
        mneg_ready = sem("mneg_ready")
        crow_out = [sem(f"crow_out{s}") for s in range(2)]
        pre_in = sem("pre_in")
        phase_ready = sem("phase_ready")
        emb_ready = sem("emb_ready")
        silu_ready = sem("silu_ready")
        zexp_ready = sem("zexp_ready")
        var_ready = sem("var_ready")
        rstd_ready = sem("rstd_ready")
        norm_ready = sem("norm_ready")
        xn_ready = sem("xn_ready")
        x0_ready = sem("x0_ready")
        scale_full = sem("scale_full")
        scaled_ready = sem("scaled_ready")
        turn_full = sem("turn_full")
        turned_ready = sem("turned_ready")
        blk_done = sem("blk_done")
        blkc_in = sem("blkc_in")
        w_in = [sem(f"w_in{s}") for s in range(3)]
        hi_ready = sem("hi_ready")
        score_full = sem("score_full")
        exp_done = sem("exp_done")
        max_done = sem("max_done")
        neg_max_ready = sem("neg_max_ready")
        prob_ready = sem("prob_ready")
        pv_done = sem("pv_done")
        psum_done = sem("psum_done")
        o_copied = sem("o_copied")
        xbias_done = sem("xbias_done")
        out_done = sem("out_done")
        sums_read = sem("sums_read")

        keep = ExitStack()
        sk = sb_in(keep)
        mneg = sk("mneg", [P, T, N], BF16)
        condT = sk("condT", [COND + 1, N], F32)
        fw1 = sk("fw1", [2 * FREQS, COND], F32)
        fw2 = sk("fw2", [COND, COND], F32)
        fb1 = sk("fb1", [COND, 1], F32)
        fb2 = sk("fb2", [COND, 1], F32)
        freq = sk("freq", [2 * FREQS, 1], F32)
        quarter = sk("quarter", [2 * FREQS, 1], F32)
        noise = yT[0:2 * FREQS, 0, :]
        turns = yT[0:2 * FREQS, 1, :]
        whole = yT[0:2 * FREQS, 2, :]
        emb = yT[0:2 * FREQS, 3, :]
        z = hidT[0:COND, 0, :]
        zexp = hidT[0:COND, 1, :]
        silu = hidT[0:COND, 2, :]

        adj = ExitStack()
        sa = sb_in(adj)
        onehot_src = sa("onehot_src", [128, 4, N], F16)
        onehot_dst = sa("onehot_dst", [128, 4, P], F16)
        col_iota = sa("col_iota", [128, N], F16)
        run = sa("run", [P, 2, N], F16)
        row_hot = sa("row_hot", [P, 4, 128], F16)
        slot_hot = sa("slot_hot", [P, 4, 2, SLOTS], F16)
        carry = sa("carry", [P, 2, P], F16)
        typed1 = mneg[:].bitcast(F16)
        crow = sa("crow", [P, 2, N], F16)
        zero_row = sa("zero_row", [P, N], F16)
        ident16 = sa("ident16", [P, P], F16)
        esrc = sa("esrc", [P, EC], I32)
        edst = sa("edst", [P, EC], I32)
        etyp = sa("etyp", [P, EC], I32)
        key = sa("key", [P, EC], F32)
        thr = sa("thr", [P, BUCKETS + 1], F32)
        ge = yT[0:P, :, :].rearrange("p k n -> p (k n)")[:, 0:(BUCKETS + 1) * EC].rearrange("p (b c) -> p b c", c=EC)
        oh = mneg[:].rearrange("p t n -> p (t n)").bitcast(F32)[:, 0:BUCKETS * EC].rearrange("p (b c) -> p b c", c=EC)
        incl = big[0:P, 0:BUCKETS * EC].rearrange("p (b c) -> p b c", c=EC)
        zero = sa("zero", [128, 1], F32)
        bsum = sa("bsum", [P, EC], F32)
        src1 = sa("src1", [P, EC], F32)
        dst1 = sa("dst1", [P, EC], F32)
        cnt = sa("cnt", [P, BUCKETS], F32)
        tri = sa("tri", [P, P], F32)
        ones_sq = sa("ones_sq", [P, 128], F32)
        toti = sa("toti", [128, BUCKETS], I32)
        ngr = sa("ngr", [128, BUCKETS], F32)
        egr = sa("egr", [128, BUCKETS], F32)
        base = sa("base", [P, BUCKETS], F32)
        base2 = sa("base2", [P, BUCKETS], F32)
        pos = sa("pos", [P, EC], F32)
        posi = sa("posi", [P, EC], I32)
        ia = sa("ia", [P, EC], I32)
        ib = sa("ib", [P, EC], I32)
        ic = sa("ic", [P, EC], I32)
        slot_row = sa("slot_row", [P, EC], F32)
        slot_col = sa("slot_col", [P, EC], F32)
        gi = sa("gi", [128, GROUPS + 1], F32)
        gcmp = sa("gcmp", [128, GROUPS + 1, BUCKETS], F32)
        bk = sa("bk", [128, GROUPS + 1], F32)
        same = sa("same", [128, GROUPS], F32)
        rowf = sa("rowf", [128, GROUPS], F32)
        rowi = sa("rowi", [128, GROUPS], I32)
        part = sa("part", [128, 1], F32)
        es = sa("es", [128, 2, SLOTS], F32)
        adj.close()

        att = ExitStack()
        sl = sb_in(att)
        qk_hi = sl("qk_hi", [128, 2, 2, N], F32R)
        qk_lo = sl("qk_lo", [128, 2, 2, N], F32R)
        prob = sl("prob", [P, 3, HALVES[0][1]], F32)
        pacc = sl("pacc", [P, N], F32)
        oT = sl("oT", [128, N], F32)
        xn = pacc[:, 0:2 * D].rearrange("p (s d) -> p s d", d=D)
        y = prob[:].rearrange("p s n -> p (s n)")[:, 0:2 * D].rearrange("p (s d) -> p s d", d=D)
        cw = sl("cw", [COND + 1, 4, D], F32)
        mrow = sl("mrow", [1, N], F32R)
        bcol = sl("bcol", [128, 3, KD], F32)
        mxp = sl("mxp", [P, T, 2], F32)
        nmx = sl("nmx", [P, T], F32)
        rden = sl("rden", [P, T], F32)
        ones_r = sl("ones_r", [1, 128], F32R)
        att.close()
        keep.close()

        post = ExitStack()
        so = sb_in(post)
        pieces = so("pieces", [P, 3, T, D], BF16)
        ct2 = so("ct2", [P, T, N], F16)
        agg = so("agg", [P, T, D], F32)
        ring = [so(f"basis{s}", [128, KD // 2, D], F32) for s in range(3)]
        py = so("py", [P, 2, D], F32)
        rest = so("rest", [P, 2, D], F32)
        prow = so("prow", [P, 2, D], F32)
        att_w = so("att_w", [128, 2, 2, BASES], F32)
        gate_w = so("gate_w", [128, 2, KD, 2], F32)
        gate = so("gate", [P, T, 2], F32)
        per_node = so("per_node", [P, T], F32)
        ones_h = so("ones_h", [P, 1], F16)
        post.close()
        mixed = [[big[:, r * KD * D:(r + 1) * KD * D].rearrange("p (k n) -> p k n", n=D) for r in range(2)],
                 [w[0], w[1]]]
        post_in = sem("post_in")
        pw_in = sem("pw_in")
        ct2_in = sem("ct2_in")
        ctr_in = sem("ctr_in")
        basis_in = [sem(f"basis_in{s}") for s in range(3)]
        basis_used = sem("basis_used")
        xout_ready = sem("xout_ready")
        row_ready = sem("row_ready")
        first_piece = sem("first_piece")
        pieces_ready = sem("pieces_ready")
        gate_exp = sem("gate_exp")
        gate_ready = sem("gate_ready")
        mixed_ready = sem("mixed_ready")
        agg_ready = sem("agg_ready")
        pbias_done = sem("pbias_done")
        tile_ready = sem("tile_ready")

        block = stack.enter_context(nc.Block())

        @block.sync
        def _(sp):
            for dst_, name in ((esrc, "src"), (edst, "dst"), (etyp, "edge_type_2")):
                sp.dma_start(dst_[:], a[name].rearrange("(p c) -> p c", c=EC)).then_inc(edges_in, 16)
            sp.dma_start(x[:], a["x"].rearrange("(t p) d -> p t d", p=P)).then_inc(pre_in, 16)
            for dst_, name in ((fw1, "L0_gnn_f_w1"), (fw2, "L0_gnn_f_w2"), (fb1, "f_b1"), (fb2, "f_b2")):
                sp.dma_start(dst_[:], a[name]).then_inc(pre_in, 16)
            for s, name in ((0, "wv"), (1, "wq"), (2, "wk")):
                sp.dma_start(w[s][:], a[name][0].rearrange("(k p) n -> p k n", p=128)).then_inc(w_in[s], 16)
            sp.wait_ge(consts_set, 1)
            for b in range(BUCKETS):
                sp.dma_start(typed_t[b * P:(b + 1) * P, :], zero_row[:]).then_inc(rows_init, 16)
            sp.wait_ge(payload_ready, 1)
            sp.dma_start(noise, a["node_vec1"].partition_broadcast(2 * FREQS)).then_inc(phase_ready, 16)
            for s in range(2):
                sp.wait_ge(rows_out[s], 16 * ((GROUPS + 1 - s) // 2))
            for t in range(0, T, 2):
                for r, to in ((0, ct), (1, typed1)):
                    sp.dma_start(to[:, t:t + 2, :], typed_t[r * N + t * P:r * N + (t + 2) * P, :]
                                 .rearrange("(t p) n -> p t n", p=P)).then_inc(typed_in[t // 2], 16)
            walk = Walk()
            walk.n = 8
            with sp.Fori(0, BLOCKS) as i:
                walk.enter(i, LIN_PER_BLOCK)
                g = plan_block(walk)
                sp.wait_ge(blk_done, at(i, 1, 1))
                sp.dma_start(brow[:], a["brow"][i].partition_broadcast(P)).then_inc(blkc_in, 16)
                sp.dma_start(cw[:], a["cw"][i]).then_inc(blkc_in, 16)
                sp.dma_start(bcol[:].rearrange("p k c -> p (k c)"), a["bcol"][i]).then_inc(blkc_in, 16)

                def load(s, name, j):
                    sp.dma_start(w[s][:], a[name][j].rearrange("(k p) n -> p k n", p=128)).then_inc(w_in[s], 16)

                sp.wait_ge(lin_full, g["v"][-1].full)
                load(0, "wo", i)
                sp.wait_ge(lin_full, g["proj"][HEADS - 1][-1].full)
                load(1, "m_w1", i)
                load(2, "m_w2", i)
                sp.wait_ge(lin_full, g["out"][HEADS - 1][-1].full)
                load(0, "wv", i + 1)
                sp.wait_ge(lin_full, g["up"][-1].full)
                load(1, "wq", i + 1)
                sp.wait_ge(lin_full, g["down"][-1].full)
                load(2, "wk", i + 1)
            walk.leave()
            sp.wait_ge(blk_done, BLOCKS + 1)
            sp.dma_start(big[0:P, :].rearrange("p (t d) -> p t d", d=D),
                         a["x"].rearrange("(t p) d -> p t d", p=P)).then_inc(post_in, 16)
            sp.dma_start(att_w[:].rearrange("p a r b -> p (a r b)"), a["att"].partition_broadcast(128)).then_inc(post_in, 16)
            sp.dma_start(gate_w[:].rearrange("p a k r -> p (a k r)"), a["gate_w"]).then_inc(post_in, 16)
            sp.dma_start(brow[:], a["post_rows"][0:3, :].partition_broadcast(P)).then_inc(post_in, 16)
            sp.dma_start(prow[:], a["post_rows"][3:5, :].partition_broadcast(P)).then_inc(post_in, 16)
            for n in range(2 * BASES * 2):
                layer, b, half = n // (2 * BASES), n // 2 % BASES, n % 2
                if n >= 3:
                    sp.wait_ge(basis_used, n - 2)
                sp.dma_start(ring[n % 3][:], a[f"basis{layer + 1}"][b, half * 256:(half + 1) * 256, :]
                             .rearrange("(k p) n -> p k n", p=128)).then_inc(basis_in[n % 3], 16)
            for t in range(T):
                sp.wait_ge(tile_ready, t + 1)
                sp.dma_start(out[t * P:(t + 1) * P, :], x[:, t, :]).then_inc(out_done, 16)
            sp.wait_ge(out_done, 16 * T)

        @block.gpsimd
        def _(pool):
            def drained_inc(s):
                nc.gpsimd.drain().then_inc(s, 1)

            nc.gpsimd.memset(zero_row[:], 0.0)
            drained_inc(consts_set)
            nc.gpsimd.iota(thr[:], pattern=[[P, BUCKETS + 1]], base=0, channel_multiplier=0,
                           allow_small_or_imprecise_dtypes=True)
            nc.gpsimd.memset(zero[:], 0.0)
            nc.gpsimd.memset(tri[:], 1.0)
            nc.gpsimd.memset(ones_sq[:], 1.0)
            nc.gpsimd.memset(ident[:], 0.0)
            nc.gpsimd.memset(ident16[:], 0.0)
            nc.gpsimd.memset(mhalf[:], -0.5)
            nc.gpsimd.memset(ones_f[:], 1.0)
            nc.gpsimd.memset(zcol[:], 0.0)
            nc.gpsimd.memset(tick[:], 0.0)
            nc.gpsimd.iota(gi[:], pattern=[[1, GROUPS + 1]], base=0, channel_multiplier=0,
                           allow_small_or_imprecise_dtypes=True)
            nc.gpsimd.iota(part[:], pattern=[[0, 1]], base=0, channel_multiplier=1,
                           allow_small_or_imprecise_dtypes=True)
            nc.gpsimd.iota(col_iota[:], pattern=[[1, N]], base=1, channel_multiplier=0,
                           allow_small_or_imprecise_dtypes=True)
            for half in range(2):
                rows = slice(half * FREQS, (half + 1) * FREQS)
                nc.gpsimd.drain()
                nc.gpsimd.iota(freq[rows, :], pattern=[[0, 1]], base=1, channel_multiplier=1,
                               allow_small_or_imprecise_dtypes=True)
                nc.gpsimd.memset(quarter[rows, :], 0.25 * half)
            nc.gpsimd.memset(condT[:], 1.0)
            nc.gpsimd.drain()
            nc.gpsimd.affine_select(out=tri[:], in_=tri[:], compare_op=ALU.is_gt, fill=0.0, base=0,
                                    pattern=[[1, P]], channel_multiplier=-1)
            nc.gpsimd.affine_select(out=ident[:], in_=ident[:], compare_op=ALU.not_equal, fill=1.0, base=0,
                                    pattern=[[-1, 128]], channel_multiplier=1)
            nc.gpsimd.affine_select(out=ident16[:], in_=ident16[:], compare_op=ALU.not_equal, fill=1.0, base=0,
                                    pattern=[[-1, P]], channel_multiplier=1)
            drained_inc(consts_set)
            pool.wait_ge(payload_ready, 1)
            for c in range(EC):
                if c >= 4:
                    pool.wait_ge(edge_placed, c - 3)
                nc.gpsimd.tensor_scalar(row_hot[:, c % 4, :], col_iota[0:P, 0:128], slot_row[:, c:c + 1], None,
                                        ALU.is_equal).then_inc(row_hot_ready, 1)
            pool.wait_ge(rows_init, 16 * BUCKETS)
            for g in range(GROUPS):
                pool.wait_ge(run_ready, g + 1)
                nc.gpsimd.indirect_dma_start(
                    out=typed_t, out_offset=bass.IndirectOffsetOnAxis(ap=rowi[0:P, g:g + 1], axis=0),
                    in_=run[:, g % 2, :], in_offset=None,
                    bounds_check=2 * N - 1, oob_is_err=False).then_inc(rows_out[g % 2], 16)
                if g == PREP[0] - 2:
                    pool.wait_ge(var_ready, 1)
                    nc.gpsimd.tensor_tensor(rstd[:], var[:], mhalf[:], ALU.pow).then_inc(rstd_ready, 1)
            with pool.Fori(0, BLOCKS) as i:
                for half in range(2):
                    pool.wait_ge(var_ready, at(i, 2, 2 + half))
                    nc.gpsimd.tensor_tensor(rstd[:], var[:], mhalf[:], ALU.pow).then_inc(rstd_ready, 1)
                    pool.wait_ge(xn_ready, at(i, 2 * T, T * (half + 1)))
                    pool.wait_ge(blkc_in, at(i, 48, 48))
                    nc.gpsimd.tensor_tensor(x[:], x[:], brow[:, 1 + half:2 + half, :].to_broadcast([P, T, D]),
                                            ALU.add).then_inc(xbias_done, 1)
                    if half:
                        continue
                    for h in range(HEADS):
                        for j in range(2 * T):
                            n = h * 2 * T + j
                            c0, nn = HALVES[j // T]
                            pool.wait_ge(prob_ready, at(i, EXPS, n + 1))
                            if j == 0 and h:
                                pool.wait_ge(sums_read, at(i, HEADS, h))
                            if j % T == 0:
                                nc.gpsimd.tensor_tensor(pacc[:, c0:c0 + nn], prob[:, n % 3, 0:nn],
                                                        zcol[:].to_broadcast([P, nn]), ALU.add).then_inc(psum_done, 1)
                            else:
                                pool.wait_ge(psum_done, at(i, EXPS, n))
                                nc.gpsimd.tensor_tensor(pacc[:, c0:c0 + nn], pacc[:, c0:c0 + nn], prob[:, n % 3, 0:nn],
                                                        ALU.add).then_inc(psum_done, 1)

            walk = Walk()
            walk.n = 8 + BLOCKS * LIN_PER_BLOCK
            g = plan_post(walk)
            pool.wait_ge(blk_done, BLOCKS + 1)
            nc.gpsimd.memset(ones_h[:], 1.0)
            nc.gpsimd.drain().then_inc(consts_set, 1)
            nc.gpsimd.dma_start(ct2[:], typed_t[N:2 * N, :].rearrange("(t p) n -> p t n", p=P)).then_inc(ct2_in, 16)
            pool.wait_ge(post_in, 80)

            def norm_power(count):
                pool.wait_ge(var_ready, count)
                nc.gpsimd.tensor_tensor(rstd[:], var[:], mhalf[:], ALU.pow).then_inc(rstd_ready, 1)

            def add_bias(rows, row, read):
                pool.wait_ge(row_ready, read)
                nc.gpsimd.tensor_tensor(x[:], x[:], rows[:, row:row + 1, :].to_broadcast([P, T, D]),
                                        ALU.add).then_inc(pbias_done, 1)

            def late_load(dst_, src_, job, signal):
                pool.wait_ge(lin_full, job.full)
                nc.gpsimd.dma_start(dst_, src_).then_inc(signal, 16)

            def matrix(name):
                return a[name].rearrange("(k p) n -> p k n", p=128)

            def count_rows(d):
                return d.rearrange("(t p) n -> p t n", p=P)

            norm_power(10)
            add_bias(brow, 0, T)
            late_load(ct[:], count_rows(typed_t[0:N, :]), g["mean1"][-1], ctr_in)
            norm_power(11)
            add_bias(brow, 2, 2 * T)
            late_load(w[2][:], matrix("root2"), g["agg", 0, 0][-1], pw_in)
            late_load(w[0][:], matrix("W1_l"), g["msg", 1, 0][-1], pw_in)
            late_load(ct[:], count_rows(crow_d), g["agg", 1, 0][-1], ctr_in)
            late_load(w[2][:], matrix("W2_l"), g["agg", 1, 0][-1], pw_in)
            late_load(w[1][:], matrix("W1_r"), g["msg", 1, 1][-1], pw_in)
            norm_power(12)
            add_bias(prow, 1, 4 * T)
            late_load(w[0][:], matrix("W2_r"), g["sage", 0][-1], pw_in)

        @block.vector
        def _(dve):
            V = nc.vector

            def statistics(count, summed=False):
                V.drain()
                if not summed:
                    for t in range(T):
                        V.bn_stats(stats[:, t, :], x[:, t, :])
                    V.drain()
                for t in range(T):
                    V.bn_aggr(mv[:, t, :], stats[:, t, :])
                V.drain()
                V.tensor_scalar(var[:], mv[:, :, 1], EPS, None, ALU.add).then_inc(var_ready, 1)
                dve.wait_ge(rstd_ready, count)
                V.scalar_tensor_tensor(out=nmr[:], in0=mv[:, :, 0], scalar=-1.0, in1=rstd[:],
                                       op0=ALU.mult, op1=ALU.mult).then_inc(norm_ready, 1)

            walk = Walk()
            jb, jt = walk.take(), walk.take()
            dve.wait_ge(edges_in, 48)
            dve.wait_ge(consts_set, 2)
            V.tensor_scalar(key[:], etyp[:], 0.0, float(N), ALU.not_equal, ALU.mult)
            V.drain()
            V.tensor_tensor(key[:], key[:], edst[:], ALU.add)
            V.drain()
            V.tensor_tensor(ge, key[:].unsqueeze(1).to_broadcast([P, BUCKETS + 1, EC]),
                            thr[:].unsqueeze(2).to_broadcast([P, BUCKETS + 1, EC]), ALU.is_ge)
            V.drain()
            V.tensor_tensor(oh, ge[:, 0:BUCKETS, :], ge[:, 1:BUCKETS + 1, :], ALU.subtract)
            V.tensor_reduce(bsum[:], ge[:, 1:BUCKETS, :].rearrange("p b c -> p c b"), AX.X, ALU.add)
            V.drain()
            V.tensor_reduce(cnt[:], oh, AX.X, ALU.add)
            V.tensor_tensor_scan(incl.rearrange("p b c -> p (b c)"), oh.rearrange("p b c -> p (b c)"),
                                 zero[0:P, :].to_broadcast([P, BUCKETS * EC]), 0.0, ALU.add, ALU.add)
            V.tensor_scalar(src1[:], esrc[:], 1.0, None, ALU.add)
            V.scalar_tensor_tensor(out=dst1[:], in0=bsum[:], scalar=-float(P), in1=key[:],
                                   op0=ALU.mult, op1=ALU.add)
            V.drain().then_inc(ecount_ready, 1)
            V.tensor_scalar(dst1[:], dst1[:], 1.0, None, ALU.add)
            dve.wait_ge(lin_full, jt.full)
            V.tensor_scalar(toti[:], lin_ps(jt, 128, BUCKETS), float(GROUP - 1), None,
                            ALU.add).then_inc(lin_empty[jt.slot], 1)
            V.tensor_copy(base[:], lin_ps(jb, P, BUCKETS)).then_inc(lin_empty[jb.slot], 1)
            V.drain()
            V.tensor_scalar(toti[:], toti[:], 9, None, ALU.logical_shift_right)
            V.drain()
            V.tensor_copy(ngr[:], toti[:])
            V.drain()
            V.tensor_tensor_scan(egr[:], ngr[:], zero[:].to_broadcast([128, BUCKETS]), 0.0, ALU.add, ALU.add)
            V.drain()
            V.tensor_tensor(base2[:], egr[0:P, :], ngr[0:P, :], ALU.subtract)
            V.drain()
            V.scalar_tensor_tensor(out=base[:], in0=base2[:], scalar=float(GROUP), in1=base[:],
                                   op0=ALU.mult, op1=ALU.add)
            V.drain()
            V.tensor_tensor(base[:, 1:], base[:, 1:], incl[:, 0:BUCKETS - 1, EC - 1], ALU.subtract)
            V.drain()
            V.tensor_tensor(incl, incl, base[:].unsqueeze(2).to_broadcast([P, BUCKETS, EC]), ALU.add)
            V.drain()
            V.tensor_tensor(incl, incl, oh, ALU.mult)
            V.drain()
            V.tensor_reduce(pos[:], incl.rearrange("p b c -> p c b"), AX.X, ALU.add)
            V.drain()
            V.tensor_scalar(posi[:], pos[:], -1.0, None, ALU.add)
            V.drain()
            V.tensor_scalar(ia[:], posi[:], 9, 2, ALU.logical_shift_right, ALU.logical_shift_left)
            V.tensor_scalar(ib[:], posi[:], 2, 127, ALU.logical_shift_right, ALU.bitwise_and)
            V.tensor_scalar(ic[:], posi[:], 3, None, ALU.bitwise_and)
            V.drain()
            V.tensor_scalar(slot_row[:], ib[:], 1.0, None, ALU.add)
            V.tensor_tensor(slot_col[:], ia[:], ic[:], ALU.add)
            V.drain()
            V.tensor_scalar(slot_col[:], slot_col[:], 1.0, None, ALU.add)
            V.drain().then_inc(payload_ready, 1)
            for c in range(EC):
                if c >= 4:
                    dve.wait_ge(edge_placed, c - 3)
                V.tensor_scalar(slot_hot[:, c % 4, 0, :], col_iota[0:P, 0:SLOTS], slot_col[:, c:c + 1], src1[:, c:c + 1],
                                ALU.is_equal, ALU.mult)
                V.tensor_scalar(slot_hot[:, c % 4, 1, :], col_iota[0:P, 0:SLOTS], slot_col[:, c:c + 1], dst1[:, c:c + 1],
                                ALU.is_equal, ALU.mult).then_inc(slot_hot_ready, 1)
            V.tensor_tensor(gcmp[:], egr[:].unsqueeze(1).to_broadcast([128, GROUPS + 1, BUCKETS]),
                            gi[:].unsqueeze(2).to_broadcast([128, GROUPS + 1, BUCKETS]), ALU.is_le)
            V.drain()
            V.tensor_reduce(bk[:], gcmp[:], AX.X, ALU.add)
            V.drain()
            V.tensor_tensor(same[:], bk[:, 0:GROUPS], bk[:, 1:GROUPS + 1], ALU.is_equal)
            V.tensor_scalar(rowf[:], bk[:, 0:GROUPS], float(P), part[:], ALU.mult, ALU.add)
            V.drain()
            V.scalar_tensor_tensor(out=rowf[:], in0=same[:], scalar=1.0e6, in1=rowf[:], op0=ALU.mult, op1=ALU.add)
            V.drain()
            V.tensor_copy(rowi[:], rowf[:])

            def first_norm():
                dve.wait_ge(pre_in, 80)
                statistics(1)
                dve.wait_ge(phase_ready, 16)
                V.tensor_scalar(turns, noise, freq[:], 1.0 / 16.0, ALU.mult, ALU.mult)
                V.drain()
                V.tensor_scalar(turns, turns, quarter[:], None, ALU.add)
                V.drain()
                V.tensor_scalar(whole, turns, 12582912.0, -12582912.0, ALU.add, ALU.add)
                V.drain()
                V.tensor_tensor(turns, turns, whole, ALU.subtract)
                V.drain().then_inc(emb_ready, 1)

            def finish_silu():
                dve.wait_ge(zexp_ready, 1)
                V.tensor_scalar(zexp, zexp, 1.0, None, ALU.add)
                V.drain()
                V.reciprocal(zexp, zexp)
                V.drain()
                V.tensor_tensor(silu, z, zexp, ALU.mult)
                V.drain().then_inc(silu_ready, 1)

            for _ in range(6):
                walk.take()

            dve.wait_ge(edge_placed, EC)
            V.tensor_copy(es[:].rearrange("p a s -> p (a s)"), o_ps[:, 0:2 * SLOTS])
            V.drain()
            for g in range(GROUPS):
                for j in range(STEPS):
                    n = g * STEPS + j
                    if n >= 4:
                        dve.wait_ge(onehot_used, n - 3)
                    V.tensor_scalar(onehot_dst[:, n % 4, :], col_iota[:, 0:P], es[:, 1, n:n + 1], None, ALU.is_equal)
                    V.tensor_scalar(onehot_src[:, n % 4, :], col_iota[:], es[:, 0, n:n + 1], None, ALU.is_equal).then_inc(onehot_ready, 1)
                if g:
                    if g >= 3:
                        dve.wait_ge(group_full, g - 1)
                    V.tensor_scalar(carry[:, g % 2, :], ident16[:], same[0:P, g - 1:g], None, ALU.mult).then_inc(carry_ready, 1)
                if g == PREP[0]:
                    first_norm()
                if g == PREP[2]:
                    finish_silu()
            for t in range(T):
                dve.wait_ge(typed_in[t // 2], 32)
                V.tensor_tensor(ct[:, t, :], ct[:, t, :], typed1[:, t, :], ALU.add).then_inc(ct_ready, 1)
            for s in range(T):
                dve.wait_ge(crow_copied, s + 1)
                V.tensor_scalar(mneg[:, s, :], crow[:, s % 2, :], 0.0, -BIG, ALU.is_equal, ALU.mult).then_inc(mneg_ready, 1)
            dve.wait_ge(x0_ready, T)
            for s in range(2):
                dve.wait_ge(crow_out[s], 16 * (T // 2))
            V.memset(ones_r[:].bitcast(F32), 1.0)
            for t in range(T):
                V.bn_stats(stats[:, t, :], x[:, t, :])
            V.drain().then_inc(blk_done, 1)

            with dve.Fori(0, BLOCKS) as i:
                walk.enter(i, LIN_PER_BLOCK)
                g = plan_block(walk)

                def scale_rows(ln):
                    for t in range(T):
                        n = ln * T + t
                        dve.wait_ge(scale_full, at(i, 2 * T, n + 1))
                        dve.wait_ge(xn_ready, at(i, 2 * T, n + 1))
                        if t >= 2:
                            dve.wait_ge(turn_full, at(i, 2 * T, n - 1))
                        V.scalar_tensor_tensor(out=y[:, t % 2, :], in0=scale_ps(t), scalar=1.0, in1=xn[:, t % 2, :],
                                               op0=ALU.add, op1=ALU.mult).then_inc(scaled_ready, 1)

                statistics(at(i, 2, 2), True)
                scale_rows(0)

                def low_parts(h):
                    for n, job in enumerate(g["proj"][h]):
                        which, (c0, nn) = n // 3, COLS[n % 3]
                        dve.wait_ge(hi_ready, at(i, 6 * HEADS, 6 * h + n + 1))
                        V.scalar_tensor_tensor(out=qk_lo[:, h % 2, which, c0:c0 + nn], in0=lin_ps(job, 128, nn),
                                               scalar=bcol[:, which, h:h + 1],
                                               in1=qk_hi[:, h % 2, which, c0:c0 + nn].bitcast(F32),
                                               op0=ALU.add, op1=ALU.subtract).then_inc(lin_empty[job.slot], 1)

                def masked_max(h, j):
                    s = SCORES["max", h, j]
                    t, (c0, nn) = j // 2, HALVES[j % 2]
                    dve.wait_ge(score_full, at(i, SCORES_PER_BLOCK, s.n + 1))
                    V.tensor_tensor(tick[:, MAXES // HEADS * h + j:MAXES // HEADS * h + j + 1], zcol[0:1, :], zcol[0:1, :], ALU.add)
                    V.tensor_tensor_reduce(out=score_ps(s.slot, nn), in0=score_ps(s.slot, nn), in1=mneg[:, t, c0:c0 + nn],
                                           scale=1.0, scalar=-BIG, op0=ALU.add, op1=ALU.max,
                                           accum_out=mxp[:, t, j % 2:j % 2 + 1]).then_inc(max_done, 1)

                def negate_max(h):
                    V.drain()
                    V.tensor_tensor(nmx[:], mxp[:, :, 0], mxp[:, :, 1], ALU.max)
                    V.drain()
                    V.tensor_scalar(nmx[:], nmx[:], -1.0, None, ALU.mult)
                    V.drain().then_inc(neg_max_ready, 1)

                low_parts(0)
                dve.wait_ge(blkc_in, at(i, 48, 48))
                for t, job in enumerate(g["v"]):
                    dve.wait_ge(lin_full, job.full)
                    V.tensor_tensor(vrow[:, t, :], lin_ps(job, P, D), brow[:, 0, :], ALU.add).then_inc(lin_empty[job.slot], 1)
                    masked_max(0, 2 * t)
                    masked_max(0, 2 * t + 1)
                low_parts(1)
                negate_max(0)
                for h in range(HEADS):
                    for j in range(2 * T):
                        n = h * 2 * T + j
                        t, (c0, nn) = j % T, HALVES[j // T]
                        if h + 1 < HEADS:
                            masked_max(h + 1, j)
                        dve.wait_ge(exp_done, at(i, EXPS, n + 1))
                        V.scalar_tensor_tensor(out=prob[:, n % 3, 0:nn], in0=prob[:, n % 3, 0:nn], scalar=BIG,
                                               in1=ct[:, t, c0:c0 + nn], op0=ALU.min, op1=ALU.mult).then_inc(prob_ready, 1)
                    if h + 1 < HEADS:
                        negate_max(h + 1)
                    if h + 2 < HEADS:
                        low_parts(h + 2)
                    job = g["den"][h]
                    dve.wait_ge(lin_full, job.full)
                    V.tensor_scalar(rden[:], lin_ps(job, P, T), 1.0e-30, None, ALU.max).then_inc(lin_empty[job.slot], 1)
                    V.drain()
                    V.reciprocal(rden[:], rden[:])
                    V.drain().then_inc(sums_read, 1)
                    if h == 0:
                        dve.wait_ge(xbias_done, at(i, 2, 1))
                    for t, job in enumerate(g["out"][h]):
                        dve.wait_ge(lin_full, job.full)
                        V.scalar_tensor_tensor(out=x[:, t, :], in0=lin_ps(job, P, D), scalar=rden[:, t:t + 1],
                                               in1=x[:, t, :], op0=ALU.mult, op1=ALU.add).then_inc(lin_empty[job.slot], 1)
                        if h == HEADS - 1:
                            V.drain()
                            V.bn_stats(stats[:, t, :], x[:, t, :])
                statistics(at(i, 2, 3), True)
                scale_rows(1)
                dve.wait_ge(xbias_done, at(i, 2, 2))
                for t, job in enumerate(g["down"]):
                    dve.wait_ge(lin_full, job.full)
                    V.tensor_tensor(x[:, t, :], x[:, t, :], lin_ps(job, P, D), ALU.add).then_inc(lin_empty[job.slot], 1)
                    V.drain()
                    V.bn_stats(stats[:, t, :], x[:, t, :])
                V.drain().then_inc(blk_done, 1)
            walk.leave()

            g = plan_post(walk)
            units = [0]

            def mix(n):
                for _ in range(n):
                    u = units[0]
                    units[0] += 1
                    layer, b, half = u // (2 * BASES), u // 2 % BASES, u % 2
                    dve.wait_ge(basis_in[u % 3], 16 * (u // 3 + 1))
                    for r in range(2):
                        acc = mixed[layer][r][:, 2 * half:2 * half + 2, :]
                        scale = att_w[:, layer, r, b:b + 1]
                        if b == 0:
                            V.tensor_scalar(acc, ring[u % 3][:], scale, None, ALU.mult)
                        else:
                            V.scalar_tensor_tensor(out=acc, in0=ring[u % 3][:], scalar=scale, in1=acc,
                                                   op0=ALU.mult, op1=ALU.add)
                    V.drain().then_inc(basis_used, 1)
                    if u % (2 * BASES) == 2 * BASES - 1:
                        V.drain().then_inc(mixed_ready, 1)

            split = [0]

            def split_rows(jobs, scale, extra):
                for t, job in enumerate(jobs):
                    split[0] += 1
                    dve.wait_ge(first_piece, split[0])
                    if scale is None:
                        V.tensor_tensor(rest[:, t % 2, :], lin_ps(job, P, D), pieces[:, 0, t, :],
                                        ALU.subtract).then_inc(lin_empty[job.slot], 1)
                    else:
                        V.scalar_tensor_tensor(out=rest[:, t % 2, :], in0=lin_ps(job, P, D), scalar=scale(t),
                                               in1=pieces[:, 0, t, :], op0=ALU.mult,
                                               op1=ALU.subtract).then_inc(lin_empty[job.slot], 1)
                    V.drain()
                    V.tensor_copy(pieces[:, 1, t, :], rest[:, t % 2, :])
                    V.drain()
                    V.tensor_tensor(pieces[:, 2, t, :], rest[:, t % 2, :], pieces[:, 1, t, :], ALU.subtract)
                    V.drain().then_inc(pieces_ready, 1)
                    mix(extra)

            def add_to(rows, t, job, scale=None):
                dve.wait_ge(lin_full, job.full)
                if scale is None:
                    return V.tensor_tensor(rows[:, t, :], rows[:, t, :], lin_ps(job, P, D), ALU.add)
                return V.scalar_tensor_tensor(out=rows[:, t, :], in0=lin_ps(job, P, D), scalar=scale, in1=rows[:, t, :],
                                              op0=ALU.mult, op1=ALU.add)

            dve.wait_ge(post_in, 80)
            V.tensor_tensor(x[:], x[:], big[0:P, :].rearrange("p (t d) -> p t d", d=D), ALU.add)
            statistics(10)
            mix(6)
            split_rows(g["beta1"], None, 1)
            job = g["count"]
            dve.wait_ge(lin_full, job.full)
            V.reciprocal(per_node[:], lin_ps(job, P, T)).then_inc(lin_empty[job.slot], 1)
            V.drain()
            dve.wait_ge(pbias_done, 1)
            for t in range(T):
                job = g["mean1"][t]
                add_to(x, t, job, per_node[:, t:t + 1]).then_inc(lin_empty[job.slot], 1)
                V.drain()
                job = g["self1"][t]
                add_to(x, t, job).then_inc(lin_empty[job.slot], 1)
                mix(3)

            statistics(11)
            mix(14)

            def gates(layer):
                dve.wait_ge(gate_exp, layer + 1)
                V.tensor_scalar(gate[:], gate[:], 1.0, None, ALU.add)
                V.drain()
                V.reciprocal(gate[:], gate[:])
                V.drain().then_inc(gate_ready, 1)

            gates(0)
            for r in range(2):
                split_rows(g["msg", 0, r], lambda t: gate[:, t, r:r + 1], 1)
                for t, job in enumerate(g["agg", 0, r]):
                    if r == 0:
                        dve.wait_ge(lin_full, job.full)
                        V.tensor_tensor(agg[:, t, :], lin_ps(job, P, D), brow[:, 1, :], ALU.add).then_inc(lin_empty[job.slot], 1)
                    else:
                        add_to(agg, t, job).then_inc(lin_empty[job.slot], 1)
                        V.drain().then_inc(agg_ready, 1)
                    mix(2)
            gates(1)
            dve.wait_ge(pbias_done, 2)
            for r in range(2):
                split_rows(g["msg", 1, r], lambda t: gate[:, t, r:r + 1], 0)
                for t, job in enumerate(g["agg", 1, r]):
                    add_to(x, t, job).then_inc(lin_empty[job.slot], 1)
                V.drain()

            statistics(12)
            job = g["degree"]
            dve.wait_ge(lin_full, job.full)
            V.tensor_scalar(per_node[:], lin_ps(job, P, T), 1.0, None, ALU.max).then_inc(lin_empty[job.slot], 1)
            V.drain()
            V.reciprocal(per_node[:], per_node[:])
            V.drain()
            split_rows(g["sage", 0], None, 0)
            for t in range(T):
                job = g["mean3", 0][t]
                dve.wait_ge(lin_full, job.full)
                V.scalar_tensor_tensor(out=agg[:, t, :], in0=lin_ps(job, P, D), scalar=per_node[:, t:t + 1],
                                       in1=prow[:, 0, :], op0=ALU.mult, op1=ALU.add).then_inc(lin_empty[job.slot], 1)
                V.drain()
                job = g["self3", 0][t]
                add_to(agg, t, job).then_inc(lin_empty[job.slot], 1)
                V.drain().then_inc(agg_ready, 1)
            split_rows(g["sage", 1], None, 0)
            dve.wait_ge(pbias_done, 3)
            for t in range(T):
                job = g["mean3", 1][t]
                add_to(x, t, job, per_node[:, t:t + 1]).then_inc(lin_empty[job.slot], 1)
                V.drain()
                job = g["self3", 1][t]
                add_to(x, t, job).then_inc(lin_empty[job.slot], 1)
                V.drain().then_inc(tile_ready, 1)

        @block.scalar
        def _(act):
            A = nc.scalar
            walk = Walk()
            walk.take(), walk.take()
            hj = [walk.take() for _ in range(3)]
            cj = [walk.take() for _ in range(3)]
            for g in range(GROUPS):
                act.wait_ge(*((group_full, g) if g else (onehot_used, STEPS)))
                if g >= 2:
                    act.wait_ge(rows_out[g % 2], 16 * (g // 2))
                A.activation(run[:, g % 2, :], ps[0:P, (g % 2) * 1536:(g % 2) * 1536 + N], ACT.Copy).then_inc(run_ready, 1)
                if g == PREP[0]:
                    act.wait_ge(norm_ready, 1)
                    for t in range(T):
                        A.activation(x[:, t, :], x[:, t, :], ACT.Relu, bias=nmr[:, t:t + 1], scale=rstd[:, t:t + 1]).then_inc(x0_ready, 1)
                    act.wait_ge(emb_ready, 1)
                    A.activation(emb, turns, ACT.Sin, scale=6.2831850)
                    A.drain().then_inc(emb_ready, 1)
                if g == PREP[1]:
                    for (c0, nn), job in zip(COLS, hj):
                        act.wait_ge(lin_full, job.full)
                        A.activation(z[:, c0:c0 + nn], lin_ps(job, COND, nn), ACT.Identity, bias=fb1[:]).then_inc(lin_empty[job.slot], 1)
                    A.drain()
                    A.activation(zexp, z, ACT.Exp, scale=-1.0).then_inc(zexp_ready, 1)
                if g == PREP[3]:
                    for (c0, nn), job in zip(COLS, cj):
                        act.wait_ge(lin_full, job.full)
                        A.activation(condT[0:COND, c0:c0 + nn], lin_ps(job, COND, nn), ACT.Identity,
                                     bias=fb2[:]).then_inc(lin_empty[job.slot], 1)
            for s in range(T):
                act.wait_ge(crow_ps_full, s + 1)
                if s >= 2:
                    act.wait_ge(crow_out[s % 2], 16 * (s // 2))
                    act.wait_ge(mneg_ready, s - 1)
                src_ps = ps[0:P, (s % 2) * 1024:(s % 2) * 1024 + 1024].bitcast(F16)
                for t0, nt in ((0, 8), (8, T - 8)):
                    A.activation(crow[:, s % 2, t0 * P:(t0 + nt) * P].rearrange("p (t n) -> p t n", n=P),
                                 src_ps[:, t0 * 128:t0 * 128 + nt * (P + 1)].rearrange("p (t n) -> p t n", n=P + 1)[:, :, 0:P],
                                 ACT.Copy)
                A.drain().then_inc(crow_copied, 1)
                act.wait_ge(crow_copied, s + 1)
                act.dma_start(crow_d[s * P:(s + 1) * P, :], crow[:, s % 2, :]).then_inc(crow_out[s % 2], 16)

            with act.Fori(0, BLOCKS) as i:
                walk.enter(i, LIN_PER_BLOCK)
                g = plan_block(walk)

                def norm(ln, count):
                    act.wait_ge(norm_ready, count)
                    for t in range(T + 1):
                        if t < T:
                            if t >= 2:
                                act.wait_ge(scaled_ready, at(i, 2 * T, ln * T + t - 1))
                            A.activation(xn[:, t % 2, :], x[:, t, :], ACT.Identity, bias=nmr[:, t:t + 1],
                                         scale=rstd[:, t:t + 1]).then_inc(xn_ready, 1)
                        if t:
                            act.wait_ge(turn_full, at(i, 2 * T, ln * T + t))
                            A.activation(yT[:, :, (t - 1) * P:t * P], turn_ps(t - 1), ACT.Copy).then_inc(turned_ready, 1)

                norm(0, at(i, 2, 2))
                act.wait_ge(blkc_in, at(i, 48, 48))

                def high_parts(h):
                    for n, job in enumerate(g["proj"][h]):
                        which, (c0, nn) = n // 3, COLS[n % 3]
                        act.wait_ge(lin_full, job.full)
                        A.activation(qk_hi[:, h % 2, which, c0:c0 + nn], lin_ps(job, 128, nn), ACT.Identity,
                                     bias=bcol[:, which, h:h + 1]).then_inc(hi_ready, 1)

                def max_row(h):
                    for n, job in enumerate(g["mrow"][h]):
                        c0, c1 = 4 * n * P, min(4 * n + 4, T) * P
                        act.wait_ge(lin_full, job.full)
                        A.activation(mrow[:, c0:c1], lin_ps(job, 1, c1 - c0), ACT.Copy).then_inc(lin_empty[job.slot], 1)

                def copy_o(h, half):
                    c0, nn = HALVES[half]
                    act.wait_ge(pv_done, at(i, EXPS, h * 2 * T + (half + 1) * T))
                    A.activation(oT[:, c0:c0 + nn], o_ps[:, 0:nn], ACT.Copy).then_inc(o_copied, 1)

                high_parts(0)
                high_parts(1)
                max_row(0)
                for h in range(HEADS):
                    for j in range(2 * T):
                        s, n = SCORES["exp", h, j], h * 2 * T + j
                        nn = HALVES[j // T][1]
                        act.wait_ge(score_full, at(i, SCORES_PER_BLOCK, s.n + 1))
                        if n >= 3:
                            act.wait_ge(pv_done, at(i, EXPS, n - 2))
                            act.wait_ge(psum_done, at(i, EXPS, n - 2))
                        A.activation(prob[:, n % 3, 0:nn], score_ps(s.slot, nn), ACT.Exp, scale=DH ** -0.5).then_inc(exp_done, 1)
                        if j == T:
                            copy_o(h, 0)
                    copy_o(h, 1)
                    if h + 2 < HEADS:
                        high_parts(h + 2)
                    if h + 1 < HEADS:
                        max_row(h + 1)
                norm(1, at(i, 2, 3))
                for n, job in enumerate(g["up"]):
                    k, (c0, nn) = n // 3, COLS[n % 3]
                    act.wait_ge(lin_full, job.full)
                    A.activation(hidT[:, k, c0:c0 + nn], lin_ps(job, 128, nn), ACT.Relu,
                                 bias=bcol[:, 2, k:k + 1]).then_inc(lin_empty[job.slot], 1)
            walk.leave()

            g = plan_post(walk)
            rows_made = [0]

            def turned(jobs, src_, func, to, ready=None, first=None, scaled=True):
                for t in range(T + 1):
                    if t < T:
                        if ready is not None:
                            act.wait_ge(ready, first + t + 1)
                        if t >= 2:
                            act.wait_ge(lin_full, jobs[t - 2].full)
                        if scaled:
                            A.activation(py[:, t % 2, :], src_[:, t, :], func, bias=nmr[:, t:t + 1],
                                         scale=rstd[:, t:t + 1]).then_inc(row_ready, 1)
                        else:
                            A.activation(py[:, t % 2, :], src_[:, t, :], func).then_inc(row_ready, 1)
                    if t:
                        job = jobs[t - 1]
                        act.wait_ge(lin_full, job.full)
                        A.activation(to[:, :, (t - 1) * P:t * P],
                                     lin_ps(job, 128, KD * P).rearrange("p (k n) -> p k n", k=KD),
                                     ACT.Copy).then_inc(lin_empty[job.slot], 1)

            def first_parts(jobs, scale=None):
                for t, job in enumerate(jobs):
                    act.wait_ge(lin_full, job.full)
                    A.activation(pieces[:, 0, t, :], lin_ps(job, P, D), ACT.Copy,
                                 scale=1.0 if scale is None else scale(t)).then_inc(first_piece, 1)

            def gate_logits(layer):
                job = g["gate", layer]
                act.wait_ge(lin_full, job.full)
                A.activation(gate[:].rearrange("p t r -> p (t r)"), lin_ps(job, P, 2 * T), ACT.Exp,
                             scale=-1.0).then_inc(lin_empty[job.slot], 1)
                A.drain().then_inc(gate_exp, 1)
                act.wait_ge(gate_ready, layer + 1)

            act.wait_ge(norm_ready, 10)
            turned(g["norm1"], x, ACT.Relu, yT)
            first_parts(g["beta1"])
            act.wait_ge(norm_ready, 11)
            turned(g["norm2"], x, ACT.Relu, yT)
            gate_logits(0)
            for r in range(2):
                first_parts(g["msg", 0, r], lambda t: gate[:, t, r:r + 1])
            turned(g["turn2"], agg, ACT.Relu, hidT, ready=agg_ready, first=0, scaled=False)
            gate_logits(1)
            for r in range(2):
                first_parts(g["msg", 1, r], lambda t: gate[:, t, r:r + 1])
            act.wait_ge(norm_ready, 12)
            turned(g["norm3"], x, ACT.Relu, yT)
            first_parts(g["sage", 0])
            turned(g["turn3"], agg, ACT.Tanh, hidT, ready=agg_ready, first=T, scaled=False)
            first_parts(g["sage", 1])

        @block.tensor
        def _(pe):
            mm = nc.tensor.matmul
            walk = Walk()

            def reuse(job):
                if job.reuse is not None:
                    pe.wait_ge(lin_empty[job.slot], job.reuse)

            jb, jt = walk.take(), walk.take()
            pe.wait_ge(consts_set, 2)
            pe.wait_ge(ecount_ready, 1)
            mm(lin_ps(jb, P, BUCKETS), tri[:], cnt[:], start=True, stop=True).then_inc(lin_full, 1)
            mm(lin_ps(jt, 128, BUCKETS), ones_sq[:], cnt[:], start=True, stop=True).then_inc(lin_full, 1)
            hj = [walk.take() for _ in range(3)]
            cj = [walk.take() for _ in range(3)]
            for c in range(EC):
                pe.wait_ge(row_hot_ready, c + 1)
                pe.wait_ge(slot_hot_ready, c + 1)
                mm(o_ps[:, 0:2 * SLOTS], row_hot[:, c % 4, :], slot_hot[:, c % 4, :, :].rearrange("p a s -> p (a s)"),
                   start=(c == 0), stop=(c == EC - 1)).then_inc(edge_placed, 1)
            for g in range(GROUPS):
                if g >= 2:
                    pe.wait_ge(run_ready, g - 1)
                for j in range(STEPS):
                    n = g * STEPS + j
                    pe.wait_ge(onehot_ready, n + 1)
                    for c0, nn in WIDE:
                        last = mm(ps[0:P, (g % 2) * 1536 + c0:(g % 2) * 1536 + c0 + nn], onehot_dst[:, n % 4, :],
                                  onehot_src[:, n % 4, c0:c0 + nn], start=(j == 0), stop=(g == 0 and j == STEPS - 1))
                    last.then_inc(onehot_used, 1)
                if g:
                    pe.wait_ge(carry_ready, g)
                    pe.wait_ge(run_ready, g)
                    for c0, nn in WIDE:
                        last = mm(ps[0:P, (g % 2) * 1536 + c0:(g % 2) * 1536 + c0 + nn], carry[:, g % 2, :],
                                  run[:, (g - 1) % 2, c0:c0 + nn], start=False, stop=True)
                    last.then_inc(group_full, 1)
                if g == PREP[1]:
                    pe.wait_ge(pre_in, 80)
                    pe.wait_ge(emb_ready, 2)
                    for (c0, nn), job in zip(COLS, hj):
                        reuse(job)
                        mm(lin_ps(job, COND, nn), fw1[:], emb[:, c0:c0 + nn], start=True, stop=True).then_inc(lin_full, 1)
                if g == PREP[3]:
                    pe.wait_ge(silu_ready, 1)
                    for (c0, nn), job in zip(COLS, cj):
                        reuse(job)
                        mm(lin_ps(job, COND, nn), fw2[:], silu[:, c0:c0 + nn], start=True, stop=True).then_inc(lin_full, 1)
            pe.wait_ge(run_ready, GROUPS)
            for s in range(T):
                if s >= 2:
                    pe.wait_ge(crow_copied, s - 1)
                dst_ps = ps[0:P, (s % 2) * 1024:(s % 2) * 1024 + 1024].bitcast(F16)
                for t in range(T):
                    if s == 0:
                        pe.wait_ge(ct_ready, t + 1)
                    c0 = t * (P + 1) if t < 8 else 1024 + (t - 8) * (P + 1)
                    last = nc.tensor.transpose(dst_ps[:, c0:c0 + P], ct[:, t, s * P:(s + 1) * P], ident16[:])
                last.then_inc(crow_ps_full, 1)
            pe.wait_ge(crow_copied, T)

            def row_product(job, lhs, t, weight):
                reuse(job)
                for k in range(KD):
                    last = mm(lin_ps(job, P, D), lhs[:, k, t * P:(t + 1) * P], weight[:, k, :],
                              start=(k == 0), stop=(k == KD - 1))
                last.then_inc(lin_full, 1)

            def col_product(job, lhs, chunk, weight, m):
                c0, nn = COLS[chunk]
                reuse(job)
                for k in range(KD):
                    last = mm(lin_ps(job, 128, nn), weight[:, k, m * 128:(m + 1) * 128], lhs[:, k, c0:c0 + nn],
                              start=(k == 0), stop=(k == KD - 1))
                last.then_inc(lin_full, 1)

            with pe.Fori(0, BLOCKS) as i:
                walk.enter(i, LIN_PER_BLOCK)
                g = plan_block(walk)
                pe.wait_ge(blkc_in, at(i, 48, 48))

                def affine(ln):
                    for t in range(T + 1):
                        if t < T:
                            mm(scale_ps(t), condT[:, t * P:(t + 1) * P], cw[:, 2 * ln, :],
                               start=True, stop=True).then_inc(scale_full, 1)
                        if t:
                            n = ln * T + t
                            pe.wait_ge(scaled_ready, at(i, 2 * T, n))
                            if t > 2:
                                pe.wait_ge(turned_ready, at(i, 2 * T, n - 2))
                            for k in range(KD):
                                o = turn_ps(t - 1)[:, k, :]
                                mm(o, y[:, (t - 1) % 2, k * 128:(k + 1) * 128], ident[0:P, 0:P], start=True, stop=False)
                                last = mm(o, cw[:, 2 * ln + 1, k * 128:(k + 1) * 128], condT[:, (t - 1) * P:t * P],
                                          start=False, stop=True)
                            last.then_inc(turn_full, 1)
                    pe.wait_ge(turned_ready, at(i, 2 * T, (ln + 1) * T))

                affine(0)
                pe.wait_ge(w_in[1], at(i, 32, 16))
                pe.wait_ge(w_in[2], at(i, 32, 16))

                def project(h):
                    for n, job in enumerate(g["proj"][h]):
                        col_product(job, yT, n % 3, w[1 + n // 3], h)

                def projected(h):
                    for job in g["proj"][h][-2:]:
                        pe.wait_ge(lin_empty[job.slot], job.emptied)

                def slot_free(s):
                    if s.before is not None:
                        b = s.before
                        if b.kind == "max":
                            pe.wait_ge(max_done, at(i, MAXES, b.h * 2 * T + b.j + 1))
                        else:
                            pe.wait_ge(exp_done, at(i, EXPS, b.h * 2 * T + b.j + 1))

                def max_scores(h, j):
                    s = SCORES["max", h, j]
                    t, (c0, nn) = j // 2, HALVES[j % 2]
                    slot_free(s)
                    for b0 in (0, 512):
                        bn = min(nn - b0, 512)
                        last = mm(score_ps(s.slot, nn)[:, b0:b0 + bn], qk_hi[:, h % 2, 0, t * P:(t + 1) * P],
                                  qk_hi[:, h % 2, 1, c0 + b0:c0 + b0 + bn], start=True, stop=True)
                    last.then_inc(score_full, 1)

                def exp_scores(h, j):
                    s = SCORES["exp", h, j]
                    t, (c0, nn) = j % T, HALVES[j // T]
                    slot_free(s)
                    rows = slice(t * P, (t + 1) * P)
                    hi, lo = qk_hi[:, h % 2, :, :], qk_lo[:, h % 2, :, :]
                    for b0 in (0, 512):
                        bn = min(nn - b0, 512)
                        cols = slice(c0 + b0, c0 + b0 + bn)
                        o = score_ps(s.slot, nn)[:, b0:b0 + bn]
                        mm(o, hi[:, 1, rows], hi[:, 0, cols], start=True, stop=False)
                        mm(o, hi[:, 1, rows], lo[:, 0, cols], start=False, stop=False)
                        mm(o, lo[:, 1, rows], hi[:, 0, cols], start=False, stop=False)
                        last = mm(o, ones_r[:, 0:P], mrow[:, cols], start=False, stop=True)
                    last.then_inc(score_full, 1)

                def weighted_values(h, j):
                    n, t, (c0, nn) = h * 2 * T + j, j % T, HALVES[j // T]
                    pe.wait_ge(prob_ready, at(i, EXPS, n + 1))
                    if t == 0 and n >= T:
                        pe.wait_ge(o_copied, at(i, 2 * HEADS, n // T))
                    for b0 in (0, 512):
                        bn = min(nn - b0, 512)
                        last = mm(o_ps[:, b0:b0 + bn], vrow[:, t, h * DH:(h + 1) * DH], prob[:, n % 3, b0:b0 + bn],
                                  start=(t == 0), stop=(t == T - 1))
                    last.then_inc(pv_done, 1)

                def max_row(h):
                    pe.wait_ge(neg_max_ready, at(i, HEADS, h + 1))
                    for n, job in enumerate(g["mrow"][h]):
                        reuse(job)
                        tiles = range(4 * n, min(4 * n + 4, T))
                        for t in tiles:
                            last = mm(lin_ps(job, 1, P, (t - 4 * n) * P), nmx[:, t:t + 1], ident[0:P, 0:P],
                                      start=True, stop=True)
                        last.then_inc(lin_full, 1)
                    for job in g["mrow"][h][-2:]:
                        pe.wait_ge(lin_empty[job.slot], job.emptied)

                project(0)
                pe.wait_ge(w_in[0], at(i, 32, 16))
                for t, job in enumerate(g["v"]):
                    row_product(job, yT, t, w[0])
                    if t == 0:
                        projected(0)
                    max_scores(0, 2 * t)
                    max_scores(0, 2 * t + 1)
                project(1)
                max_row(0)
                projected(1)
                for job in g["v"][-2:]:
                    pe.wait_ge(lin_empty[job.slot], job.emptied)
                for h in range(HEADS):
                    for j in range(2 * T):
                        exp_scores(h, j)
                        if h + 1 < HEADS:
                            max_scores(h + 1, j)
                        if j:
                            weighted_values(h, j - 1)
                    weighted_values(h, 2 * T - 1)
                    if h + 2 < HEADS:
                        project(h + 2)
                    if h + 1 < HEADS:
                        max_row(h + 1)
                    if h + 2 < HEADS:
                        projected(h + 2)
                    job = g["den"][h]
                    reuse(job)
                    pe.wait_ge(psum_done, at(i, EXPS, (h + 1) * 2 * T))
                    for t in range(T):
                        last = mm(lin_ps(job, P, 1, t), pacc[:, t * P:(t + 1) * P], ones_f[0:P, 0:1], start=True, stop=True)
                    last.then_inc(lin_full, 1)
                    if h == 0:
                        pe.wait_ge(w_in[0], at(i, 32, 32))
                    pe.wait_ge(o_copied, at(i, 2 * HEADS, 2 * h + 2))
                    for t, job in enumerate(g["out"][h]):
                        reuse(job)
                        mm(lin_ps(job, P, D), oT[:, t * P:(t + 1) * P], w[0][:, h, :], start=True, stop=True).then_inc(lin_full, 1)
                affine(1)
                pe.wait_ge(w_in[1], at(i, 32, 32))
                for n, job in enumerate(g["up"]):
                    col_product(job, yT, n % 3, w[1], n // 3)
                for job in g["up"][-2:]:
                    pe.wait_ge(lin_empty[job.slot], job.emptied)
                pe.wait_ge(w_in[2], at(i, 32, 32))
                for t, job in enumerate(g["down"]):
                    row_product(job, hidT, t, w[2])
            walk.leave()


            g = plan_post(walk)
            rows_turned = [0]
            split = [0]

            def turn(jobs):
                for t, job in enumerate(jobs):
                    reuse(job)
                    rows_turned[0] += 1
                    pe.wait_ge(row_ready, rows_turned[0])
                    for k in range(KD):
                        last = nc.tensor.transpose(lin_ps(job, 128, P, k * P), py[:, t % 2, k * 128:(k + 1) * 128],
                                                   ident[0:P, 0:P])
                    last.then_inc(lin_full, 1)
                for job in jobs[-2:]:
                    pe.wait_ge(lin_empty[job.slot], job.emptied)

            def gather(job, counts, t, first, self_=None):
                reuse(job)
                if self_ is not None:
                    lhs, weight = self_
                    for k in range(KD):
                        mm(lin_ps(job, P, D), lhs[:, k, t * P:(t + 1) * P], weight[:, k, :], start=(k == 0), stop=False)
                for k in range(T):
                    if t == 0:
                        pe.wait_ge(pieces_ready, first + k + 1)
                    for piece in range(3):
                        last = mm(lin_ps(job, P, D), counts[:, k, t * P:(t + 1) * P], pieces[:, piece, k, :],
                                  start=(self_ is None and k == 0 and piece == 0), stop=(k == T - 1 and piece == 2))
                last.then_inc(lin_full, 1)

            def edge_counts(job, mats):
                reuse(job)
                for t in range(T):
                    for k in range(T):
                        last = mm(lin_ps(job, P, 1, t), mats[:, k, t * P:(t + 1) * P], ones_h[:], start=(k == 0), stop=(k == T - 1))
                last.then_inc(lin_full, 1)

            pe.wait_ge(consts_set, 3)
            turn(g["norm1"])
            pe.wait_ge(w_in[0], 32 * BLOCKS + 16)
            for t, job in enumerate(g["beta1"]):
                row_product(job, yT, t, w[0])
            edge_counts(g["count"], ct)
            pe.wait_ge(w_in[1], 32 * BLOCKS + 16)
            for t in range(T):
                gather(g["mean1"][t], ct, t, 0)
                row_product(g["self1"][t], yT, t, w[1])

            turn(g["norm2"])
            pe.wait_ge(w_in[2], 32 * BLOCKS + 16)
            pe.wait_ge(ctr_in, 16)
            pe.wait_ge(ct2_in, 16)
            for layer, lhs in ((0, yT), (1, hidT)):
                job = g["gate", layer]
                reuse(job)
                for t in range(T):
                    for k in range(KD):
                        last = mm(lin_ps(job, P, 2, 2 * t), lhs[:, k, t * P:(t + 1) * P], gate_w[:, layer, k, :],
                                  start=(k == 0), stop=(k == KD - 1))
                last.then_inc(lin_full, 1)
                pe.wait_ge(mixed_ready, layer + 1)
                if layer:
                    pe.wait_ge(pw_in, 16)
                for r, counts in ((0, ct), (1, ct2)):
                    for t, job in enumerate(g["msg", layer, r]):
                        row_product(job, lhs, t, mixed[layer][r])
                    for t, job in enumerate(g["agg", layer, r]):
                        gather(job, counts, t, T * (1 + 2 * layer + r), (lhs, w[2]) if r == 0 else None)
                if layer == 0:
                    turn(g["turn2"])

            turn(g["norm3"])
            pe.wait_ge(ctr_in, 32)
            edge_counts(g["degree"], ct)
            pe.wait_ge(pw_in, 64)
            for t, job in enumerate(g["sage", 0]):
                row_product(job, yT, t, w[0])
            for t in range(T):
                gather(g["mean3", 0][t], ct, t, 5 * T)
                row_product(g["self3", 0][t], yT, t, w[1])
            turn(g["turn3"])
            for t, job in enumerate(g["sage", 1]):
                row_product(job, hidT, t, w[2])
            pe.wait_ge(pw_in, 80)
            for t in range(T):
                gather(g["mean3", 1][t], ct, t, 6 * T)
                row_product(g["self3", 1][t], hidT, t, w[0])


def kernel(**inputs):
    import concourse.bacc as bacc
    from concourse.bass_utils import run_bass_kernel_spmd as launch

    c = np.ascontiguousarray
    g = {k: np.asarray(v) for k, v in inputs.items()}
    L0 = {k[7:]: v for k, v in g.items() if k.startswith("L0_gnn_")}
    arrays = {
        "x": c(g["x"]), "src": c(g["src"]), "dst": c(g["dst"]), "edge_type_2": c(g["edge_type_2"]),
        "node_vec1": c(g["node_vec1"].reshape(N)),
        "L0_gnn_f_w1": c(L0["f_w1"]), "L0_gnn_f_w2": c(L0["f_w2"]),
        "f_b1": c(L0["f_b1"].reshape(COND, 1)), "f_b2": c(L0["f_b2"].reshape(COND, 1)),
        "wv": c(np.concatenate([L0["wv"], g["L1_gnn_wn"][None]])),
        "wq": c(np.concatenate([L0["wq"], g["L1_gnn_wc"][None]])),
        "wk": c(np.concatenate([L0["wk"], g["L2_gnn_root1"][None]])),
        "wo": c(L0["wo"]), "m_w1": c(L0["m_w1"]), "m_w2": c(L0["m_w2"]),
        "brow": c(np.stack([L0["bv"], L0["bo"], L0["m_b2"]], 1)),
        "bcol": c(np.stack([L0["bq"], L0["bk"], L0["m_b1"]], 1).reshape(BLOCKS, 3, KD, 128)
                  .transpose(0, 3, 1, 2).reshape(BLOCKS, 128, 3 * KD)),
        "cw": c(np.stack([np.concatenate([L0[m + "_w"], L0[m + "_b"][:, None, :]], 1)
                          for m in ("s1", "b1", "s2", "b2")], 2)),
    }
    arrays.update({
        "basis1": c(g["L2_gnn_basis1"]), "basis2": c(g["L2_gnn_basis2"]),
        "att": c(np.stack([g["L2_gnn_att1"], g["L2_gnn_att2"]]).reshape(-1)),
        "gate_w": c(np.stack([g["L2_gnn_gate_w1"], g["L2_gnn_gate_w2"]])[..., 0]
                    .reshape(2, 2, KD, 128).transpose(3, 0, 2, 1).reshape(128, 4 * KD)),
        "root2": c(g["L2_gnn_root2"]),
        "post_rows": c(np.stack([g["L1_gnn_bias"], g["L2_gnn_bias1"], g["L2_gnn_bias2"], g["L3_gnn_b1"], g["L3_gnn_b2"]])),
        "W1_l": c(g["L3_gnn_W1_l"].T), "W1_r": c(g["L3_gnn_W1_r"].T),
        "W2_l": c(g["L3_gnn_W2_l"].T), "W2_r": c(g["L3_gnn_W2_r"].T),
    })
    nc = bacc.Bacc("TRN2", target_bir_lowering=False, num_devices=1, dynamic_dma_scratch_size=8192)
    aps = {k: nc.dram_tensor("in_" + k, v.shape, mybir.dt.from_np(v.dtype), kind="ExternalInput").ap()
           for k, v in arrays.items()}
    out = nc.dram_tensor("out", (N, D), F32, kind="ExternalOutput").ap()
    build(nc, aps, out)
    return launch(nc, [{"in_" + k: v for k, v in arrays.items()}], core_ids=[0]).results[0]["out"]
```

```python
from contextlib import ExitStack

import numpy as np
import concourse.bass as bass
from concourse import mybir

F32, F32R, F16, BF16 = mybir.dt.float32, mybir.dt.float32r, mybir.dt.float16, mybir.dt.bfloat16
I32 = mybir.dt.int32
ALU, ACT, AX = mybir.AluOpType, mybir.ActivationFunctionType, mybir.AxisListType

N, D, E = 1250, 512, 20000
P = 125
T = N // P
KD = D // 128
HEADS, BLOCKS, BASES = 4, 4, 30
DH = D // HEADS
COND, FREQS = 16, 32
EC = E // P
BUCKETS = 2 * T
GROUP, STEPS = 512, 4
GROUPS = (E + BUCKETS * (GROUP - 1)) // GROUP
SLOTS = GROUPS * STEPS
QUARTER = 314
HALF = 2 * QUARTER
HALVES = (0, N - HALF)
COLS = ((0, 418), (418, 416), (834, 416))
WIDE = ((0, 512), (512, 512), (1024, 226))
EPS = 1e-5
BIG = 1.0e30
PREP = (10, 20, 30)
COND_AT = (40, 43, 46)


class Job:

    def __init__(self, slot, full, reuse, emptied):
        self.slot, self.full, self.reuse, self.emptied = slot, full, reuse, emptied


class Walk:

    def __init__(self):
        self.n, self.i, self.per = 0, None, 0

    def enter(self, i, per):
        self.i, self.per = i, per

    def leave(self):
        self.n, self.i = self.n + (BLOCKS - 1) * self.per, None

    def take(self):
        n, self.n = self.n, self.n + 1
        if self.i is None:
            return Job(n % 2, n + 1, n // 2 or None, n // 2 + 1)
        a, b = self.i * self.per, self.i * (self.per // 2)
        return Job(n % 2, a + (n + 1), b + n // 2, b + (n // 2 + 1))


def at(i, per, k):
    return k if i is None else i * per + k


def plan_block(w):
    g = {"proj": {}, "mrow": {}, "den": {}, "out": {}}

    def project(h):
        if h < HEADS:
            g["proj"][h] = [w.take() for _ in range(6)]

    def max_row(h):
        if h < HEADS:
            g["mrow"][h] = [w.take() for _ in range(3)]

    project(0)
    g["v"] = [w.take() for _ in range(T)]
    project(1)
    max_row(0)
    for h in range(HEADS):
        project(h + 2)
        max_row(h + 1)
        g["den"][h] = w.take()
        g["out"][h] = [w.take() for _ in range(T)]
    g["up"] = [w.take() for _ in range(3 * KD)]
    g["down"] = [w.take() for _ in range(T)]
    return g


_w = Walk()
plan_block(_w)
LIN_PER_BLOCK = _w.n


def plan_post(w):
    g = {}

    def tiles(*names):
        for name in names:
            g[name] = [w.take() for _ in range(T)]

    def woven(*names):
        for name in names:
            g[name] = []
        for _ in range(T):
            for name in names:
                g[name].append(w.take())

    tiles("norm1", "beta1")
    g["count"] = w.take()
    woven("mean1", "self1")
    tiles("norm2")
    g["gate", 0] = w.take()
    tiles(("msg", 0, 0), ("agg", 0, 0), ("msg", 0, 1), ("agg", 0, 1), "turn2")
    g["gate", 1] = w.take()
    tiles(("msg", 1, 0), ("agg", 1, 0), ("msg", 1, 1), ("agg", 1, 1))
    tiles("norm3")
    g["degree"] = w.take()
    tiles(("sage", 0))
    woven(("mean3", 0), ("self3", 0))
    tiles("turn3", ("sage", 1))
    woven(("mean3", 1), ("self3", 1))
    return g


class Score:

    def __init__(self, n, kind, h, j, before):
        self.n, self.slot, self.kind, self.h, self.j, self.before = n, n % 2, kind, h, j, before


def plan_scores():
    out, last = [], [None, None]

    def add(kind, h, j):
        s = Score(len(out), kind, h, j, last[len(out) % 2])
        last[s.slot] = s
        out.append(s)

    for j in range(2 * T):
        add("max", 0, j)
    for h in range(HEADS):
        for j in range(2 * T):
            add("exp", h, j)
            if h + 1 < HEADS:
                add("max", h + 1, j)
    return out


SCORES = {(s.kind, s.h, s.j): s for s in plan_scores()}
SCORES_PER_BLOCK = len(SCORES)
EXPS = MAXES = HEADS * 2 * T


def build(nc, a, out):
    stack = ExitStack()
    with stack:
        def sem(name):
            return stack.enter_context(nc.semaphore(name))

        def sb_in(ctx):
            return lambda name, shape, dt: ctx.enter_context(nc.sbuf_tensor(name, shape, dt))

        sb = sb_in(stack)
        typed_t = nc.dram_tensor("typed_t", (2 * N, N), F16, kind="Internal").ap()
        crow_d = nc.dram_tensor("crow_d", (N, N), F16, kind="Internal").ap()

        x = sb("x", [P, T, D], F32)
        yT = sb("yT", [128, KD, N], F32)
        big = sb("big", [128, T * D], F32)
        vrow = big[0:P, :].rearrange("p (t d) -> p t d", d=D)
        hidT = big[:, 0:KD * N].rearrange("p (k n) -> p k n", n=N)
        w = [sb(f"w{s}", [128, KD, D], F32) for s in range(3)]
        ct = sb("ct", [P, T, N], F16)
        ident = sb("ident", [128, 128], F32)
        brow = sb("brow", [P, 3, D], F32)
        stats = sb("stats", [P, T, 6], F32)
        mv = sb("mv", [P, T, 2], F32)
        var = sb("var", [P, T], F32)
        rstd = sb("rstd", [P, T], F32)
        nmr = sb("nmr", [P, T], F32)
        mhalf = sb("mhalf", [P, T], F32)
        ones_f = sb("ones_f", [128, 1], F32)
        zcol = sb("zcol", [128, 1], F32)
        tick = sb("tick", [1, MAXES], F32)
        ps = stack.enter_context(nc.psum_tensor("ps", [128, 8 * 512], F32))

        def in_banks(p, c0):
            return ps[0:p, c0:c0 + 1024].rearrange("p (b n) -> p b n", n=512)[:, :, 0:QUARTER]

        def in_quarters(rows):
            return rows.rearrange("p (b n) -> p b n", n=QUARTER)

        def lin_ps(job, parts, n, c0=0):
            return ps[0:parts, 3072 + 512 * job.slot + c0:3072 + 512 * job.slot + c0 + n]

        def score_ps(slot):
            return in_banks(P, slot * 1024)

        o_ps = ps[:, 2048:3072]
        o_halves = in_banks(128, 2048)

        def scale_ps(t):
            return ps[0:P, (t % 2) * 1024:(t % 2) * 1024 + D]

        def turn_ps(t):
            return ps[:, (t % 2) * 1024 + 512:(t % 2) * 1024 + 1024].rearrange("p (k n) -> p k n", k=KD)

        lin_full = sem("lin_full")
        lin_empty = [sem(f"lin_empty{s}") for s in range(2)]
        consts_set = sem("consts_set")
        edges_in = sem("edges_in")
        rows_init = sem("rows_init")
        payload_ready = sem("payload_ready")
        ecount_ready = sem("ecount_ready")
        slot_hot_ready = sem("slot_hot_ready")
        row_hot_ready = sem("row_hot_ready")
        edge_placed = sem("edge_placed")
        carry_ready = sem("carry_ready")
        onehot_ready = sem("onehot_ready")
        onehot_used = sem("onehot_used")
        group_full = sem("group_full")
        run_ready = sem("run_ready")
        rows_out = [sem(f"rows_out{s}") for s in range(2)]
        typed_in = [sem(f"typed_in{t}") for t in range(T // 2)]
        ct_ready = sem("ct_ready")
        crow_ps_full = sem("crow_ps_full")
        crow_copied = sem("crow_copied")
        mneg_ready = sem("mneg_ready")
        crow_out = [sem(f"crow_out{s}") for s in range(2)]
        pre_in = sem("pre_in")
        phase_ready = sem("phase_ready")
        emb_ready = sem("emb_ready")
        silu_ready = sem("silu_ready")
        zexp_ready = sem("zexp_ready")
        var_ready = sem("var_ready")
        rstd_ready = sem("rstd_ready")
        norm_ready = sem("norm_ready")
        xn_ready = sem("xn_ready")
        x0_ready = sem("x0_ready")
        scale_full = sem("scale_full")
        stage_in = sem("stage_in")
        cw_ready = sem("cw_ready")
        cond_hi = sem("cond_hi")
        scaled_ready = sem("scaled_ready")
        turn_full = sem("turn_full")
        turned_ready = sem("turned_ready")
        blk_done = sem("blk_done")
        blkc_in = sem("blkc_in")
        w_in = [sem(f"w_in{s}") for s in range(3)]
        hi_ready = sem("hi_ready")
        score_full = sem("score_full")
        exp_done = sem("exp_done")
        max_done = sem("max_done")
        neg_max_ready = sem("neg_max_ready")
        prob_ready = sem("prob_ready")
        pv_done = sem("pv_done")
        psum_done = sem("psum_done")
        o_copied = sem("o_copied")
        xbias_done = sem("xbias_done")
        out_done = sem("out_done")
        sums_read = sem("sums_read")

        keep = ExitStack()
        sk = sb_in(keep)
        mneg = sk("mneg", [P, T, N], BF16)
        condS = sk("condS", [128, N + 2], F32R)
        fw1 = sk("fw1", [2 * FREQS, COND], F32)
        fw2 = sk("fw2", [COND, 128], F32)
        fb1 = sk("fb1", [COND, 1], F32)
        fb2 = sk("fb2", [128, 1], F32)
        freq = sk("freq", [2 * FREQS, 1], F32)
        quarter = sk("quarter", [2 * FREQS, 1], F32)
        noise = yT[0:2 * FREQS, 0, :]
        turns = yT[0:2 * FREQS, 1, :]
        whole = yT[0:2 * FREQS, 2, :]
        emb = yT[0:2 * FREQS, 3, :]
        z = hidT[0:COND, 0, :]
        zexp = hidT[0:COND, 1, :]
        silu = hidT[0:COND, 2, :]

        adj = ExitStack()
        sa = sb_in(adj)
        onehot_src = sa("onehot_src", [128, 4, N], F16)
        onehot_dst = sa("onehot_dst", [128, 4, P], F16)
        col_iota = sa("col_iota", [128, N], F16)
        run = sa("run", [P, 2, N], F16)
        row_hot = sa("row_hot", [P, 4, 128], F16)
        slot_hot = sa("slot_hot", [P, 4, 2, SLOTS], F16)
        carry = sa("carry", [P, 2, P], F16)
        typed1 = mneg[:].bitcast(F16)
        crow = sa("crow", [P, 2, N], F16)
        zero_row = sa("zero_row", [P, N], F16)
        ident16 = sa("ident16", [P, P], F16)
        esrc = sa("esrc", [P, EC], I32)
        edst = sa("edst", [P, EC], I32)
        etyp = sa("etyp", [P, EC], I32)
        key = sa("key", [P, EC], F32)
        thr = sa("thr", [P, BUCKETS + 1], F32)
        ge = yT[0:P, :, :].rearrange("p k n -> p (k n)")[:, 0:(BUCKETS + 1) * EC].rearrange("p (b c) -> p b c", c=EC)
        oh = mneg[:].rearrange("p t n -> p (t n)").bitcast(F32)[:, 0:BUCKETS * EC].rearrange("p (b c) -> p b c", c=EC)
        incl = big[0:P, 0:BUCKETS * EC].rearrange("p (b c) -> p b c", c=EC)
        zero = sa("zero", [128, 1], F32)
        bsum = sa("bsum", [P, EC], F32)
        src1 = sa("src1", [P, EC], F32)
        dst1 = sa("dst1", [P, EC], F32)
        cnt = sa("cnt", [P, BUCKETS], F32)
        tri = sa("tri", [P, P], F32)
        ones_sq = sa("ones_sq", [P, 128], F32)
        toti = sa("toti", [128, BUCKETS], I32)
        ngr = sa("ngr", [128, BUCKETS], F32)
        egr = sa("egr", [128, BUCKETS], F32)
        base = sa("base", [P, BUCKETS], F32)
        base2 = sa("base2", [P, BUCKETS], F32)
        pos = sa("pos", [P, EC], F32)
        posi = sa("posi", [P, EC], I32)
        ia = sa("ia", [P, EC], I32)
        ib = sa("ib", [P, EC], I32)
        ic = sa("ic", [P, EC], I32)
        slot_row = sa("slot_row", [P, EC], F32)
        slot_col = sa("slot_col", [P, EC], F32)
        gi = sa("gi", [128, GROUPS + 1], F32)
        gcmp = sa("gcmp", [128, GROUPS + 1, BUCKETS], F32)
        bk = sa("bk", [128, GROUPS + 1], F32)
        same = sa("same", [128, GROUPS], F32)
        rowf = sa("rowf", [128, GROUPS], F32)
        rowi = sa("rowi", [128, GROUPS], I32)
        part = sa("part", [128, 1], F32)
        es = sa("es", [128, 2, SLOTS], F32)
        adj.close()

        att = ExitStack()
        sl = sb_in(att)
        qk_hi = sl("qk_hi", [128, 2, 2, N], F32R)
        qk_lo = sl("qk_lo", [128, 2, 2, N], F32R)
        prob = sl("prob", [P, 3, HALF], F32)
        pacc = sl("pacc", [P, N], F32)
        oT = sl("oT", [128, N], F32)
        xn = pacc[:, 0:2 * D].rearrange("p (s d) -> p s d", d=D)
        y = prob[:].rearrange("p s n -> p (s n)")[:, 0:2 * D].rearrange("p (s d) -> p s d", d=D)
        cw = sl("cw", [128, 4, D], F32R)
        stage = oT[:, 0:2 * D].rearrange("p (a d) -> p a d", d=D)
        mrow = sl("mrow", [1, N], F32R)
        bcol = sl("bcol", [128, 3, KD], F32)
        mxp = sl("mxp", [P, T, 2], F32)
        nmx = sl("nmx", [P, T], F32R)
        mx = sl("mx", [P, T], F32)
        ident_r = sl("ident_r", [P, P + 1], F32R)
        rden = sl("rden", [P, T], F32)
        ones_r = sl("ones_r", [1, 128], F32R)
        att.close()
        keep.close()

        post = ExitStack()
        so = sb_in(post)
        pieces = so("pieces", [P, 2, T, D], F32R)
        counts_r = so("counts_r", [P, 2, T, P], F32R)
        ct2 = so("ct2", [P, T, N], F16)
        agg = so("agg", [P, T, D], F32)
        ring = [so(f"basis{s}", [128, D], F32) for s in range(3)]
        py = so("py", [P, 2, D], F32)
        att_w = big[:, KD * N:KD * N + 4 * BASES].rearrange("p (a r b) -> p a r b", a=2, r=2)
        gate_w = so("gate_w", [128, 2, KD, 2], F32)
        gate = so("gate", [P, T, 2], F32)
        per_node = stats[:].rearrange("p t s -> p (t s)")[:, 0:T]
        ones_h = so("ones_h", [P, 1], F16)
        post.close()
        mixed = [[big[:, r * KD * D:(r + 1) * KD * D].rearrange("p (k n) -> p k n", n=D) for r in range(2)],
                 [w[0], w[1]]]
        post_in = sem("post_in")
        pw_in = sem("pw_in")
        ct2_in = sem("ct2_in")
        ctr_in = sem("ctr_in")
        basis_in = [sem(f"basis_in{s}") for s in range(3)]
        basis_used = sem("basis_used")
        row_ready = sem("row_ready")
        first_piece = sem("first_piece")
        pieces_ready = sem("pieces_ready")
        counts_ready = sem("counts_ready")
        rows3_in = sem("rows3_in")
        att_in = sem("att_in")
        gate_exp = sem("gate_exp")
        gate_ready = sem("gate_ready")
        mixed_ready = sem("mixed_ready")
        agg_ready = sem("agg_ready")
        pbias_done = sem("pbias_done")
        tile_ready = sem("tile_ready")

        block = stack.enter_context(nc.Block())

        @block.sync
        def _(sp):
            for dst_, name in ((esrc, "src"), (edst, "dst"), (etyp, "edge_type_2")):
                sp.dma_start(dst_[:], a[name].rearrange("(p c) -> p c", c=EC)).then_inc(edges_in, 16)
            sp.dma_start(x[:], a["x"].rearrange("(t p) d -> p t d", p=P)).then_inc(pre_in, 16)
            for dst_, name in ((fw1, "L0_gnn_f_w1"), (fw2, "fw2_stack"), (fb1, "f_b1"), (fb2, "fb2_stack")):
                sp.dma_start(dst_[:], a[name]).then_inc(pre_in, 16)
            for s, name in ((0, "wv"), (1, "wq"), (2, "wk")):
                sp.dma_start(w[s][:], a[name][0].rearrange("(k p) n -> p k n", p=128)).then_inc(w_in[s], 16)
            sp.wait_ge(consts_set, 1)
            for b in range(BUCKETS):
                sp.dma_start(typed_t[b * P:(b + 1) * P, :], zero_row[:]).then_inc(rows_init, 16)
            sp.wait_ge(payload_ready, 1)
            sp.dma_start(noise, a["node_vec1"].partition_broadcast(2 * FREQS)).then_inc(phase_ready, 16)
            for s in range(2):
                sp.wait_ge(rows_out[s], 16 * ((GROUPS + 1 - s) // 2))
            for t in range(0, T, 2):
                for r, to in ((0, ct), (1, typed1)):
                    sp.dma_start(to[:, t:t + 2, :], typed_t[r * N + t * P:r * N + (t + 2) * P, :]
                                 .rearrange("(t p) n -> p t n", p=P)).then_inc(typed_in[t // 2], 16)
            walk = Walk()
            walk.n = 8
            sp.wait_ge(blk_done, 1)
            sp.dma_start(stage, a["cw1"][0]).then_inc(stage_in, 16)
            with sp.Fori(0, BLOCKS) as i:
                walk.enter(i, LIN_PER_BLOCK)
                g = plan_block(walk)
                sp.wait_ge(blk_done, at(i, 1, 1))
                sp.dma_start(brow[:], a["brow"][i].partition_broadcast(P)).then_inc(blkc_in, 16)
                sp.wait_ge(cw_ready, at(i, 2, 1))
                sp.dma_start(stage, a["cw2"][i]).then_inc(stage_in, 16)
                sp.dma_start(bcol[:].rearrange("p k c -> p (k c)"), a["bcol"][i]).then_inc(blkc_in, 16)

                def load(s, name, j):
                    sp.dma_start(w[s][:], a[name][j].rearrange("(k p) n -> p k n", p=128)).then_inc(w_in[s], 16)

                sp.wait_ge(lin_full, g["v"][-1].full)
                load(0, "wo", i)
                sp.wait_ge(lin_full, g["proj"][HEADS - 1][-1].full)
                load(1, "m_w1", i)
                load(2, "m_w2", i)
                sp.wait_ge(lin_full, g["out"][HEADS - 1][-1].full)
                load(0, "wv", i + 1)
                sp.wait_ge(cw_ready, at(i, 2, 2))
                sp.dma_start(stage, a["cw1"][i + 1]).then_inc(stage_in, 16)
                sp.wait_ge(lin_full, g["up"][-1].full)
                load(1, "wq", i + 1)
                sp.wait_ge(lin_full, g["down"][-1].full)
                load(2, "wk", i + 1)
            walk.leave()
            sp.wait_ge(blk_done, BLOCKS + 1)
            sp.wait_ge(cw_ready, 2 * BLOCKS + 1)
            sp.dma_start(big[0:P, :].rearrange("p (t d) -> p t d", d=D),
                         a["x"].rearrange("(t p) d -> p t d", p=P)).then_inc(post_in, 16)
            sp.dma_start(gate_w[:].rearrange("p a k r -> p (a k r)"), a["gate_w"]).then_inc(post_in, 16)
            sp.dma_start(brow[:], a["post_rows"][0:3, :].partition_broadcast(P)).then_inc(post_in, 16)
            sp.wait_ge(norm_ready, 10)
            sp.dma_start(big[:, KD * N:KD * N + 4 * BASES], a["att"].partition_broadcast(128)).then_inc(att_in, 16)
            for n in range(2 * BASES * KD):
                layer, b, k = n // (KD * BASES), n // KD % BASES, n % KD
                if n >= 3:
                    sp.wait_ge(basis_used, n - 2)
                sp.dma_start(ring[n % 3][:], a[f"basis{layer + 1}"][b, k * 128:(k + 1) * 128, :]).then_inc(basis_in[n % 3], 16)
            sp.wait_ge(pbias_done, 2)
            sp.dma_start(brow[:, 2, :], a["post_rows"][4, :].partition_broadcast(P)).then_inc(rows3_in, 16)
            sp.dma_start(brow[:, 0, :], a["post_rows"][3, :].partition_broadcast(P)).then_inc(rows3_in, 16)
            for t in range(T):
                sp.wait_ge(tile_ready, t + 1)
                sp.dma_start(out[t * P:(t + 1) * P, :], x[:, t, :]).then_inc(out_done, 16)
            sp.wait_ge(out_done, 16 * T)

        @block.gpsimd
        def _(pool):
            def drained_inc(s):
                nc.gpsimd.drain().then_inc(s, 1)

            nc.gpsimd.memset(zero_row[:], 0.0)
            drained_inc(consts_set)
            nc.gpsimd.iota(thr[:], pattern=[[P, BUCKETS + 1]], base=0, channel_multiplier=0,
                           allow_small_or_imprecise_dtypes=True)
            nc.gpsimd.memset(zero[:], 0.0)
            nc.gpsimd.memset(tri[:], 1.0)
            nc.gpsimd.memset(ones_sq[:], 1.0)
            nc.gpsimd.memset(ident[:], 0.0)
            nc.gpsimd.memset(ident16[:], 0.0)
            nc.gpsimd.memset(mhalf[:], -0.5)
            nc.gpsimd.memset(ones_f[:], 1.0)
            nc.gpsimd.memset(zcol[:], 0.0)
            nc.gpsimd.memset(tick[:], 0.0)
            nc.gpsimd.iota(gi[:], pattern=[[1, GROUPS + 1]], base=0, channel_multiplier=0,
                           allow_small_or_imprecise_dtypes=True)
            nc.gpsimd.iota(part[:], pattern=[[0, 1]], base=0, channel_multiplier=1,
                           allow_small_or_imprecise_dtypes=True)
            nc.gpsimd.iota(col_iota[:], pattern=[[1, N]], base=1, channel_multiplier=0,
                           allow_small_or_imprecise_dtypes=True)
            for half in range(2):
                rows = slice(half * FREQS, (half + 1) * FREQS)
                nc.gpsimd.drain()
                nc.gpsimd.iota(freq[rows, :], pattern=[[0, 1]], base=1, channel_multiplier=1,
                               allow_small_or_imprecise_dtypes=True)
                nc.gpsimd.memset(quarter[rows, :], 0.25 * half)
            nc.gpsimd.drain()
            nc.gpsimd.affine_select(out=tri[:], in_=tri[:], compare_op=ALU.is_gt, fill=0.0, base=0,
                                    pattern=[[1, P]], channel_multiplier=-1)
            nc.gpsimd.affine_select(out=ident[:], in_=ident[:], compare_op=ALU.not_equal, fill=1.0, base=0,
                                    pattern=[[-1, 128]], channel_multiplier=1)
            nc.gpsimd.affine_select(out=ident16[:], in_=ident16[:], compare_op=ALU.not_equal, fill=1.0, base=0,
                                    pattern=[[-1, P]], channel_multiplier=1)
            drained_inc(consts_set)
            pool.wait_ge(payload_ready, 1)
            for c in range(EC):
                if c >= 4:
                    pool.wait_ge(edge_placed, c - 3)
                nc.gpsimd.tensor_scalar(row_hot[:, c % 4, :], col_iota[0:P, 0:128], slot_row[:, c:c + 1], None,
                                        ALU.is_equal).then_inc(row_hot_ready, 1)
            pool.wait_ge(rows_init, 16 * BUCKETS)
            for g in range(GROUPS):
                pool.wait_ge(run_ready, g + 1)
                nc.gpsimd.indirect_dma_start(
                    out=typed_t, out_offset=bass.IndirectOffsetOnAxis(ap=rowi[0:P, g:g + 1], axis=0),
                    in_=run[:, g % 2, :], in_offset=None,
                    bounds_check=2 * N - 1, oob_is_err=False).then_inc(rows_out[g % 2], 16)
                if g == PREP[0] - 2:
                    pool.wait_ge(var_ready, 1)
                    nc.gpsimd.tensor_tensor(rstd[:], var[:], mhalf[:], ALU.pow).then_inc(rstd_ready, 1)

            def stack_matrices(ln, loads):
                pool.wait_ge(stage_in, loads)
                mine = cw[:, 2 * ln:2 * ln + 2, :]
                nc.gpsimd.tensor_tensor(mine, stage, zcol[:].unsqueeze(1).to_broadcast([128, 2, D]), ALU.add)
                nc.gpsimd.drain()
                for rows in (slice(32, 64), slice(96, 128)):
                    nc.gpsimd.tensor_tensor(mine[rows], stage[rows], mine[rows].bitcast(F32), ALU.subtract)
                    nc.gpsimd.drain()

            stack_matrices(0, 16)
            nc.gpsimd.drain().then_inc(cw_ready, 1)
            with pool.Fori(0, BLOCKS) as i:
                for half in range(2):
                    pool.wait_ge(var_ready, at(i, 2, 2 + half))
                    nc.gpsimd.tensor_tensor(rstd[:], var[:], mhalf[:], ALU.pow).then_inc(rstd_ready, 1)
                    if half == 0:
                        stack_matrices(1, at(i, 32, 32))
                        nc.gpsimd.drain().then_inc(cw_ready, 1)
                    pool.wait_ge(xn_ready, at(i, 2 * T, T * (half + 1)))
                    pool.wait_ge(blkc_in, at(i, 32, 32))
                    nc.gpsimd.tensor_tensor(x[:], x[:], brow[:, 1 + half:2 + half, :].to_broadcast([P, T, D]),
                                            ALU.add).then_inc(xbias_done, 1)
                    if half:
                        stack_matrices(0, at(i, 32, 48))
                        nc.gpsimd.drain().then_inc(cw_ready, 1)
                        continue
                    for h in range(HEADS):
                        for j in range(2 * T):
                            n = h * 2 * T + j
                            c0 = HALF * (j // T)
                            nn = HALVES[j // T] + HALF - c0
                            p0 = c0 - HALVES[j // T]
                            pool.wait_ge(prob_ready, at(i, EXPS, n + 1))
                            if j == 0 and h:
                                pool.wait_ge(sums_read, at(i, HEADS, h))
                            if j % T == 0:
                                nc.gpsimd.tensor_tensor(pacc[:, c0:c0 + nn], prob[:, n % 3, p0:p0 + nn],
                                                        zcol[0:P, :].to_broadcast([P, nn]), ALU.add).then_inc(psum_done, 1)
                            else:
                                pool.wait_ge(psum_done, at(i, EXPS, n))
                                nc.gpsimd.tensor_tensor(pacc[:, c0:c0 + nn], pacc[:, c0:c0 + nn], prob[:, n % 3, p0:p0 + nn],
                                                        ALU.add).then_inc(psum_done, 1)

            walk = Walk()
            walk.n = 8 + BLOCKS * LIN_PER_BLOCK
            g = plan_post(walk)
            pool.wait_ge(blk_done, BLOCKS + 1)
            nc.gpsimd.memset(ones_h[:], 1.0)
            nc.gpsimd.drain().then_inc(consts_set, 1)
            nc.gpsimd.dma_start(ct2[:], typed_t[N:2 * N, :].rearrange("(t p) n -> p t n", p=P)).then_inc(ct2_in, 16)
            pool.wait_ge(post_in, 48)

            def norm_power(count):
                pool.wait_ge(var_ready, count)
                nc.gpsimd.tensor_tensor(rstd[:], var[:], mhalf[:], ALU.pow).then_inc(rstd_ready, 1)

            def add_bias(rows, row, read):
                pool.wait_ge(row_ready, read)
                nc.gpsimd.tensor_tensor(x[:], x[:], rows[:, row:row + 1, :].to_broadcast([P, T, D]),
                                        ALU.add).then_inc(pbias_done, 1)

            def late_load(dst_, src_, job, signal):
                pool.wait_ge(lin_full, job.full)
                nc.gpsimd.dma_start(dst_, src_).then_inc(signal, 16)

            def matrix(name):
                return a[name].rearrange("(k p) n -> p k n", p=128)

            def count_rows(d):
                return d.rearrange("(t p) n -> p t n", p=P)

            norm_power(10)
            add_bias(brow, 0, T)
            late_load(ct[:], count_rows(typed_t[0:N, :]), g["mean1"][-1], ctr_in)
            norm_power(11)
            add_bias(brow, 2, 2 * T)
            late_load(w[2][:], matrix("root2"), g["agg", 0, 0][-1], pw_in)
            late_load(w[0][:], matrix("W1_l"), g["msg", 1, 0][-1], pw_in)
            late_load(ct[:], count_rows(crow_d), g["agg", 1, 0][-1], ctr_in)
            late_load(w[2][:], matrix("W2_l"), g["agg", 1, 0][-1], pw_in)
            late_load(w[1][:], matrix("W1_r"), g["msg", 1, 1][-1], pw_in)
            norm_power(12)
            pool.wait_ge(rows3_in, 32)
            add_bias(brow, 2, 4 * T)
            late_load(w[0][:], matrix("W2_r"), g["sage", 0][-1], pw_in)

        @block.vector
        def _(dve):
            V = nc.vector

            def statistics(count, summed=False):
                V.drain()
                if not summed:
                    for t in range(T):
                        V.bn_stats(stats[:, t, :], x[:, t, :])
                    V.drain()
                for t in range(T):
                    V.bn_aggr(mv[:, t, :], stats[:, t, :])
                V.drain()
                V.tensor_scalar(var[:], mv[:, :, 1], EPS, None, ALU.add).then_inc(var_ready, 1)
                dve.wait_ge(rstd_ready, count)
                V.scalar_tensor_tensor(out=nmr[:], in0=mv[:, :, 0], scalar=-1.0, in1=rstd[:],
                                       op0=ALU.mult, op1=ALU.mult).then_inc(norm_ready, 1)

            walk = Walk()
            jb, jt = walk.take(), walk.take()
            dve.wait_ge(edges_in, 48)
            dve.wait_ge(consts_set, 2)
            V.tensor_scalar(key[:], etyp[:], 0.0, float(N), ALU.not_equal, ALU.mult)
            V.drain()
            V.tensor_tensor(key[:], key[:], edst[:], ALU.add)
            V.drain()
            V.tensor_tensor(ge, key[:].unsqueeze(1).to_broadcast([P, BUCKETS + 1, EC]),
                            thr[:].unsqueeze(2).to_broadcast([P, BUCKETS + 1, EC]), ALU.is_ge)
            V.drain()
            V.tensor_tensor(oh, ge[:, 0:BUCKETS, :], ge[:, 1:BUCKETS + 1, :], ALU.subtract)
            V.tensor_reduce(bsum[:], ge[:, 1:BUCKETS, :].rearrange("p b c -> p c b"), AX.X, ALU.add)
            V.drain()
            V.tensor_reduce(cnt[:], oh, AX.X, ALU.add)
            V.tensor_tensor_scan(incl.rearrange("p b c -> p (b c)"), oh.rearrange("p b c -> p (b c)"),
                                 zero[0:P, :].to_broadcast([P, BUCKETS * EC]), 0.0, ALU.add, ALU.add)
            V.tensor_scalar(src1[:], esrc[:], 1.0, None, ALU.add)
            V.scalar_tensor_tensor(out=dst1[:], in0=bsum[:], scalar=-float(P), in1=key[:],
                                   op0=ALU.mult, op1=ALU.add)
            V.drain().then_inc(ecount_ready, 1)
            V.tensor_scalar(dst1[:], dst1[:], 1.0, None, ALU.add)
            dve.wait_ge(lin_full, jt.full)
            V.tensor_scalar(toti[:], lin_ps(jt, 128, BUCKETS), float(GROUP - 1), None,
                            ALU.add).then_inc(lin_empty[jt.slot], 1)
            V.tensor_copy(base[:], lin_ps(jb, P, BUCKETS)).then_inc(lin_empty[jb.slot], 1)
            V.drain()
            V.tensor_scalar(toti[:], toti[:], 9, None, ALU.logical_shift_right)
            V.drain()
            V.tensor_copy(ngr[:], toti[:])
            V.drain()
            V.tensor_tensor_scan(egr[:], ngr[:], zero[:].to_broadcast([128, BUCKETS]), 0.0, ALU.add, ALU.add)
            V.drain()
            V.tensor_tensor(base2[:], egr[0:P, :], ngr[0:P, :], ALU.subtract)
            V.drain()
            V.scalar_tensor_tensor(out=base[:], in0=base2[:], scalar=float(GROUP), in1=base[:],
                                   op0=ALU.mult, op1=ALU.add)
            V.drain()
            V.tensor_tensor(base[:, 1:], base[:, 1:], incl[:, 0:BUCKETS - 1, EC - 1], ALU.subtract)
            V.drain()
            V.tensor_tensor(incl, incl, base[:].unsqueeze(2).to_broadcast([P, BUCKETS, EC]), ALU.add)
            V.drain()
            V.tensor_tensor(incl, incl, oh, ALU.mult)
            V.drain()
            V.tensor_reduce(pos[:], incl.rearrange("p b c -> p c b"), AX.X, ALU.add)
            V.drain()
            V.tensor_scalar(posi[:], pos[:], -1.0, None, ALU.add)
            V.drain()
            V.tensor_scalar(ia[:], posi[:], 9, 2, ALU.logical_shift_right, ALU.logical_shift_left)
            V.tensor_scalar(ib[:], posi[:], 2, 127, ALU.logical_shift_right, ALU.bitwise_and)
            V.tensor_scalar(ic[:], posi[:], 3, None, ALU.bitwise_and)
            V.drain()
            V.tensor_scalar(slot_row[:], ib[:], 1.0, None, ALU.add)
            V.tensor_tensor(slot_col[:], ia[:], ic[:], ALU.add)
            V.drain()
            V.tensor_scalar(slot_col[:], slot_col[:], 1.0, None, ALU.add)
            V.drain().then_inc(payload_ready, 1)
            for c in range(EC):
                if c >= 4:
                    dve.wait_ge(edge_placed, c - 3)
                V.tensor_scalar(slot_hot[:, c % 4, 0, :], col_iota[0:P, 0:SLOTS], slot_col[:, c:c + 1], src1[:, c:c + 1],
                                ALU.is_equal, ALU.mult)
                V.tensor_scalar(slot_hot[:, c % 4, 1, :], col_iota[0:P, 0:SLOTS], slot_col[:, c:c + 1], dst1[:, c:c + 1],
                                ALU.is_equal, ALU.mult).then_inc(slot_hot_ready, 1)
            V.tensor_tensor(gcmp[:], egr[:].unsqueeze(1).to_broadcast([128, GROUPS + 1, BUCKETS]),
                            gi[:].unsqueeze(2).to_broadcast([128, GROUPS + 1, BUCKETS]), ALU.is_le)
            V.drain()
            V.tensor_reduce(bk[:], gcmp[:], AX.X, ALU.add)
            V.drain()
            V.tensor_tensor(same[:], bk[:, 0:GROUPS], bk[:, 1:GROUPS + 1], ALU.is_equal)
            V.tensor_scalar(rowf[:], bk[:, 0:GROUPS], float(P), part[:], ALU.mult, ALU.add)
            V.drain()
            V.scalar_tensor_tensor(out=rowf[:], in0=same[:], scalar=1.0e6, in1=rowf[:], op0=ALU.mult, op1=ALU.add)
            V.drain()
            V.tensor_copy(rowi[:], rowf[:])

            def first_norm():
                dve.wait_ge(pre_in, 80)
                statistics(1)
                dve.wait_ge(phase_ready, 16)
                V.tensor_scalar(turns, noise, freq[:], 1.0 / 16.0, ALU.mult, ALU.mult)
                V.drain()
                V.tensor_scalar(turns, turns, quarter[:], None, ALU.add)
                V.drain()
                V.tensor_scalar(whole, turns, 12582912.0, -12582912.0, ALU.add, ALU.add)
                V.drain()
                V.tensor_tensor(turns, turns, whole, ALU.subtract)
                V.drain().then_inc(emb_ready, 1)

            def finish_silu():
                dve.wait_ge(zexp_ready, 1)
                V.tensor_scalar(zexp, zexp, 1.0, None, ALU.add)
                V.drain()
                V.reciprocal(zexp, zexp)
                V.drain()
                V.tensor_tensor(silu, z, zexp, ALU.mult)
                V.drain().then_inc(silu_ready, 1)

            for _ in range(3):
                walk.take()
            cj = [walk.take() for _ in range(3)]

            def cond_low(n):
                (c0, nn), job = COLS[n], cj[n]
                dve.wait_ge(cond_hi, n + 1)
                V.scalar_tensor_tensor(out=condS[64:128, c0:c0 + nn],
                                       in0=ps[64:128, 3072 + 512 * job.slot:3072 + 512 * job.slot + nn],
                                       scalar=fb2[64:128, :], in1=condS[64:128, c0:c0 + nn].bitcast(F32),
                                       op0=ALU.add, op1=ALU.subtract).then_inc(lin_empty[job.slot], 1)

            dve.wait_ge(edge_placed, EC)
            V.tensor_copy(es[:].rearrange("p a s -> p (a s)"), o_ps[:, 0:2 * SLOTS])
            V.drain()
            for g in range(GROUPS):
                for j in range(STEPS):
                    n = g * STEPS + j
                    if n >= 4:
                        dve.wait_ge(onehot_used, n - 3)
                    V.tensor_scalar(onehot_dst[:, n % 4, :], col_iota[:, 0:P], es[:, 1, n:n + 1], None, ALU.is_equal)
                    V.tensor_scalar(onehot_src[:, n % 4, :], col_iota[:], es[:, 0, n:n + 1], None, ALU.is_equal).then_inc(onehot_ready, 1)
                if g:
                    if g >= 3:
                        dve.wait_ge(group_full, g - 1)
                    V.tensor_scalar(carry[:, g % 2, :], ident16[:], same[0:P, g - 1:g], None, ALU.mult).then_inc(carry_ready, 1)
                if g == PREP[0]:
                    first_norm()
                if g == PREP[2]:
                    finish_silu()
                if g - 2 in COND_AT:
                    cond_low(COND_AT.index(g - 2))
            for t in range(T):
                dve.wait_ge(typed_in[t // 2], 32)
                V.tensor_tensor(ct[:, t, :], ct[:, t, :], typed1[:, t, :], ALU.add).then_inc(ct_ready, 1)
            for s in range(T):
                dve.wait_ge(crow_copied, s + 1)
                V.tensor_scalar(mneg[:, s, :], crow[:, s % 2, :], 0.0, -BIG, ALU.is_equal, ALU.mult).then_inc(mneg_ready, 1)
            dve.wait_ge(x0_ready, T)
            for s in range(2):
                dve.wait_ge(crow_out[s], 16 * (T // 2))
            V.memset(ones_r[:].bitcast(F32), 1.0)
            V.memset(condS[:, N:N + 2].bitcast(F32), 0.0)
            V.memset(ident_r[:].bitcast(F32), 0.0)
            V.drain()
            V.tensor_copy(ident_r[:, 0:P], ident[0:P, 0:P])
            for t in range(T):
                V.bn_stats(stats[:, t, :], x[:, t, :])
            V.drain().then_inc(blk_done, 1)

            with dve.Fori(0, BLOCKS) as i:
                walk.enter(i, LIN_PER_BLOCK)
                g = plan_block(walk)

                def scale_rows(ln):
                    for t in range(T):
                        n = ln * T + t
                        dve.wait_ge(scale_full, at(i, 2 * T, n + 1))
                        dve.wait_ge(xn_ready, at(i, 2 * T, n + 1))
                        if t >= 2:
                            dve.wait_ge(turn_full, at(i, 2 * T, n - 1))
                        V.scalar_tensor_tensor(out=y[:, t % 2, :], in0=scale_ps(t), scalar=1.0, in1=xn[:, t % 2, :],
                                               op0=ALU.add, op1=ALU.mult).then_inc(scaled_ready, 1)

                statistics(at(i, 2, 2), True)
                scale_rows(0)

                def low_parts(h):
                    for n, job in enumerate(g["proj"][h]):
                        which, (c0, nn) = n // 3, COLS[n % 3]
                        dve.wait_ge(hi_ready, at(i, 6 * HEADS, 6 * h + n + 1))
                        V.scalar_tensor_tensor(out=qk_lo[:, h % 2, which, c0:c0 + nn], in0=lin_ps(job, 128, nn),
                                               scalar=bcol[:, which, h:h + 1],
                                               in1=qk_hi[:, h % 2, which, c0:c0 + nn].bitcast(F32),
                                               op0=ALU.add, op1=ALU.subtract).then_inc(lin_empty[job.slot], 1)

                def masked_max(h, j):
                    s = SCORES["max", h, j]
                    t, c0 = j // 2, HALVES[j % 2]
                    dve.wait_ge(score_full, at(i, SCORES_PER_BLOCK, s.n + 1))
                    V.tensor_tensor(tick[:, MAXES // HEADS * h + j:MAXES // HEADS * h + j + 1], zcol[0:1, :], zcol[0:1, :], ALU.add)
                    V.tensor_tensor_reduce(out=score_ps(s.slot), in0=score_ps(s.slot), in1=in_quarters(mneg[:, t, c0:c0 + HALF]),
                                           scale=1.0, scalar=-BIG, op0=ALU.add, op1=ALU.max,
                                           accum_out=mxp[:, t, j % 2:j % 2 + 1]).then_inc(max_done, 1)

                def negate_max(h):
                    V.drain()
                    V.tensor_tensor(mx[:], mxp[:, :, 0], mxp[:, :, 1], ALU.max)
                    V.drain()
                    V.tensor_scalar(nmx[:], mx[:], -1.0, None, ALU.mult)
                    V.drain().then_inc(neg_max_ready, 1)

                low_parts(0)
                dve.wait_ge(blkc_in, at(i, 32, 32))
                for t, job in enumerate(g["v"]):
                    dve.wait_ge(lin_full, job.full)
                    V.tensor_tensor(vrow[:, t, :], lin_ps(job, P, D), brow[:, 0, :], ALU.add).then_inc(lin_empty[job.slot], 1)
                    masked_max(0, 2 * t)
                    masked_max(0, 2 * t + 1)
                low_parts(1)
                negate_max(0)
                for h in range(HEADS):
                    for j in range(2 * T):
                        n = h * 2 * T + j
                        t, c0, nn = j % T, HALVES[j // T], HALF
                        if h + 1 < HEADS:
                            masked_max(h + 1, j)
                        dve.wait_ge(exp_done, at(i, EXPS, n + 1))
                        V.scalar_tensor_tensor(out=prob[:, n % 3, 0:nn], in0=prob[:, n % 3, 0:nn], scalar=BIG,
                                               in1=ct[:, t, c0:c0 + nn], op0=ALU.min, op1=ALU.mult).then_inc(prob_ready, 1)
                    if h + 1 < HEADS:
                        negate_max(h + 1)
                    if h + 2 < HEADS:
                        low_parts(h + 2)
                    job = g["den"][h]
                    dve.wait_ge(lin_full, job.full)
                    V.tensor_scalar(rden[:], lin_ps(job, P, T), 1.0e-30, None, ALU.max).then_inc(lin_empty[job.slot], 1)
                    V.drain()
                    V.reciprocal(rden[:], rden[:])
                    V.drain().then_inc(sums_read, 1)
                    if h == 0:
                        dve.wait_ge(xbias_done, at(i, 2, 1))
                    for t, job in enumerate(g["out"][h]):
                        dve.wait_ge(lin_full, job.full)
                        V.scalar_tensor_tensor(out=x[:, t, :], in0=lin_ps(job, P, D), scalar=rden[:, t:t + 1],
                                               in1=x[:, t, :], op0=ALU.mult, op1=ALU.add).then_inc(lin_empty[job.slot], 1)
                        if h == HEADS - 1:
                            V.drain()
                            V.bn_stats(stats[:, t, :], x[:, t, :])
                statistics(at(i, 2, 3), True)
                scale_rows(1)
                dve.wait_ge(xbias_done, at(i, 2, 2))
                for t, job in enumerate(g["down"]):
                    dve.wait_ge(lin_full, job.full)
                    V.tensor_tensor(x[:, t, :], x[:, t, :], lin_ps(job, P, D), ALU.add).then_inc(lin_empty[job.slot], 1)
                    V.drain()
                    V.bn_stats(stats[:, t, :], x[:, t, :])
                V.drain().then_inc(blk_done, 1)
            walk.leave()

            g = plan_post(walk)
            units = [0]

            def mix(n):
                for _ in range(2 * n):
                    u = units[0]
                    units[0] += 1
                    layer, b, k = u // (KD * BASES), u // KD % BASES, u % KD
                    dve.wait_ge(basis_in[u % 3], 16 * (u // 3 + 1))
                    for r in range(2):
                        acc = mixed[layer][r][:, k, :]
                        scale = att_w[:, layer, r, b:b + 1]
                        if b == 0:
                            V.tensor_scalar(acc, ring[u % 3][:], scale, None, ALU.mult)
                        else:
                            V.scalar_tensor_tensor(out=acc, in0=ring[u % 3][:], scalar=scale, in1=acc,
                                                   op0=ALU.mult, op1=ALU.add)
                    V.drain().then_inc(basis_used, 1)
                    if u % (KD * BASES) == KD * BASES - 1:
                        V.drain().then_inc(mixed_ready, 1)

            split = [0]

            def split_rows(jobs, scale, extra):
                for t, job in enumerate(jobs):
                    split[0] += 1
                    dve.wait_ge(first_piece, split[0])
                    if scale is None:
                        V.tensor_tensor(pieces[:, 1, t, :], lin_ps(job, P, D), pieces[:, 0, t, :].bitcast(F32),
                                        ALU.subtract).then_inc(lin_empty[job.slot], 1)
                    else:
                        V.scalar_tensor_tensor(out=pieces[:, 1, t, :], in0=lin_ps(job, P, D), scalar=scale(t),
                                               in1=pieces[:, 0, t, :].bitcast(F32), op0=ALU.mult,
                                               op1=ALU.subtract).then_inc(lin_empty[job.slot], 1)
                    V.drain().then_inc(pieces_ready, 1)
                    mix(extra)

            def add_to(rows, t, job, scale=None):
                dve.wait_ge(lin_full, job.full)
                if scale is None:
                    return V.tensor_tensor(rows[:, t, :], rows[:, t, :], lin_ps(job, P, D), ALU.add)
                return V.scalar_tensor_tensor(out=rows[:, t, :], in0=lin_ps(job, P, D), scalar=scale, in1=rows[:, t, :],
                                              op0=ALU.mult, op1=ALU.add)

            dve.wait_ge(post_in, 48)
            V.tensor_tensor(x[:], x[:], big[0:P, :].rearrange("p (t d) -> p t d", d=D), ALU.add)
            statistics(10)
            dve.wait_ge(att_in, 16)
            mix(6)
            split_rows(g["beta1"], None, 1)
            job = g["count"]
            dve.wait_ge(lin_full, job.full)
            V.reciprocal(per_node, lin_ps(job, P, T)).then_inc(lin_empty[job.slot], 1)
            V.drain()
            dve.wait_ge(pbias_done, 1)
            for t in range(T):
                job = g["mean1"][t]
                add_to(x, t, job, per_node[:, t:t + 1]).then_inc(lin_empty[job.slot], 1)
                V.drain()
                job = g["self1"][t]
                add_to(x, t, job).then_inc(lin_empty[job.slot], 1)
                mix(3)

            statistics(11)
            mix(14)

            def gates(layer):
                dve.wait_ge(gate_exp, layer + 1)
                V.tensor_scalar(gate[:], gate[:], 1.0, None, ALU.add)
                V.drain()
                V.reciprocal(gate[:], gate[:])
                V.drain().then_inc(gate_ready, 1)

            gates(0)
            for r in range(2):
                split_rows(g["msg", 0, r], lambda t: gate[:, t, r:r + 1], 1)
                for t, job in enumerate(g["agg", 0, r]):
                    if r == 0:
                        dve.wait_ge(lin_full, job.full)
                        V.tensor_tensor(agg[:, t, :], lin_ps(job, P, D), brow[:, 1, :], ALU.add).then_inc(lin_empty[job.slot], 1)
                    else:
                        add_to(agg, t, job).then_inc(lin_empty[job.slot], 1)
                        V.drain().then_inc(agg_ready, 1)
                    mix(2)
            gates(1)
            dve.wait_ge(pbias_done, 2)
            for r in range(2):
                split_rows(g["msg", 1, r], lambda t: gate[:, t, r:r + 1], 0)
                for t, job in enumerate(g["agg", 1, r]):
                    add_to(x, t, job).then_inc(lin_empty[job.slot], 1)
                V.drain()

            dve.wait_ge(rows3_in, 32)
            statistics(12)
            job = g["degree"]
            dve.wait_ge(lin_full, job.full)
            V.tensor_scalar(per_node, lin_ps(job, P, T), 1.0, None, ALU.max).then_inc(lin_empty[job.slot], 1)
            V.drain()
            V.reciprocal(per_node, per_node)
            V.drain()
            split_rows(g["sage", 0], None, 0)
            for t in range(T):
                job = g["mean3", 0][t]
                dve.wait_ge(lin_full, job.full)
                V.scalar_tensor_tensor(out=agg[:, t, :], in0=lin_ps(job, P, D), scalar=per_node[:, t:t + 1],
                                       in1=brow[:, 0, :], op0=ALU.mult, op1=ALU.add).then_inc(lin_empty[job.slot], 1)
                V.drain()
                job = g["self3", 0][t]
                add_to(agg, t, job).then_inc(lin_empty[job.slot], 1)
                V.drain().then_inc(agg_ready, 1)
            split_rows(g["sage", 1], None, 0)
            dve.wait_ge(pbias_done, 3)
            for t in range(T):
                job = g["mean3", 1][t]
                add_to(x, t, job, per_node[:, t:t + 1]).then_inc(lin_empty[job.slot], 1)
                V.drain()
                job = g["self3", 1][t]
                add_to(x, t, job).then_inc(lin_empty[job.slot], 1)
                V.drain().then_inc(tile_ready, 1)

        @block.scalar
        def _(act):
            A = nc.scalar
            walk = Walk()
            walk.take(), walk.take()
            hj = [walk.take() for _ in range(3)]
            cj = [walk.take() for _ in range(3)]
            for g in range(GROUPS):
                act.wait_ge(*((group_full, g) if g else (onehot_used, STEPS)))
                if g >= 2:
                    act.wait_ge(rows_out[g % 2], 16 * (g // 2))
                A.activation(run[:, g % 2, :], ps[0:P, (g % 2) * 1536:(g % 2) * 1536 + N], ACT.Copy).then_inc(run_ready, 1)
                if g == PREP[0]:
                    act.wait_ge(norm_ready, 1)
                    for t in range(T):
                        A.activation(x[:, t, :], x[:, t, :], ACT.Relu, bias=nmr[:, t:t + 1], scale=rstd[:, t:t + 1]).then_inc(x0_ready, 1)
                    act.wait_ge(emb_ready, 1)
                    A.activation(emb, turns, ACT.Sin, scale=6.2831850)
                    A.drain().then_inc(emb_ready, 1)
                if g == PREP[1]:
                    for (c0, nn), job in zip(COLS, hj):
                        act.wait_ge(lin_full, job.full)
                        A.activation(z[:, c0:c0 + nn], lin_ps(job, COND, nn), ACT.Identity, bias=fb1[:]).then_inc(lin_empty[job.slot], 1)
                    A.drain()
                    A.activation(zexp, z, ACT.Exp, scale=-1.0).then_inc(zexp_ready, 1)
                if g in COND_AT:
                    (c0, nn), job = COLS[COND_AT.index(g)], cj[COND_AT.index(g)]
                    act.wait_ge(lin_full, job.full)
                    A.activation(condS[:, c0:c0 + nn], lin_ps(job, 128, nn), ACT.Identity, bias=fb2[:]).then_inc(cond_hi, 1)
            for s in range(T):
                act.wait_ge(crow_ps_full, s + 1)
                if s >= 2:
                    act.wait_ge(crow_out[s % 2], 16 * (s // 2))
                    act.wait_ge(mneg_ready, s - 1)
                src_ps = ps[0:P, (s % 2) * 1024:(s % 2) * 1024 + 1024].bitcast(F16)
                for t0, nt in ((0, 8), (8, T - 8)):
                    A.activation(crow[:, s % 2, t0 * P:(t0 + nt) * P].rearrange("p (t n) -> p t n", n=P),
                                 src_ps[:, t0 * 128:t0 * 128 + nt * (P + 1)].rearrange("p (t n) -> p t n", n=P + 1)[:, :, 0:P],
                                 ACT.Copy)
                A.drain().then_inc(crow_copied, 1)
                act.wait_ge(crow_copied, s + 1)
                act.dma_start(crow_d[s * P:(s + 1) * P, :], crow[:, s % 2, :]).then_inc(crow_out[s % 2], 16)

            with act.Fori(0, BLOCKS) as i:
                walk.enter(i, LIN_PER_BLOCK)
                g = plan_block(walk)

                def norm(ln, count):
                    act.wait_ge(norm_ready, count)
                    for t in range(T + 1):
                        if t < T:
                            if t >= 2:
                                act.wait_ge(scaled_ready, at(i, 2 * T, ln * T + t - 1))
                            A.activation(xn[:, t % 2, :], x[:, t, :], ACT.Identity, bias=nmr[:, t:t + 1],
                                         scale=rstd[:, t:t + 1]).then_inc(xn_ready, 1)
                        if t:
                            act.wait_ge(turn_full, at(i, 2 * T, ln * T + t))
                            A.activation(yT[:, :, (t - 1) * P:t * P], turn_ps(t - 1)[:, :, 0:P], ACT.Copy).then_inc(turned_ready, 1)

                norm(0, at(i, 2, 2))
                act.wait_ge(blkc_in, at(i, 32, 32))

                def high_parts(h):
                    for n, job in enumerate(g["proj"][h]):
                        which, (c0, nn) = n // 3, COLS[n % 3]
                        act.wait_ge(lin_full, job.full)
                        A.activation(qk_hi[:, h % 2, which, c0:c0 + nn], lin_ps(job, 128, nn), ACT.Identity,
                                     bias=bcol[:, which, h:h + 1]).then_inc(hi_ready, 1)

                def max_row(h):
                    for n, job in enumerate(g["mrow"][h]):
                        t0, t1 = 4 * n, min(4 * n + 4, T)
                        act.wait_ge(lin_full, job.full)
                        A.activation(mrow[:, t0 * P:t1 * P].rearrange("o (t n) -> o t n", n=P),
                                     lin_ps(job, 1, (t1 - t0) * (P + 1)).rearrange("o (t n) -> o t n", n=P + 1)[:, :, 0:P],
                                     ACT.Copy).then_inc(lin_empty[job.slot], 1)

                def copy_o(h, half):
                    act.wait_ge(pv_done, at(i, EXPS, h * 2 * T + (half + 1) * T))
                    if h == 0 and half == 0:
                        act.wait_ge(cw_ready, at(i, 2, 2))
                    if half:
                        act.wait_ge(o_copied, at(i, 2 * HEADS, 2 * h + 1))
                    A.activation(in_quarters(oT[:, HALVES[half]:HALVES[half] + HALF]), o_halves, ACT.Copy).then_inc(o_copied, 1)

                high_parts(0)
                high_parts(1)
                max_row(0)
                for h in range(HEADS):
                    for j in range(2 * T):
                        s, n = SCORES["exp", h, j], h * 2 * T + j
                        act.wait_ge(score_full, at(i, SCORES_PER_BLOCK, s.n + 1))
                        if n >= 3:
                            act.wait_ge(pv_done, at(i, EXPS, n - 2))
                            act.wait_ge(psum_done, at(i, EXPS, n - 2))
                        A.activation(in_quarters(prob[:, n % 3, :]), score_ps(s.slot), ACT.Exp, scale=DH ** -0.5).then_inc(exp_done, 1)
                        if j == T:
                            copy_o(h, 0)
                    copy_o(h, 1)
                    if h + 2 < HEADS:
                        high_parts(h + 2)
                    if h + 1 < HEADS:
                        max_row(h + 1)
                norm(1, at(i, 2, 3))
                for n, job in enumerate(g["up"]):
                    k, (c0, nn) = n // 3, COLS[n % 3]
                    act.wait_ge(lin_full, job.full)
                    A.activation(hidT[:, k, c0:c0 + nn], lin_ps(job, 128, nn), ACT.Relu,
                                 bias=bcol[:, 2, k:k + 1]).then_inc(lin_empty[job.slot], 1)
            walk.leave()

            g = plan_post(walk)
            rows_made = [0]

            def turned(jobs, src_, func, to, ready=None, first=None, scaled=True):
                for t in range(T + 1):
                    if t < T:
                        if ready is not None:
                            act.wait_ge(ready, first + t + 1)
                        if t >= 2:
                            act.wait_ge(lin_full, jobs[t - 2].full)
                        if scaled:
                            A.activation(py[:, t % 2, :], src_[:, t, :], func, bias=nmr[:, t:t + 1],
                                         scale=rstd[:, t:t + 1]).then_inc(row_ready, 1)
                        else:
                            A.activation(py[:, t % 2, :], src_[:, t, :], func).then_inc(row_ready, 1)
                    if t:
                        job = jobs[t - 1]
                        act.wait_ge(lin_full, job.full)
                        A.activation(to[:, :, (t - 1) * P:t * P],
                                     lin_ps(job, 128, KD * P).rearrange("p (k n) -> p k n", k=KD),
                                     ACT.Copy).then_inc(lin_empty[job.slot], 1)

            converted = []

            def convert_counts(counts, gathers, tiles):
                for t in tiles:
                    n = len(converted)
                    if n >= 2:
                        act.wait_ge(lin_full, converted[n - 2].full)
                    A.activation(counts_r[:, n % 2, :, :], counts[:, :, t * P:(t + 1) * P], ACT.Copy).then_inc(counts_ready, 1)
                    converted.append(gathers[t])

            def high_parts_and_counts(jobs, counts, gathers, scale=None):
                convert_counts(counts, gathers, range(2))
                for t, job in enumerate(jobs):
                    act.wait_ge(lin_full, job.full)
                    A.activation(pieces[:, 0, t, :], lin_ps(job, P, D), ACT.Copy,
                                 scale=1.0 if scale is None else scale(t)).then_inc(first_piece, 1)
                convert_counts(counts, gathers, range(2, T))

            def gate_logits(layer):
                job = g["gate", layer]
                act.wait_ge(lin_full, job.full)
                A.activation(gate[:].rearrange("p t r -> p (t r)"), lin_ps(job, P, 2 * T), ACT.Exp,
                             scale=-1.0).then_inc(lin_empty[job.slot], 1)
                A.drain().then_inc(gate_exp, 1)
                act.wait_ge(gate_ready, layer + 1)

            act.wait_ge(norm_ready, 10)
            turned(g["norm1"], x, ACT.Relu, yT)
            high_parts_and_counts(g["beta1"], ct, g["mean1"])
            act.wait_ge(norm_ready, 11)
            turned(g["norm2"], x, ACT.Relu, yT)
            gate_logits(0)
            act.wait_ge(ctr_in, 16)
            act.wait_ge(ct2_in, 16)
            for r, counts in ((0, ct), (1, ct2)):
                high_parts_and_counts(g["msg", 0, r], counts, g["agg", 0, r], lambda t: gate[:, t, r:r + 1])
            turned(g["turn2"], agg, ACT.Relu, hidT, ready=agg_ready, first=0, scaled=False)
            gate_logits(1)
            for r, counts in ((0, ct), (1, ct2)):
                high_parts_and_counts(g["msg", 1, r], counts, g["agg", 1, r], lambda t: gate[:, t, r:r + 1])
            act.wait_ge(norm_ready, 12)
            turned(g["norm3"], x, ACT.Relu, yT)
            act.wait_ge(ctr_in, 32)
            high_parts_and_counts(g["sage", 0], ct, g["mean3", 0])
            turned(g["turn3"], agg, ACT.Tanh, hidT, ready=agg_ready, first=T, scaled=False)
            high_parts_and_counts(g["sage", 1], ct, g["mean3", 1])

        @block.tensor
        def _(pe):
            mm = nc.tensor.matmul
            walk = Walk()

            def reuse(job):
                if job.reuse is not None:
                    pe.wait_ge(lin_empty[job.slot], job.reuse)

            jb, jt = walk.take(), walk.take()
            pe.wait_ge(consts_set, 2)
            pe.wait_ge(ecount_ready, 1)
            mm(lin_ps(jb, P, BUCKETS), tri[:], cnt[:], start=True, stop=True).then_inc(lin_full, 1)
            mm(lin_ps(jt, 128, BUCKETS), ones_sq[:], cnt[:], start=True, stop=True).then_inc(lin_full, 1)
            hj = [walk.take() for _ in range(3)]
            cj = [walk.take() for _ in range(3)]
            for c in range(EC):
                pe.wait_ge(row_hot_ready, c + 1)
                pe.wait_ge(slot_hot_ready, c + 1)
                mm(o_ps[:, 0:2 * SLOTS], row_hot[:, c % 4, :], slot_hot[:, c % 4, :, :].rearrange("p a s -> p (a s)"),
                   start=(c == 0), stop=(c == EC - 1)).then_inc(edge_placed, 1)
            for g in range(GROUPS):
                if g >= 2:
                    pe.wait_ge(run_ready, g - 1)
                for j in range(STEPS):
                    n = g * STEPS + j
                    pe.wait_ge(onehot_ready, n + 1)
                    for c0, nn in WIDE:
                        last = mm(ps[0:P, (g % 2) * 1536 + c0:(g % 2) * 1536 + c0 + nn], onehot_dst[:, n % 4, :],
                                  onehot_src[:, n % 4, c0:c0 + nn], start=(j == 0), stop=(g == 0 and j == STEPS - 1))
                    last.then_inc(onehot_used, 1)
                if g:
                    pe.wait_ge(carry_ready, g)
                    pe.wait_ge(run_ready, g)
                    for c0, nn in WIDE:
                        last = mm(ps[0:P, (g % 2) * 1536 + c0:(g % 2) * 1536 + c0 + nn], carry[:, g % 2, :],
                                  run[:, (g - 1) % 2, c0:c0 + nn], start=False, stop=True)
                    last.then_inc(group_full, 1)
                if g == PREP[1]:
                    pe.wait_ge(pre_in, 80)
                    pe.wait_ge(emb_ready, 2)
                    for (c0, nn), job in zip(COLS, hj):
                        reuse(job)
                        mm(lin_ps(job, COND, nn), fw1[:], emb[:, c0:c0 + nn], start=True, stop=True).then_inc(lin_full, 1)
                if g in COND_AT:
                    pe.wait_ge(silu_ready, 1)
                    (c0, nn), job = COLS[COND_AT.index(g)], cj[COND_AT.index(g)]
                    reuse(job)
                    mm(lin_ps(job, 128, nn), fw2[:], silu[:, c0:c0 + nn], start=True, stop=True).then_inc(lin_full, 1)
            pe.wait_ge(run_ready, GROUPS)
            for s in range(T):
                if s >= 2:
                    pe.wait_ge(crow_copied, s - 1)
                dst_ps = ps[0:P, (s % 2) * 1024:(s % 2) * 1024 + 1024].bitcast(F16)
                for t in range(T):
                    if s == 0:
                        pe.wait_ge(ct_ready, t + 1)
                    c0 = t * (P + 1) if t < 8 else 1024 + (t - 8) * (P + 1)
                    last = nc.tensor.transpose(dst_ps[:, c0:c0 + P], ct[:, t, s * P:(s + 1) * P], ident16[:])
                last.then_inc(crow_ps_full, 1)
            pe.wait_ge(crow_copied, T)

            def row_product(job, lhs, t, weight):
                reuse(job)
                for k in range(KD):
                    last = mm(lin_ps(job, P, D), lhs[:, k, t * P:(t + 1) * P], weight[:, k, :],
                              start=(k == 0), stop=(k == KD - 1))
                last.then_inc(lin_full, 1)

            def col_product(job, lhs, chunk, weight, m):
                c0, nn = COLS[chunk]
                reuse(job)
                for k in range(KD):
                    last = mm(lin_ps(job, 128, nn), weight[:, k, m * 128:(m + 1) * 128], lhs[:, k, c0:c0 + nn],
                              start=(k == 0), stop=(k == KD - 1))
                last.then_inc(lin_full, 1)

            with pe.Fori(0, BLOCKS) as i:
                walk.enter(i, LIN_PER_BLOCK)
                g = plan_block(walk)
                pe.wait_ge(cw_ready, at(i, 2, 1))

                def affine(ln):
                    for t in range(T + 1):
                        if t < T:
                            mm(scale_ps(t), condS[:, t * P:(t + 1) * P], cw[:, 2 * ln, :],
                               start=True, stop=True).then_inc(scale_full, 1)
                        if t:
                            n = ln * T + t
                            pe.wait_ge(scaled_ready, at(i, 2 * T, n))
                            if t > 2:
                                pe.wait_ge(turned_ready, at(i, 2 * T, n - 2))
                            for k in range(KD):
                                o = turn_ps(t - 1)[:, k, 0:P + 1]
                                mm(o, cw[:, 2 * ln + 1, k * 128:(k + 1) * 128], condS[:, (t - 1) * P:t * P + 1],
                                   start=True, stop=False)
                                last = mm(o[:, 0:P], y[:, (t - 1) % 2, k * 128:(k + 1) * 128], ident[0:P, 0:P],
                                          start=False, stop=True)
                            last.then_inc(turn_full, 1)
                    pe.wait_ge(turned_ready, at(i, 2 * T, (ln + 1) * T))

                affine(0)
                pe.wait_ge(w_in[1], at(i, 32, 16))
                pe.wait_ge(w_in[2], at(i, 32, 16))

                def project(h):
                    for n, job in enumerate(g["proj"][h]):
                        col_product(job, yT, n % 3, w[1 + n // 3], h)

                def projected(h):
                    for job in g["proj"][h][-2:]:
                        pe.wait_ge(lin_empty[job.slot], job.emptied)

                def slot_free(s):
                    if s.before is not None:
                        b = s.before
                        if b.kind == "max":
                            pe.wait_ge(max_done, at(i, MAXES, b.h * 2 * T + b.j + 1))
                        else:
                            pe.wait_ge(exp_done, at(i, EXPS, b.h * 2 * T + b.j + 1))

                def max_scores(h, j):
                    s = SCORES["max", h, j]
                    t = j // 2
                    slot_free(s)
                    for b in range(2):
                        c0 = HALVES[j % 2] + b * QUARTER
                        last = mm(score_ps(s.slot)[:, b, :], qk_hi[:, h % 2, 0, t * P:(t + 1) * P],
                                  qk_hi[:, h % 2, 1, c0:c0 + QUARTER], start=True, stop=True)
                    last.then_inc(score_full, 1)

                def exp_scores(h, j):
                    s = SCORES["exp", h, j]
                    t = j % T
                    slot_free(s)
                    rows = slice(t * P, (t + 1) * P)
                    hi, lo = qk_hi[:, h % 2, :, :], qk_lo[:, h % 2, :, :]
                    for b in range(2):
                        c0 = HALVES[j // T] + b * QUARTER
                        cols = slice(c0, c0 + QUARTER)
                        o = score_ps(s.slot)[:, b, :]
                        mm(o, hi[:, 1, rows], hi[:, 0, cols], start=True, stop=False)
                        mm(o, hi[:, 1, rows], lo[:, 0, cols], start=False, stop=False)
                        mm(o, lo[:, 1, rows], hi[:, 0, cols], start=False, stop=False)
                        last = mm(o, ones_r[:, 0:P], mrow[:, cols], start=False, stop=True)
                    last.then_inc(score_full, 1)

                def weighted_values(h, j):
                    n, t = h * 2 * T + j, j % T
                    pe.wait_ge(prob_ready, at(i, EXPS, n + 1))
                    if t == 0 and n >= T:
                        pe.wait_ge(o_copied, at(i, 2 * HEADS, n // T))
                    for b in range(2):
                        last = mm(o_halves[:, b, :], vrow[:, t, h * DH:(h + 1) * DH],
                                  prob[:, n % 3, b * QUARTER:(b + 1) * QUARTER],
                                  start=(t == 0), stop=(t == T - 1))
                    last.then_inc(pv_done, 1)

                def max_row(h):
                    pe.wait_ge(neg_max_ready, at(i, HEADS, h + 1))
                    for n, job in enumerate(g["mrow"][h]):
                        reuse(job)
                        tiles = range(4 * n, min(4 * n + 4, T))
                        for t in tiles:
                            last = mm(lin_ps(job, 1, P + 1, (t - 4 * n) * (P + 1)), nmx[:, t:t + 1], ident_r[:],
                                      start=True, stop=True)
                        last.then_inc(lin_full, 1)
                    for job in g["mrow"][h][-2:]:
                        pe.wait_ge(lin_empty[job.slot], job.emptied)

                project(0)
                pe.wait_ge(w_in[0], at(i, 32, 16))
                for t, job in enumerate(g["v"]):
                    row_product(job, yT, t, w[0])
                    if t == 0:
                        projected(0)
                    max_scores(0, 2 * t)
                    max_scores(0, 2 * t + 1)
                project(1)
                max_row(0)
                projected(1)
                for job in g["v"][-2:]:
                    pe.wait_ge(lin_empty[job.slot], job.emptied)
                for h in range(HEADS):
                    for j in range(2 * T):
                        exp_scores(h, j)
                        if h + 1 < HEADS:
                            max_scores(h + 1, j)
                        if j:
                            weighted_values(h, j - 1)
                    weighted_values(h, 2 * T - 1)
                    if h + 2 < HEADS:
                        project(h + 2)
                    if h + 1 < HEADS:
                        max_row(h + 1)
                    if h + 2 < HEADS:
                        projected(h + 2)
                    job = g["den"][h]
                    reuse(job)
                    pe.wait_ge(psum_done, at(i, EXPS, (h + 1) * 2 * T))
                    for t in range(T):
                        last = mm(lin_ps(job, P, 1, t), pacc[:, t * P:(t + 1) * P], ones_f[0:P, 0:1], start=True, stop=True)
                    last.then_inc(lin_full, 1)
                    if h == 0:
                        pe.wait_ge(w_in[0], at(i, 32, 32))
                    pe.wait_ge(o_copied, at(i, 2 * HEADS, 2 * h + 2))
                    for t, job in enumerate(g["out"][h]):
                        reuse(job)
                        mm(lin_ps(job, P, D), oT[:, t * P:(t + 1) * P], w[0][:, h, :], start=True, stop=True).then_inc(lin_full, 1)
                pe.wait_ge(cw_ready, at(i, 2, 2))
                affine(1)
                pe.wait_ge(w_in[1], at(i, 32, 32))
                for n, job in enumerate(g["up"]):
                    col_product(job, yT, n % 3, w[1], n // 3)
                for job in g["up"][-2:]:
                    pe.wait_ge(lin_empty[job.slot], job.emptied)
                pe.wait_ge(w_in[2], at(i, 32, 32))
                for t, job in enumerate(g["down"]):
                    row_product(job, hidT, t, w[2])
            walk.leave()

            g = plan_post(walk)
            rows_turned = [0]
            split = [0]

            def turn(jobs):
                for t, job in enumerate(jobs):
                    reuse(job)
                    rows_turned[0] += 1
                    pe.wait_ge(row_ready, rows_turned[0])
                    for k in range(KD):
                        last = nc.tensor.transpose(lin_ps(job, 128, P, k * P), py[:, t % 2, k * 128:(k + 1) * 128],
                                                   ident[0:P, 0:P])
                    last.then_inc(lin_full, 1)
                for job in jobs[-2:]:
                    pe.wait_ge(lin_empty[job.slot], job.emptied)

            gathered = [0]

            def gather(job, t, first, self_=None):
                reuse(job)
                if self_ is not None:
                    lhs, weight = self_
                    for k in range(KD):
                        mm(lin_ps(job, P, D), lhs[:, k, t * P:(t + 1) * P], weight[:, k, :], start=(k == 0), stop=False)
                slot = gathered[0] % 2
                gathered[0] += 1
                pe.wait_ge(counts_ready, gathered[0])
                for k in range(T):
                    if t == 0:
                        pe.wait_ge(pieces_ready, first + k + 1)
                    for piece in range(2):
                        last = mm(lin_ps(job, P, D), counts_r[:, slot, k, :], pieces[:, piece, k, :],
                                  start=(self_ is None and k == 0 and piece == 0), stop=(k == T - 1 and piece == 1))
                last.then_inc(lin_full, 1)

            def edge_counts(job, mats):
                reuse(job)
                for t in range(T):
                    for k in range(T):
                        last = mm(lin_ps(job, P, 1, t), mats[:, k, t * P:(t + 1) * P], ones_h[:], start=(k == 0), stop=(k == T - 1))
                last.then_inc(lin_full, 1)

            pe.wait_ge(consts_set, 3)
            turn(g["norm1"])
            pe.wait_ge(w_in[0], 32 * BLOCKS + 16)
            for t, job in enumerate(g["beta1"]):
                row_product(job, yT, t, w[0])
            edge_counts(g["count"], ct)
            pe.wait_ge(w_in[1], 32 * BLOCKS + 16)
            for t in range(T):
                gather(g["mean1"][t], t, 0)
                row_product(g["self1"][t], yT, t, w[1])

            turn(g["norm2"])
            pe.wait_ge(w_in[2], 32 * BLOCKS + 16)
            pe.wait_ge(ctr_in, 16)
            pe.wait_ge(ct2_in, 16)
            for layer, lhs in ((0, yT), (1, hidT)):
                job = g["gate", layer]
                reuse(job)
                for t in range(T):
                    for k in range(KD):
                        last = mm(lin_ps(job, P, 2, 2 * t), lhs[:, k, t * P:(t + 1) * P], gate_w[:, layer, k, :],
                                  start=(k == 0), stop=(k == KD - 1))
                last.then_inc(lin_full, 1)
                pe.wait_ge(mixed_ready, layer + 1)
                if layer:
                    pe.wait_ge(pw_in, 16)
                for r in range(2):
                    for t, job in enumerate(g["msg", layer, r]):
                        row_product(job, lhs, t, mixed[layer][r])
                    for t, job in enumerate(g["agg", layer, r]):
                        gather(job, t, T * (1 + 2 * layer + r), (lhs, w[2]) if r == 0 else None)
                if layer == 0:
                    turn(g["turn2"])

            turn(g["norm3"])
            pe.wait_ge(ctr_in, 32)
            edge_counts(g["degree"], ct)
            pe.wait_ge(pw_in, 64)
            for t, job in enumerate(g["sage", 0]):
                row_product(job, yT, t, w[0])
            for t in range(T):
                gather(g["mean3", 0][t], t, 5 * T)
                row_product(g["self3", 0][t], yT, t, w[1])
            turn(g["turn3"])
            for t, job in enumerate(g["sage", 1]):
                row_product(job, hidT, t, w[2])
            pe.wait_ge(pw_in, 80)
            for t in range(T):
                gather(g["mean3", 1][t], t, 6 * T)
                row_product(g["self3", 1][t], hidT, t, w[0])


def kernel(**inputs):
    import concourse.bacc as bacc
    from concourse.bass_utils import run_bass_kernel_spmd as launch

    c = np.ascontiguousarray
    g = {k: np.asarray(v) for k, v in inputs.items()}
    L0 = {k[7:]: v for k, v in g.items() if k.startswith("L0_gnn_")}
    fw2_stack = np.zeros((COND, 128), np.float32)
    fb2_stack = np.zeros((128, 1), np.float32)
    cw_stack = np.zeros((BLOCKS + 1, 2, 128, 2, D), np.float32)
    for r in range(0, 128, 32):
        fw2_stack[:, r:r + COND] = L0["f_w2"]
        fb2_stack[r:r + COND, 0] = L0["f_b2"]
        fb2_stack[r + COND, 0] = 1.0
        for k, m in enumerate(("s1", "b1", "s2", "b2")):
            cw_stack[:BLOCKS, k // 2, r:r + COND, k % 2] = L0[m + "_w"]
            cw_stack[:BLOCKS, k // 2, r + COND, k % 2] = L0[m + "_b"]
    arrays = {
        "x": c(g["x"]), "src": c(g["src"]), "dst": c(g["dst"]), "edge_type_2": c(g["edge_type_2"]),
        "node_vec1": c(g["node_vec1"].reshape(N)),
        "L0_gnn_f_w1": c(L0["f_w1"]), "f_b1": c(L0["f_b1"].reshape(COND, 1)),
        "fw2_stack": fw2_stack, "fb2_stack": fb2_stack,
        "wv": c(np.concatenate([L0["wv"], g["L1_gnn_wn"][None]])),
        "wq": c(np.concatenate([L0["wq"], g["L1_gnn_wc"][None]])),
        "wk": c(np.concatenate([L0["wk"], g["L2_gnn_root1"][None]])),
        "wo": c(L0["wo"]), "m_w1": c(L0["m_w1"]), "m_w2": c(L0["m_w2"]),
        "brow": c(np.stack([L0["bv"], L0["bo"], L0["m_b2"]], 1)),
        "bcol": c(np.stack([L0["bq"], L0["bk"], L0["m_b1"]], 1).reshape(BLOCKS, 3, KD, 128)
                  .transpose(0, 3, 1, 2).reshape(BLOCKS, 128, 3 * KD)),
        "cw1": c(cw_stack[:, 0]), "cw2": c(cw_stack[:, 1]),
    }
    arrays.update({
        "basis1": c(g["L2_gnn_basis1"]), "basis2": c(g["L2_gnn_basis2"]),
        "att": c(np.stack([g["L2_gnn_att1"], g["L2_gnn_att2"]]).reshape(-1)),
        "gate_w": c(np.stack([g["L2_gnn_gate_w1"], g["L2_gnn_gate_w2"]])[..., 0]
                    .reshape(2, 2, KD, 128).transpose(3, 0, 2, 1).reshape(128, 4 * KD)),
        "root2": c(g["L2_gnn_root2"]),
        "post_rows": c(np.stack([g["L1_gnn_bias"], g["L2_gnn_bias1"], g["L2_gnn_bias2"], g["L3_gnn_b1"], g["L3_gnn_b2"]])),
        "W1_l": c(g["L3_gnn_W1_l"].T), "W1_r": c(g["L3_gnn_W1_r"].T),
        "W2_l": c(g["L3_gnn_W2_l"].T), "W2_r": c(g["L3_gnn_W2_r"].T),
    })
    nc = bacc.Bacc("TRN2", target_bir_lowering=False, num_devices=1, dynamic_dma_scratch_size=4096)
    aps = {k: nc.dram_tensor("in_" + k, v.shape, mybir.dt.from_np(v.dtype), kind="ExternalInput").ap()
           for k, v in arrays.items()}
    out = nc.dram_tensor("out", (N, D), F32, kind="ExternalOutput").ap()
    build(nc, aps, out)
    return launch(nc, [{"in_" + k: v for k, v in arrays.items()}], core_ids=[0]).results[0]["out"]
```
